# Optimizing a Trainium2 kernel written in Bass

```python
import numpy as np
import jax
import jax.numpy as jnp

def _softmax(x, axis=-1):
    return jax.nn.softmax(x, axis=axis)

def _gelu(x):
    return jax.nn.gelu(x, approximate=True)

def _silu(x):
    return jax.nn.silu(x)

def _sigmoid(x):
    return jax.nn.sigmoid(x)

def _layernorm(x, axis=-1, eps=1e-05):
    m = jnp.mean(x, axis=axis, keepdims=True)
    v = jnp.var(x, axis=axis, keepdims=True)
    return (x - m) / jnp.sqrt(v + eps)

def _scatter_add(tgt, idx, src, axis=0):
    return tgt.at[idx].add(src)

def _segment_sum(src, seg, n):
    return jax.ops.segment_sum(src, seg, n)
kernel_name = 'mk_adj_resnorm_d4_adj_r2_0cf339'

def setup_inputs(seed: int=0):
    np.random.seed(seed)
    _w = jnp.asarray

    def _rec_inputs():
        import jax
        import jax.numpy as jnp
        _gk = jax.random.key(seed)
        x = -0.0003929 + 0.9999 * jax.random.normal(jax.random.fold_in(_gk, 1), (32, 256, 128), jnp.float32)
        _a = jax.random.bernoulli(jax.random.fold_in(_gk, 2), 0.0078125, (256, 256))
        _a = jnp.logical_or(_a, jnp.swapaxes(_a, -1, -2))
        _a = jnp.logical_or(_a, jnp.eye(256, dtype=bool))
        _af = _a.astype(jnp.float32)
        _af = _af * jax.random.uniform(jax.random.fold_in(_gk, 3), (256, 256), jnp.float32, 0.05, 1)
        adj = _af
        return (x, adj)
    x, adj = _rec_inputs()

    def _L0_gnn_setup():
        import jax, jax.numpy as jnp
        import numpy as np
        EPS = 1e-05

        def _batchnorm(x, gamma, beta):
            mu = jnp.mean(x, axis=0)
            var = jnp.var(x, axis=0)
            return (x - mu) * jax.lax.rsqrt(var + EPS) * gamma + beta
        key = jax.random.key(seed)
        ks = jax.random.split(key, 4)
        b, n, d, h, o = (32, 1024, 128, 256, 128)
        features = jax.random.normal(ks[0], (b, n, d), dtype=jnp.float32)
        A = jax.random.uniform(ks[1], (n, n), dtype=jnp.float32)
        lim1 = float(np.sqrt(6.0 / (d + h)))
        W1 = jax.random.uniform(ks[2], (h, d), minval=-lim1, maxval=lim1, dtype=jnp.float32)
        b1 = jnp.zeros((h,), jnp.float32)
        lim2 = float(np.sqrt(6.0 / (h + o)))
        W2 = jax.random.uniform(ks[3], (o, h), minval=-lim2, maxval=lim2, dtype=jnp.float32)
        b2 = jnp.zeros((o,), jnp.float32)
        g1 = jnp.ones((h,), jnp.float32)
        be1 = jnp.zeros((h,), jnp.float32)
        g2 = jnp.ones((o,), jnp.float32)
        be2 = jnp.zeros((o,), jnp.float32)
        return {'features': features, 'A': A, 'W1': W1, 'b1': b1, 'g1': g1, 'be1': be1, 'W2': W2, 'b2': b2, 'g2': g2, 'be2': be2}
    _L0_gnn_all = _L0_gnn_setup()
    _L0_gnn_in = {k: v for k, v in _L0_gnn_all.items() if k in ('W1', 'b1', 'g1', 'be1', 'W2', 'b2', 'g2', 'be2')}
    del _L0_gnn_all

    def _L1_gnn_setup():
        import jax, jax.numpy as jnp
        import numpy as np
        BT, N, D, HEADS, E = (512, 64, 128, 4, 256)
        LRELU_SLOPE = 0.2
        EPS = 1e-08
        key = jax.random.key(seed)
        ks = jax.random.split(key, 8)
        d = D
        return {'H': jax.random.normal(ks[0], (BT, N, d), jnp.float32), 'W_lin': jax.random.normal(ks[1], (d, d), jnp.float32) / np.sqrt(d).astype(np.float32), 'W_val': jax.random.normal(ks[2], (d, d), jnp.float32) / np.sqrt(d).astype(np.float32), 'a': jax.random.normal(ks[3], (HEADS, d // HEADS), jnp.float32), 'W_out': jax.random.normal(ks[4], (d, d), jnp.float32) / np.sqrt(d).astype(np.float32), 'A0': jax.random.uniform(ks[5], (N, N), jnp.float32), 'src': jax.random.randint(ks[6], (E,), 0, N, jnp.int32), 'dst': jax.random.randint(ks[7], (E,), 0, N, jnp.int32)}
    _L1_gnn_all = _L1_gnn_setup()
    _L1_gnn_in = {k: v for k, v in _L1_gnn_all.items() if k in ('W_lin', 'W_val', 'a', 'W_out', 'src', 'dst')}
    del _L1_gnn_all

    def _L2_gnn_setup():
        import jax, jax.numpy as jnp
        import numpy as np
        N = 2048
        NFEAT, NHID, NCLASS = (128, 256, 128)
        B = 4

        def _slconv(x, adj, S, W):
            support = jnp.einsum('bnf,fh->bnh', x, W)
            weighting = adj * S
            return jnp.einsum('nm,bmh->bnh', weighting, support)
        key = jax.random.key(seed)
        ks = jax.random.split(key, 6)
        x = jax.random.normal(ks[0], (B, N, NFEAT), dtype=jnp.float32)
        adj = jax.random.uniform(ks[1], (N, N), dtype=jnp.float32)
        S = jnp.ones((N, N), dtype=jnp.float32)
        W1 = jax.random.normal(ks[2], (NFEAT, NHID), dtype=jnp.float32) / np.sqrt(NFEAT)
        W2 = jax.random.normal(ks[3], (NHID, 2 * NHID), dtype=jnp.float32) / np.sqrt(NHID)
        W3 = jax.random.normal(ks[4], (2 * NHID, NCLASS), dtype=jnp.float32) / np.sqrt(2 * NHID)
        return {'x': x, 'adj': adj, 'S': S, 'W1': W1, 'W2': W2, 'W3': W3}
    _L2_gnn_all = _L2_gnn_setup()
    _L2_gnn_in = {k: v for k, v in _L2_gnn_all.items() if k in ('W1', 'W2', 'W3')}
    del _L2_gnn_all

    def _L3_gnn_setup():
        import jax, jax.numpy as jnp
        import numpy as np
        ALPHA = 0.2
        key = jax.random.key(seed)
        k1, k2, k3, k4 = jax.random.split(key, 4)
        B, N, Fin, Fout = (8, 1024, 128, 128)
        h = jax.random.normal(k1, (B, N, Fin), dtype=jnp.float32)
        adj = jax.random.randint(k2, (N, N), 0, 2).astype(jnp.float32)
        adj = jnp.maximum(adj, jnp.eye(N, dtype=jnp.float32))

        def xavier(k, shape, gain=1.414):
            fan_in, fan_out = (shape[0], shape[1])
            a = gain * np.sqrt(6.0 / (fan_in + fan_out))
            return jax.random.uniform(k, shape, dtype=jnp.float32, minval=-a, maxval=a)
        W = xavier(k3, (Fin, Fout))
        a = xavier(k4, (2 * Fout, 1))
        return {'h': h, 'adj_matrix': adj, 'W': W, 'a': a}
    _L3_gnn_all = _L3_gnn_setup()
    _L3_gnn_in = {k: v for k, v in _L3_gnn_all.items() if k in ('W', 'a')}
    del _L3_gnn_all
    return {'x': x, 'adj': adj, 'L0_gnn_W1': _L0_gnn_in['W1'], 'L0_gnn_b1': _L0_gnn_in['b1'], 'L0_gnn_g1': _L0_gnn_in['g1'], 'L0_gnn_be1': _L0_gnn_in['be1'], 'L0_gnn_W2': _L0_gnn_in['W2'], 'L0_gnn_b2': _L0_gnn_in['b2'], 'L0_gnn_g2': _L0_gnn_in['g2'], 'L0_gnn_be2': _L0_gnn_in['be2'], 'L1_gnn_W_lin': _L1_gnn_in['W_lin'], 'L1_gnn_W_val': _L1_gnn_in['W_val'], 'L1_gnn_a': _L1_gnn_in['a'], 'L1_gnn_W_out': _L1_gnn_in['W_out'], 'L1_gnn_src': _L1_gnn_in['src'], 'L1_gnn_dst': _L1_gnn_in['dst'], 'L2_gnn_W1': _L2_gnn_in['W1'], 'L2_gnn_W2': _L2_gnn_in['W2'], 'L2_gnn_W3': _L2_gnn_in['W3'], 'L3_gnn_W': _L3_gnn_in['W'], 'L3_gnn_a': _L3_gnn_in['a']}

def reference(x, adj, L0_gnn_W1, L0_gnn_b1, L0_gnn_g1, L0_gnn_be1, L0_gnn_W2, L0_gnn_b2, L0_gnn_g2, L0_gnn_be2, L1_gnn_W_lin, L1_gnn_W_val, L1_gnn_a, L1_gnn_W_out, L1_gnn_src, L1_gnn_dst, L2_gnn_W1, L2_gnn_W2, L2_gnn_W3, L3_gnn_W, L3_gnn_a):
    import jax
    import jax.numpy as jnp

    def _L0_gnn_ref(features, A, W1, b1, g1, be1, W2, b2, g2, be2):
        import jax, jax.numpy as jnp
        import numpy as np
        EPS = 1e-05

        def _batchnorm(x, gamma, beta):
            mu = jnp.mean(x, axis=0)
            var = jnp.var(x, axis=0)
            return (x - mu) * jax.lax.rsqrt(var + EPS) * gamma + beta
        b, n, d = features.shape
        A_norm = A + jnp.eye(n, dtype=A.dtype)
        deg = jnp.sum(A_norm, axis=0) + jnp.sum(A_norm, axis=1) - jnp.diagonal(A_norm)
        dinv = jax.lax.rsqrt(deg)
        A_hat = A_norm * dinv[:, None] * dinv[None, :]
        agg = jnp.einsum('nm,bmd->bnd', A_hat, features)
        x = agg.reshape(-1, d)
        h = jax.nn.relu(_batchnorm(x @ W1.T + b1, g1, be1))
        out = h @ W2.T + b2
        out = _batchnorm(out, g2, be2)
        return out.reshape(b, n, -1)

    def _L1_gnn_ref(H, W_lin, W_val, a, W_out, A0, src, dst):
        import jax, jax.numpy as jnp
        import numpy as np
        BT, N, D, HEADS, E = (512, 64, 128, 4, 256)
        LRELU_SLOPE = 0.2
        EPS = 1e-08
        bt, n, d = H.shape
        h, dh = a.shape
        Xq = (H @ W_lin.T).reshape(bt, n, h, dh)
        Xv = (H @ W_val.T).reshape(bt, n, h, dh)
        Qs = Xq[:, src]
        Kt = Xq[:, dst]
        e = jnp.einsum('behd,hd->beh', jax.nn.leaky_relu(Qs + Kt, LRELU_SLOPE), a)
        e = e + jnp.log(A0[src, dst] + EPS)[None, :, None]
        e_t = e.transpose(1, 0, 2)
        m = jax.ops.segment_max(e_t, src, num_segments=n)
        ex = jnp.exp(e_t - m[src])
        denom = jax.ops.segment_sum(ex, src, num_segments=n)
        attn = ex / denom[src]
        Vt = Xv[:, dst].transpose(1, 0, 2, 3)
        Y = jax.ops.segment_sum(attn[..., None] * Vt, src, num_segments=n)
        Y = Y.transpose(1, 0, 2, 3).reshape(bt, n, d)
        return Y @ W_out.T

    def _L2_gnn_ref(x, adj, S, W1, W2, W3):
        import jax, jax.numpy as jnp
        import numpy as np
        N = 2048
        NFEAT, NHID, NCLASS = (128, 256, 128)
        B = 4

        def _slconv(x, adj, S, W):
            support = jnp.einsum('bnf,fh->bnh', x, W)
            weighting = adj * S
            return jnp.einsum('nm,bmh->bnh', weighting, support)
        h = jax.nn.relu(_slconv(x, adj, S, W1))
        h = jax.nn.relu(_slconv(h, adj, S, W2))
        return _slconv(h, adj, S, W3)

    def _L3_gnn_ref(h, adj_matrix, W, a):
        import jax, jax.numpy as jnp
        import numpy as np
        ALPHA = 0.2
        Fout = W.shape[1]
        Wh = jnp.einsum('bnf,fo->bno', h, W)
        a1, a2 = (a[:Fout, 0], a[Fout:, 0])
        s1 = Wh @ a1
        s2 = Wh @ a2
        e = s1[:, :, None] + s2[:, None, :]
        e = jnp.where(e >= 0, e, ALPHA * e)
        e = jnp.where(adj_matrix[None] == 0, -jnp.inf, e)
        attention = jax.nn.softmax(e, axis=-1)
        h_prime = jnp.einsum('bij,bjo->bio', attention, Wh)
        return h_prime
    x = _layernorm(x + _L0_gnn_ref(x, adj, L0_gnn_W1, L0_gnn_b1, L0_gnn_g1, L0_gnn_be1, L0_gnn_W2, L0_gnn_b2, L0_gnn_g2, L0_gnn_be2), axis=-1)
    x = _layernorm(x + _L1_gnn_ref(x, L1_gnn_W_lin, L1_gnn_W_val, L1_gnn_a, L1_gnn_W_out, adj, L1_gnn_src, L1_gnn_dst), axis=-1)
    x = _layernorm(x + _L2_gnn_ref(x, adj, adj, L2_gnn_W1, L2_gnn_W2, L2_gnn_W3), axis=-1)
    x = _layernorm(x + _L3_gnn_ref(x, adj, L3_gnn_W, L3_gnn_a), axis=-1)
    return x

_drawn_inputs = setup_inputs


def setup_inputs(seed=0):
    import zlib

    import numpy as np

    out = dict(_drawn_inputs(seed))
    spreads = {'L0_gnn_b1': (0.0, 0.1),
     'L0_gnn_g1': (1.0, 0.2),
     'L0_gnn_be1': (0.0, 0.1),
     'L0_gnn_b2': (0.0, 0.1),
     'L0_gnn_g2': (1.0, 0.2),
     'L0_gnn_be2': (0.0, 0.1)}
    factors = {}
    for name, (base, spread) in spreads.items():
        noise = np.random.default_rng([zlib.crc32(name.encode()), seed]).standard_normal(out[name].shape)
        drawn = base * np.exp(spread * noise) if base else spread * noise
        out[name] = jnp.asarray(drawn.astype(out[name].dtype))
    for name, factor in factors.items():
        out[name] = (out[name] * factor).astype(out[name].dtype)
    return out
```

```python
from contextlib import ExitStack

import concourse.bass as bass
from concourse import mybir

F32 = mybir.dt.float32
F32R = mybir.dt.float32r
I32 = mybir.dt.int32
ALU = mybir.AluOpType
ACT = mybir.ActivationFunctionType
AX_X = mybir.AxisListType.X

P = 128
B, N, D = 32, 256, 128
T = N // P
E = 256
ET = E // P
HEADS = 4
DH = D // HEADS
H0 = 256
H2A, H2B = 256, 512
GA, GB = H2A // P, H2B // P
Q = B // 2
IT = Q // 2
W = 2 * N
BN_EPS = 1e-5
LN_EPS = 1e-5
LOG_EPS = 1e-8
SLOPE = 0.2
BIG = 1e30


def build(nc, x, adj, adj_t, w1_t, w2_t, bn_cols, wv_t, wq_t, a_head, wo_t, src,
          dst, edge_cols, l2w1, l2w2, l2w3, l3w, l3a, l3w_t, out):
    ctx = ExitStack()
    with ctx:
        def sb(name, shape, dt=F32, scope=ctx):
            return scope.enter_context(nc.sbuf_tensor(name, shape, dt))

        def sem(name):
            return ctx.enter_context(nc.semaphore(name))

        def hilo(name, shape, scope=ctx):
            return sb(name + "_hi", shape, F32R, scope), sb(name + "_lo", shape, F32R, scope)

        psum = ctx.enter_context(nc.psum_tensor("psum", [P, 8, 512], F32))

        def bank(k, n=1):
            return psum[:, k:k + n, :]

        def vq_bank(s):
            k = 4 if s == 0 else 0
            return bank(k, 2).rearrange("p t (j c) -> p t j c", j=2)

        ident = sb("ident", [P, P])
        ones = sb("ones", [P, P])
        iota_row = sb("iota_row", [P, N])
        iota_col = sb("iota_col", [P, T])
        adj_sb = sb("adj_sb", [P, T, N])
        adjt_sb = sb("adjt_sb", [P, T, N])
        a_hat_t = sb("a_hat_t", [P, T, N])
        wgt = hilo("wgt", [P, T, N])
        mask = sb("mask", [P, T, N])
        w1t = sb("w1t", [P, H0])
        w2t = sb("w2t", [P, H0 // P, D])
        wvq_raw = sb("wvq_raw", [P, 2, D])
        wvq = hilo("wvq", [P, 2 * D])
        wot = sb("wot", [P, D])
        head_a = sb("head_a", [P, HEADS])
        l2w1_raw = sb("l2w1_raw", [P, H2A])
        l2w1_s = hilo("l2w1_s", [P, H2A])
        l2w2_raw = sb("l2w2_raw", [P, GA, H2B])
        l2w2_s = hilo("l2w2_s", [P, GA, H2B])
        l2w3_s = sb("l2w3_s", [P, GB, D])
        l3w_s = sb("l3w_s", [P, D])
        l3wt_s = sb("l3wt_s", [P, D])
        l3a_s = sb("l3a_s", [P, 2])
        wa = sb("wa", [P, 2])
        wa2_bc = sb("wa2_bc", [P, P])
        bnp = sb("bnp", [P, 9])
        sel_sum = sb("sel_sum", [P, T, E], F32R)
        sel_dst = sb("sel_dst", [P, T, E], F32R)
        sel_src_t = sb("sel_src_t", [P, ET, N])
        reset = sb("reset", [P, 2, E])
        keep = sb("keep", [P, E])
        log_a = sb("log_a", [P, E])
        keep_x = sb("keep_x", [P, Q, W])
        xn = keep_x[:].rearrange("p q (t j d) -> p q t j d", t=T, j=2)
        oraw = keep_x
        gr = ctx.enter_context(nc.semaphore("setup_chain_vector"))
        pz = ctx.enter_context(nc.semaphore("setup_chain_pool"))

        s_small, s_adj, s_edge, s_wts = sem("in_small"), sem("in_adj"), sem("in_edge"), sem("in_weights")
        s_setup_pe, s_setup_pev = sem("setup_pe_done"), sem("setup_psum_read")
        s_log = sem("log_done")
        s_ahat = sem("a_hat_ready")
        s_wsplit = sem("weights_split")

        bst1 = sb("bst1", [P, H0 // P, Q, 6])
        bst2 = sb("bst2", [P, Q, 6])
        bagg = sb("bagg", [P, 3, 2])
        bco = sb("bco", [P, 3, 4])
        xin = sb("xin", [P, 2, T, 2, D])
        aggt = sb("aggt", [P, 2, W])
        x_in = [sem("x_in0"), sem("x_in1")]
        agg_done, agg_out = sem("agg_done"), sem("agg_out")
        h_done, h_out = sem("h_done"), sem("h_out")
        h_stat, bn1_ready = sem("h_stat"), sem("bn1_ready")
        relu_ready, o_done, o_out = sem("relu_ready"), sem("o_done"), sem("o_out")
        o_stat, bn2_ready = sem("o_stat"), sem("bn2_ready")
        bn_chain = sem("bn_chain")

        def wait_apart(eng, signal, value):
            eng.wait_ge(pz if eng is block_pool[0] else gr, 1)
            eng.wait_ge(signal, value)

        block_pool = [None]

        def ln_sems(tag):
            return [sem(f"ln_{tag}_{k}") for k in ("y", "stats", "aggr", "var", "rstd", "done")]

        lnst = sb("lnst", [P, 2, 4, 6])
        lnag = sb("lnag", [P, 2, 4, 2])
        lnr = sb("lnr", [P, 2, 4])
        lnv = sb("lnv", [P, 2, 4])
        eps4 = sb("eps4", [P, 4])
        mhalf = sb("mhalf", [P, N])
        pow_in, pow_out = sem("pow_in"), sem("pow_out")
        deg_bc = sb("deg_bc", [P, N])
        deg = sb("deg", [P, T])

        def ln_stats(dve, y, s, q, sems):
            y_ok, stats, aggr = sems[:3]
            wait_apart(dve, y_ok, q + 1)
            for k in range(4):
                i = dve.bn_stats(lnst[:, s, k, :], y(k // 2, k % 2))
            i.then_inc(stats, 1)
            wait_apart(dve, stats, q + 1)
            for k in range(4):
                i = dve.bn_aggr(lnag[:, s, k, :], lnst[:, s, k, :])
            i.then_inc(aggr, 1)

        def ln_rstd(pool, s, q, sems):
            aggr, var_ok, rstd = sems[2:5]
            pool.wait_ge(aggr, q + 1)
            pool.tensor_tensor(lnv[:, s, :], lnag[:, s, :, 1], eps4[:], ALU.add).then_inc(var_ok, 1)
            pool.wait_ge(var_ok, q + 1)
            pool.tensor_tensor(lnr[:, s, :], lnv[:, s, :], mhalf[:, 0:4], ALU.pow).then_inc(rstd, 1)

        def ln_apply(dve, y, dst_of, s, q, sems):
            dve.wait_ge(sems[4], q + 1)
            for k in range(4):
                i = dve.tensor_scalar(dst_of(k // 2, k % 2), y(k // 2, k % 2), lnag[:, s, k, 0:1],
                                      lnr[:, s, k:k + 1], ALU.subtract, ALU.mult)
            i.then_inc(sems[5], 1)

        def three(pe, o, lhs, rhs, start, stop):
            pe.matmul(o, lhs[0], rhs[0], start=start, stop=False)
            pe.matmul(o, lhs[0], rhs[1], start=False, stop=False)
            return pe.matmul(o, lhs[1], rhs[0], start=False, stop=stop)

        bnt = sb("bnt", [P, 2, W])
        y0 = sb("y0", [P, 2, T, 2, D])
        x1r = sb("x1r", [P, 2, T, 2, D])
        xt = hilo("xt", [P, 2, W])
        z1 = sb("z1", [P, 2, W])
        l1 = sb("l1", [P, 2, W])
        ln0 = ln_sems("0")
        bnt_ready, t1_done, x1_kept = sem("bnt_ready"), sem("t1_done"), sem("x1_kept")
        t2_done, xt_hi, xt_lo = sem("t2_done"), sem("xt_hi"), sem("xt_lo")
        vq_done, vq_hi_ok, vq_lo_ok = sem("vq_done"), sem("vq_hi"), sem("vq_lo")
        g_done, z_ready, l_ready, e_done = sem("g_done"), sem("z_ready"), sem("l_ready"), sem("e_done")
        ve_done, ve_out = sem("ve_done"), sem("ve_out")
        x_in2 = [sem("x_again0"), sem("x_again1")]
        sm = sem("softmax_chain")
        sm_exp, sm_t1, sm_t2 = sem("softmax_exp"), sem("scores_turned"), sem("attn_turned")
        wv_ready, y1_done, y1_out, o1_done = sem("wv_ready"), sem("y1_done"), sem("y1_out"), sem("o1_done")
        ln1 = ln_sems("1")
        xs_hi, xs_lo = sem("xs_hi"), sem("xs_lo")
        pt_done, pt_hi, pt_lo = sem("pt_done"), sem("pt_hi"), sem("pt_lo")
        h1_done, h1_hi, h1_lo = sem("h1_done"), sem("h1_hi"), sem("h1_lo")
        qt_done, qt_hi, qt_lo = sem("qt_done"), sem("qt_hi"), sem("qt_lo")
        h2_done, h2_out = sem("h2_done"), sem("h2_out")
        s3_done, s3_hi, s3_lo = sem("s3_done"), sem("s3_hi"), sem("s3_lo")
        o2_done = sem("o2_done")
        ln2 = ln_sems("2")
        x3_ready, t3_done, xt3_out = sem("x3_ready"), sem("t3_done"), sem("xt3_out")
        s2_done, s1_out, tm_done, m_step = sem("s2_done"), sem("s1_out"), sem("tm_done"), sem("m_step")
        zt_ready, lk_ready, ex_ready = sem("zt_ready"), sem("lk_ready"), sem("ex_ready")
        exr_done, ext_out = sem("ex_turned"), sem("ext_out")
        ax_done, ax_out, o3_done, r_step = sem("ax_done"), sem("ax_out"), sem("o3_done"), sem("r_step")
        ln3 = ln_sems("3")
        stored = [sem("stored0"), sem("stored1")]

        x_nat = x.rearrange("b (t n) d -> n t b d", n=P)
        out_nat = out.rearrange("b (t n) d -> n t b d", n=P)

        scope_e = ExitStack()
        edge_i = sb("edge_i", [P, 2, E], I32, scope_e)
        edge_f = sb("edge_f", [P, 2, E], F32, scope_e)
        ecol_i = sb("ecol_i", [P, 2, ET], I32, scope_e)
        ecol_f = sb("ecol_f", [P, 2, ET], F32, scope_e)
        key_row = sb("key_row", [P, E], F32, scope_e)
        key_col = sb("key_col", [P, ET], F32, scope_e)
        less = sb("less", [P, ET, E], F32, scope_e)
        rank = sb("rank", [P, ET], F32, scope_e)
        perm = sb("perm", [P, ET, E], F32, scope_e)
        ecol_bc = sb("ecol_bc", [P, 2, ET, P], F32, scope_e)
        sorted_bc = sb("sorted_bc", [P, 2, E], F32, scope_e)
        sorted_col = sb("sorted_col", [P, ET], F32, scope_e)
        ssrc = sb("ssrc", [P, T, E], F32, scope_e)
        sdst = sb("sdst", [P, T, E], F32, scope_e)
        prod = sb("prod", [P, T, E], F32, scope_e)
        diff = sb("diff", [P, 2, E], F32, scope_e)
        sq = sb("sq", [P, T, N], F32, scope_e)
        degm = sb("degm", [P, T, N], F32, scope_e)
        dinv_bc = sb("dinv_bc", [P, N], F32, scope_e)
        dinv = sb("dinv", [P, T], F32, scope_e)
        at1 = sb("at1", [P, T, N], F32, scope_e)
        scope_e.close()
        scope0 = ExitStack()
        hraw = sb("hraw", [P, H0 // P, Q, W], scope=scope0)
        scope0.close()
        scope3 = ExitStack()
        vall = sb("vall", [P, ET, B, D], scope=scope3)
        vq = hilo("vq", [P, 2, T, 2, 2 * D], scope3)
        esb = sb("esb", [P, ET, P], scope=scope3)
        sc = sb("sc", [P, 6, E], scope=scope3)
        attn_t = sb("attn_t", [P, ET, P], scope=scope3)
        wv = sb("wv", [P, 2, ET, 2, D], scope=scope3)
        y1t = sb("y1t", [P, 2, W], scope=scope3)
        scope3.close()
        scope4 = ExitStack()
        xs = hilo("xs", [P, 2, T, 2, D], scope4)
        pt = hilo("pt", [P, 2, W], scope4)
        h1 = hilo("h1", [P, 2, 2, T, H2A], scope4)
        qt = hilo("qt", [P, 2, GA, W], scope4)
        h2 = sb("h2", [P, 2, GB, W], scope=scope4)
        s3 = hilo("s3", [P, 2, T, 2, D], scope4)
        scope4.close()
        scope5 = ExitStack()
        x3r = sb("x3r", [P, 2, T, 2, D], scope=scope5)
        xt3 = sb("xt3", [P, 2, W], scope=scope5)
        tm = sb("tm", [P, 2, 4, N], scope=scope5)
        zt = sb("zt", [P, 2, 4, N], scope=scope5)
        lk = sb("lk", [P, 2, 4, N], scope=scope5)
        ex = sb("ex", [P, 2, 4, N], scope=scope5)
        ext = sb("ext", [P, 2, 2, 2, N], scope=scope5)
        axt = sb("axt", [P, 2, W], scope=scope5)
        y3 = sb("y3", [P, 2, T, 2, D], scope=scope5)
        ob = sb("ob", [P, 2, T, 2, D], scope=scope5)
        m3 = sb("m3", [P, 2, 4], scope=scope5)
        s1c = sb("s1c", [P, 2, 4], scope=scope5)
        zm = sb("zm", [P, 2, 3, 4], scope=scope5)
        rs = sb("rs", [P, 2, 4], scope=scope5)
        ri = sb("ri", [P, 2, 4], scope=scope5)
        scope5.close()

        SMALL = 4
        block = ctx.enter_context(nc.Block())

        @block.sync
        def _(sp):
            sp.dma_start(adj_sb[:], adj.rearrange("(t p) m -> p t m", p=P)).then_inc(s_adj, 16)
            sp.dma_start(adjt_sb[:], adj_t.rearrange("(t p) m -> p t m", p=P)).then_inc(s_adj, 16)

            def load_x(s, q, to):
                sp.dma_start(xin[:, s, 0, :, :], x_nat[:, 0, bass.ds(2 * q, 2), :]).then_inc(to[s], 16)
                sp.dma_start(xin[:, s, 1, :, :], x_nat[:, 1, bass.ds(2 * q, 2), :]).then_inc(to[s], 16)

            load_x(0, 0, x_in)
            load_x(1, 1, x_in)
            sp.dma_start(w1t[:], w1_t).then_inc(s_small, 16)
            sp.dma_start(w2t[:], w2_t.rearrange("(k p) o -> p k o", p=P)).then_inc(s_small, 16)
            sp.dma_start(bnp[:], bn_cols).then_inc(s_small, 16)
            sp.dma_start(l3a_s[:], l3a).then_inc(s_small, 16)
            for k, v in enumerate((src, dst)):
                sp.dma_start(edge_i[:, k, :], v.partition_broadcast(P)).then_inc(s_edge, 16)
            sp.dma_start(ecol_i[:].rearrange("p a t -> p (a t)"), edge_cols).then_inc(s_edge, 16)
            with sp.Fori(1, IT) as p:
                for s in range(2):
                    sp.wait_ge(agg_done, 2 * p + s - 1)
                    load_x(s, 2 * p + s, x_in)
            sp.wait_ge(agg_done, Q)
            load_x(0, 0, x_in2)
            load_x(1, 1, x_in2)
            with sp.Fori(1, IT) as p:
                for s in range(2):
                    sp.wait_ge(ln0[0], 2 * p + s - 1)
                    load_x(s, 2 * p + s, x_in2)
            with sp.Fori(0, IT) as p:
                for s in range(2):
                    sp.wait_ge(ln3[5], 2 * p + s + 1)
                    for t in range(T):
                        sp.dma_start(out_nat[:, t, bass.ds(4 * p + 2 * s, 2), :], ob[:, s, t, :, :]).then_inc(stored[s], 16)
            for s in range(2):
                sp.wait_ge(stored[s], 32 * IT)

        @block.gpsimd
        def _(pool):
            block_pool[0] = pool
            pool.memset(ident[:], 0.0).then_inc(pz, 1)
            pool.memset(ones[:], 1.0).then_inc(pz, 1)
            pool.iota(iota_row[:], pattern=[[1, N]], base=0, channel_multiplier=0,
                      allow_small_or_imprecise_dtypes=True).then_inc(pz, 1)
            pool.iota(iota_col[:], pattern=[[P, T]], base=0, channel_multiplier=1,
                      allow_small_or_imprecise_dtypes=True).then_inc(pz, 1)
            pool.memset(head_a[:], 0.0).then_inc(pz, 1)
            pool.wait_ge(pz, 5)
            pool.affine_select(out=ident[:], in_=ident[:], compare_op=ALU.not_equal, fill=1.0, base=0,
                               pattern=[[-1, P]], channel_multiplier=1).then_inc(pz, 1)
            pool.memset(eps4[:], LN_EPS).then_inc(pz, 1)
            pool.memset(mhalf[:], -0.5).then_inc(pz, 1)
            for h in range(HEADS):
                pool.dma_start(head_a[h * DH:(h + 1) * DH, h:h + 1],
                               a_head[h * DH:(h + 1) * DH, :]).then_inc(s_wts, 16)
            for to, frm in ((wvq_raw[:, 0, :], wv_t), (wvq_raw[:, 1, :], wq_t), (wot[:], wo_t),
                            (l2w1_raw[:], l2w1), (l2w2_raw[:], l2w2.rearrange("(k p) g -> p k g", p=P)),
                            (l2w3_s[:], l2w3.rearrange("(k p) g -> p k g", p=P)), (l3w_s[:], l3w), (l3wt_s[:], l3w_t)):
                pool.dma_start(to, frm).then_inc(s_wts, 16)
            pool.wait_ge(pz, 8)
            pool.wait_ge(pow_in, 1)
            pool.tensor_tensor(dinv_bc[:], deg_bc[:], mhalf[:], ALU.pow)
            pool.tensor_tensor(dinv[:], deg[:], mhalf[:, 0:T], ALU.pow).then_inc(pow_out, 1)
            pool.wait_ge(s_wts, 16 * 12)
            pairs = ((wvq, wvq_raw[:].rearrange("p a b -> p (a b)")), (l2w1_s, l2w1_raw[:]), (l2w2_s, l2w2_raw[:]))
            for hl, raw in pairs:
                pool.tensor_copy(hl[0][:], raw).then_inc(pz, 1)
            pool.wait_ge(pz, 11)
            for hl, raw in pairs:
                pool.tensor_tensor(hl[1][:], raw, hl[0][:], ALU.subtract).then_inc(s_wsplit, 1)
            for k in range(3):
                pool.wait_ge(pow_in, k + 2)
                pool.tensor_tensor(bco[:, k, 1:2], bco[:, k, 1:2], mhalf[:, 0:1], ALU.pow).then_inc(pow_out, 1)
            with pool.Fori(0, IT) as p:
                for s in range(2):
                    ln_rstd(pool, s, 2 * p + s, ln0)
                for s in range(2):
                    pool.wait_ge(ln0[5], 2 * p + s + 1)
                    pool.tensor_copy(xn[:, 2 * p + s], x1r[:, s]).then_inc(x1_kept, 1)

            with pool.Fori(0, IT) as p:
                for s in range(2):
                    ln_rstd(pool, s, 2 * p + s, ln1)

            def split_x(s, q, first):
                src_x = xn[:, q]
                pool.wait_ge(ln1[5], q + 1)
                if not first:
                    pool.wait_ge(pt_done, q - 1)
                pool.tensor_copy(xs[0][:, s], src_x).then_inc(xs_hi, 1)
                wait_apart(pool, xs_hi, q + 1)
                pool.tensor_tensor(xs[1][:, s], src_x, xs[0][:, s], ALU.subtract).then_inc(xs_lo, 1)

            pool.wait_ge(o1_done, Q)
            split_x(0, 0, True)
            split_x(1, 1, True)
            with pool.Fori(1, IT) as p:
                for s in range(2):
                    split_x(s, 2 * p + s, False)
                for s in range(2):
                    ln_rstd(pool, s, 2 * p + s - 2, ln2)
            for s in range(2):
                ln_rstd(pool, s, Q - 2 + s, ln2)

            def take_x(s, q, first):
                pool.wait_ge(ln2[5], q + 1)
                if not first:
                    pool.wait_ge(ax_done, q - 1)
                pool.tensor_copy(x3r[:, s], xn[:, q]).then_inc(x3_ready, 1)

            pool.wait_ge(o2_done, Q)
            take_x(0, 0, True)
            take_x(1, 1, True)
            with pool.Fori(1, IT) as p:
                for s in range(2):
                    take_x(s, 2 * p + s, False)
                for s in range(2):
                    ln_rstd(pool, s, 2 * p + s - 2, ln3)
            for s in range(2):
                ln_rstd(pool, s, Q - 2 + s, ln3)

        @block.vector
        def _(dve):
            steps = [0]

            def link(ins):
                steps[0] += 1
                ins.then_inc(gr, 1)
                dve.wait_ge(gr, steps[0])

            dve.wait_ge(pz, 6)
            dve.wait_ge(s_adj, 32)
            for t in range(T):
                i = dve.tensor_tensor(degm[:, t, :], adj_sb[:, t, :], adjt_sb[:, t, :], ALU.add)
            link(i)
            for t in range(T):
                i = dve.tensor_tensor(at1[:, t, t * P:(t + 1) * P], adj_sb[:, t, t * P:(t + 1) * P], ident[:], ALU.mult)
            link(i)
            for t in range(T):
                blk = slice(t * P, (t + 1) * P)
                i = dve.tensor_tensor(degm[:, t, blk], degm[:, t, blk], at1[:, t, blk], ALU.subtract)
            link(i)
            for t in range(T):
                blk = slice(t * P, (t + 1) * P)
                i = dve.tensor_tensor(degm[:, t, blk], degm[:, t, blk], ident[:], ALU.add)
            link(i)
            i = dve.tensor_copy(at1[:], adjt_sb[:])
            link(i)
            for t in range(T):
                blk = slice(t * P, (t + 1) * P)
                i = dve.tensor_tensor(at1[:, t, blk], at1[:, t, blk], ident[:], ALU.add)
            link(i)
            dve.wait_ge(s_setup_pe, 1)
            dve.tensor_copy(deg_bc[:], bank(0)[:, 0, 0:N])
            dve.tensor_copy(deg[:], bank(1)[:, 0, 0:T]).then_inc(pow_in, 1)
            dve.wait_ge(pow_out, 1)
            for t in range(T):
                i = dve.scalar_tensor_tensor(out=a_hat_t[:, t, :], in0=at1[:, t, :], scalar=dinv[:, t:t + 1],
                                             in1=dinv_bc[:], op0=ALU.mult, op1=ALU.mult)
            i.then_inc(s_ahat, 1)

            def edge_setup():
                dve.wait_ge(s_edge, 48)
                dve.tensor_copy(edge_f[:], edge_i[:])
                link(dve.tensor_copy(ecol_f[:], ecol_i[:]))
                dve.scalar_tensor_tensor(out=key_row[:], in0=edge_f[:, 0, :], scalar=float(E), in1=iota_row[:, 0:E],
                                         op0=ALU.mult, op1=ALU.add)
                link(dve.scalar_tensor_tensor(out=key_col[:], in0=ecol_f[:, 0, :], scalar=float(E), in1=iota_col[:, 0:ET],
                                              op0=ALU.mult, op1=ALU.add))
                for t in range(ET):
                    i = dve.tensor_scalar(less[:, t, :], key_row[:], key_col[:, t:t + 1], None, ALU.is_lt)
                link(i)
                link(dve.reduce_sum(rank[:], less[:], AX_X))
                for t in range(ET):
                    i = dve.tensor_scalar(perm[:, t, :], iota_row[:, 0:E], rank[:, t:t + 1], None, ALU.is_equal)
                for k in range(2):
                    for t in range(ET):
                        i = dve.tensor_scalar(ecol_bc[:, k, t, :], ones[:], ecol_f[:, k, t:t + 1], None, ALU.mult)
                link(i)
                dve.wait_ge(s_setup_pe, 2)
                dve.tensor_copy(sorted_bc[:], bank(0)[:, 0, :].rearrange("p (a e) -> p a e", a=2))
                link(dve.tensor_copy(sorted_col[:], bank(1)[:, 0, 0:ET]))
                for t in range(T):
                    dve.tensor_scalar(ssrc[:, t, :], sorted_bc[:, 0, :], iota_col[:, t:t + 1], None, ALU.is_equal)
                    dve.tensor_scalar(sdst[:, t, :], sorted_bc[:, 1, :], iota_col[:, t:t + 1], None, ALU.is_equal)
                for t in range(ET):
                    dve.tensor_scalar(sel_src_t[:, t, :], iota_row[:], sorted_col[:, t:t + 1], None, ALU.is_equal)
                dve.memset(diff[:], 0.0)
                link(dve.memset(reset[:], 0.0))
                dve.tensor_copy(sel_dst[:], sdst[:])
                dve.tensor_tensor(sel_sum[:], ssrc[:], sdst[:], ALU.add)
                dve.tensor_tensor(diff[:, 0, 1:E], sorted_bc[:, 0, 1:E], sorted_bc[:, 0, 0:E - 1], ALU.not_equal)
                link(dve.tensor_tensor(diff[:, 1, 0:E - 1], sorted_bc[:, 0, 1:E], sorted_bc[:, 0, 0:E - 1], ALU.not_equal))
                dve.tensor_scalar(reset[:], diff[:], -BIG, None, ALU.mult)
                link(dve.tensor_scalar(keep[:], diff[:, 0, :], -1.0, 1.0, ALU.mult, ALU.add))
                dve.wait_ge(s_setup_pe, 3)
                link(dve.tensor_tensor(prod[:], bank(2)[:, 0, :].rearrange("p (t e) -> p t e", t=T), ssrc[:], ALU.mult))
                dve.wait_ge(s_setup_pe, 4)
                link(dve.tensor_scalar(prod[:, 0, :], bank(0)[:, 0, 0:E], LOG_EPS, None, ALU.add))

            def weight_setup():
                link(dve.tensor_tensor(sq[:], adjt_sb[:], adjt_sb[:], ALU.mult))
                link(dve.tensor_copy(wgt[0][:], sq[:]))
                link(dve.tensor_tensor(wgt[1][:], sq[:], wgt[0][:], ALU.subtract))
                dve.tensor_scalar(mask[:], adj_sb[:], 0.0, -BIG, ALU.is_equal, ALU.mult)
                dve.wait_ge(s_setup_pe, 5)
                link(dve.tensor_copy(wa[:], bank(1)[:, 0, 0:2]))
                link(dve.tensor_scalar(wa2_bc[:], ones[:], wa[:, 1:2], None, ALU.mult))

            edge_setup()
            weight_setup()

            def pass1(p):
                for s in range(2):
                    q = 2 * p + s
                    dve.wait_ge(agg_done, q + 1)
                    dve.tensor_copy(aggt[:, s, :], bank(s)[:, 0, :]).then_inc(agg_out, 1)
                for s in range(2):
                    q = 2 * p + s
                    wait_apart(dve, h_out, q + 1)
                    for k in range(H0 // P):
                        i = dve.bn_stats(bst1[:, k, q, :], hraw[:, k, q, :])
                    i.then_inc(h_stat, 1)

            with dve.Fori(0, IT) as p:
                pass1(p)
            dve.wait_ge(h_stat, Q)

            cs = [0]

            def bn_link(ins):
                cs[0] += 1
                ins.then_inc(bn_chain, 1)
                dve.wait_ge(bn_chain, cs[0])

            def coefficients(k, stats, bias, gamma, beta):
                bn_link(dve.bn_aggr(bagg[:, k, :], stats))
                dve.tensor_tensor(bco[:, k, 0:1], bagg[:, k, 0:1], bias, ALU.add)
                dve.tensor_scalar(bco[:, k, 1:2], bagg[:, k, 1:2], BN_EPS, None, ALU.add).then_inc(pow_in, 1)
                dve.wait_ge(pow_out, k + 2)
                bn_link(dve.tensor_tensor(bco[:, k, 2:3], bco[:, k, 1:2], gamma, ALU.mult))
                bn_link(dve.tensor_tensor(bco[:, k, 3:4], bias, bco[:, k, 0:1], ALU.subtract))
                bn_link(dve.tensor_tensor(bco[:, k, 3:4], bco[:, k, 3:4], bco[:, k, 2:3], ALU.mult))
                bn_link(dve.tensor_tensor(bco[:, k, 3:4], bco[:, k, 3:4], beta, ALU.add))

            dve.wait_ge(s_small, 16 * SMALL)
            for k in range(2):
                coefficients(k, bst1[:, k].rearrange("p q c -> p (q c)"), bnp[:, k:k + 1], bnp[:, 2 + k:3 + k], bnp[:, 4 + k:5 + k])
            dve.tensor_copy(bagg[:, 2, :], bagg[:, 1, :]).then_inc(bn1_ready, 1)

            with dve.Fori(0, IT) as p:
                for s in range(2):
                    q = 2 * p + s
                    dve.wait_ge(o_done, q + 1)
                    dve.tensor_copy(oraw[:, q, :], bank(s)[:, 0, :]).then_inc(o_out, 1)
                    wait_apart(dve, o_out, q + 1)
                    dve.bn_stats(bst2[:, q, :], oraw[:, q, :]).then_inc(o_stat, 1)
            dve.wait_ge(o_stat, Q)
            coefficients(2, bst2[:].rearrange("p q c -> p (q c)"), bnp[:, 6:7], bnp[:, 7:8], bnp[:, 8:9])
            dve.tensor_copy(bagg[:, 0, :], bagg[:, 1, :]).then_inc(bn2_ready, 1)

            def layer1a(p, first):
                for s in range(2):
                    q = 2 * p + s
                    dve.wait_ge(t1_done, q + 1)
                    dve.wait_ge(x_in2[s], 32 * (p + 1))
                    dve.tensor_tensor(y0[:, s], bank(s)[:, 0, :].rearrange("p (t j d) -> p t j d", t=T, j=2),
                                      xin[:, s], ALU.add).then_inc(ln0[0], 1)
                    ln_stats(dve, lambda t, j: y0[:, s, t, j, :], s, q, ln0)
                for s in range(2):
                    q = 2 * p + s
                    if not first:
                        dve.wait_ge(x1_kept, q - 1)
                        dve.wait_ge(t2_done, q - 1)
                    ln_apply(dve, lambda t, j: y0[:, s, t, j, :], lambda t, j: x1r[:, s, t, j, :], s, q, ln0)
                for s in range(2):
                    q = 2 * p + s
                    dve.wait_ge(xt_hi, q + 1)
                    dve.tensor_tensor(xt[1][:, s, :], bank(2 + s)[:, 0, :], xt[0][:, s, :], ALU.subtract).then_inc(xt_lo, 1)
                for s in range(2):
                    q = 2 * p + s
                    dve.wait_ge(vq_hi_ok, q + 1)
                    dve.tensor_tensor(vq[1][:, s], vq_bank(s), vq[0][:, s], ALU.subtract).then_inc(vq_lo_ok, 1)
                for s in range(2):
                    q = 2 * p + s
                    dve.wait_ge(z_ready, q + 1)
                    dve.scalar_tensor_tensor(out=l1[:, s, :], in0=z1[:, s, :], scalar=SLOPE, in1=z1[:, s, :],
                                             op0=ALU.mult, op1=ALU.max).then_inc(l_ready, 1)

            dve.wait_ge(o_done, Q)
            layer1a(0, True)
            with dve.Fori(1, IT) as p:
                layer1a(p, False)

            ss = [0]

            def sm_link(ins):
                ss[0] += 1
                ins.then_inc(sm, 1)
                dve.wait_ge(sm, ss[0])

            dve.wait_ge(e_done, Q)
            sm_link(dve.tensor_copy(esb[:], bank(7)[:, 0, 0:2 * P].rearrange("p (t c) -> p t c", t=ET)))
            dve.wait_ge(sm_t1, 1)
            dve.wait_ge(s_log, 1)
            score, fwd, top, ssum, total = (sc[:, k, :] for k in range(5))
            rev = slice(None, None, -1)
            sm_link(dve.tensor_tensor(score, bank(6)[:, 0, 0:E], log_a[:], ALU.add))
            sm_link(dve.tensor_tensor_scan(fwd, reset[:, 0, :], score, -BIG, ALU.add, ALU.max))
            sm_link(dve.tensor_tensor_scan(top[:, rev], reset[:, 1, rev], fwd[:, rev], -BIG, ALU.add, ALU.max))
            sm_link(dve.tensor_tensor(score, score, top, ALU.subtract))
            dve.wait_ge(sm_exp, 1)
            sm_link(dve.tensor_tensor_scan(fwd, keep[:], sc[:, 5, :], 0.0, ALU.mult, ALU.add))
            sm_link(dve.tensor_tensor_scan(total[:, rev], reset[:, 1, rev], fwd[:, rev], -BIG, ALU.add, ALU.max))
            sm_link(dve.reciprocal(ssum, total))
            sm_link(dve.tensor_tensor(score, sc[:, 5, :], ssum, ALU.mult))
            dve.wait_ge(sm_t2, 1)
            sm_link(dve.tensor_copy(attn_t[:], bank(6)[:, 0, 0:2 * P].rearrange("p (t c) -> p t c", t=ET)))

            def weigh(s, q, first):
                if not first:
                    dve.wait_ge(y1_done, q - 1)
                v = vall[:, :, bass.ds(2 * q, 2), :].rearrange("p t j (h c) -> p t (j h) c", c=DH)
                w = wv[:, s].rearrange("p t j (h c) -> p t (j h) c", c=DH)
                for t in range(ET):
                    a = attn_t[:, t, bass.ds(2 * HEADS * q, 2 * HEADS)].unsqueeze(2).broadcast_to([P, 2 * HEADS, DH])
                    i = dve.tensor_tensor(w[:, t], v[:, t], a, ALU.mult)
                i.then_inc(wv_ready, 1)

            def add_ln(s, q, done, psum_bank, sems):
                dve.wait_ge(done, q + 1)
                xq = xn[:, q]
                dve.tensor_tensor(xq, bank(psum_bank)[:, 0, :].rearrange("p (t j d) -> p t j d", t=T, j=2), xq,
                                  ALU.add).then_inc(sems[0], 1)

            def norm(q0, sems):
                for s in range(2):
                    ln_stats(dve, lambda t, j: xn[:, q0 + s, t, j, :], s, q0 + s, sems)
                for s in range(2):
                    def at(t, j):
                        return xn[:, q0 + s, t, j, :]
                    ln_apply(dve, at, at, s, q0 + s, sems)

            dve.wait_ge(ve_out, Q)
            weigh(0, 0, True)
            weigh(1, 1, True)
            with dve.Fori(1, IT) as p:
                for s in range(2):
                    weigh(s, 2 * p + s, False)
                for s in range(2):
                    add_ln(s, 2 * p + s - 2, o1_done, 2 + s, ln1)
                norm(2 * p - 2, ln1)
            for s in range(2):
                add_ln(s, Q - 2 + s, o1_done, 2 + s, ln1)
            norm(Q - 2, ln1)

            def layer2(p, first):
                for s in range(2):
                    dve.wait_ge(pt_hi, 2 * p + s + 1)
                    dve.tensor_tensor(pt[1][:, s, :], bank(4 + s)[:, 0, :], pt[0][:, s, :], ALU.subtract).then_inc(pt_lo, 1)
                for s in range(2):
                    dve.wait_ge(h1_hi, 2 * p + s + 1)
                    dve.scalar_tensor_tensor(out=h1[1][:, s].rearrange("p j t f -> p (j t f)"),
                                             in0=bank(2 * s, 2).rearrange("p k c -> p (k c)"), scalar=0.0,
                                             in1=h1[0][:, s].rearrange("p j t f -> p (j t f)"),
                                             op0=ALU.max, op1=ALU.subtract).then_inc(h1_lo, 1)
                for s in range(2):
                    dve.wait_ge(qt_hi, 2 * p + s + 1)
                    dve.tensor_tensor(qt[1][:, s], bank(2 * s, 2), qt[0][:, s], ALU.subtract).then_inc(qt_lo, 1)
                if not first:
                    norm(2 * p - 2, ln2)
                for s in range(2):
                    dve.wait_ge(s3_hi, 2 * p + s + 1)
                    dve.tensor_tensor(s3[1][:, s], bank(s)[:, 0, :].rearrange("p (t j d) -> p t j d", t=T, j=2),
                                      s3[0][:, s], ALU.subtract).then_inc(s3_lo, 1)
                for s in range(2):
                    add_ln(s, 2 * p + s, o2_done, 2 + s, ln2)

            layer2(0, True)
            with dve.Fori(1, IT) as p:
                layer2(p, False)
            norm(Q - 2, ln2)

            def norm3(p, first):
                for s in range(2):
                    ln_stats(dve, lambda t, j: y3[:, s, t, j, :], s, 2 * p + s, ln3)
                for s in range(2):
                    if not first:
                        dve.wait_ge(stored[s], 32 * p)
                    ln_apply(dve, lambda t, j: y3[:, s, t, j, :], lambda t, j: ob[:, s, t, j, :], s, 2 * p + s, ln3)

            def layer3(p, first, second=False):
                for s in range(2):
                    q = 2 * p + s
                    dve.wait_ge(s2_done, q + 1)
                    dve.tensor_copy(s1c[:, s, :], bank(s)[:, 0, 0:4]).then_inc(s1_out, 1)
                    for k in range(4):
                        i = dve.tensor_tensor_reduce(out=tm[:, s, k, :], in0=bank(2 + s)[:, 0, (k % 2) * N:(k % 2 + 1) * N],
                                                     in1=mask[:, k // 2, :], scale=1.0, scalar=-2 * BIG, op0=ALU.add,
                                                     op1=ALU.max, accum_out=m3[:, s, k:k + 1])
                    i.then_inc(tm_done, 1)
                    dve.wait_ge(tm_done, q + 1)
                    dve.wait_ge(s1_out, q + 1)
                    dve.tensor_tensor(zm[:, s, 0, :], m3[:, s, :], s1c[:, s, :], ALU.add).then_inc(m_step, 1)
                    dve.wait_ge(m_step, 3 * q + 1)
                    dve.scalar_tensor_tensor(out=zm[:, s, 1, :], in0=zm[:, s, 0, :], scalar=SLOPE, in1=zm[:, s, 0, :],
                                             op0=ALU.mult, op1=ALU.max).then_inc(m_step, 1)
                    dve.wait_ge(m_step, 3 * q + 2)
                    dve.tensor_scalar(zm[:, s, 2, :], zm[:, s, 1, :], -1.0, None, ALU.mult).then_inc(m_step, 1)
                if not first:
                    norm3(p - 1, second)
                for s in range(2):
                    q = 2 * p + s
                    dve.wait_ge(zt_ready, q + 1)
                    dve.scalar_tensor_tensor(out=lk[:, s].rearrange("p k n -> p (k n)"),
                                             in0=zt[:, s].rearrange("p k n -> p (k n)"), scalar=SLOPE,
                                             in1=zt[:, s].rearrange("p k n -> p (k n)"),
                                             op0=ALU.mult, op1=ALU.max).then_inc(lk_ready, 1)
                for s in range(2):
                    q = 2 * p + s
                    dve.wait_ge(exr_done, q + 1)
                    dve.tensor_copy(ext[:, s].rearrange("p j t n -> p (j t n)"),
                                    bank(4 + 2 * s, 2).rearrange("p k c -> p (k c)")).then_inc(ext_out, 1)
                for s in range(2):
                    q = 2 * p + s
                    dve.wait_ge(ex_ready, q + 1)
                    dve.reciprocal(ri[:, s, :], rs[:, s, :]).then_inc(r_step, 1)
                    dve.wait_ge(r_step, q + 1)
                    dve.wait_ge(o3_done, q + 1)
                    for t in range(T):
                        for j in range(2):
                            k = 2 * t + j
                            i = dve.scalar_tensor_tensor(
                                out=y3[:, s, t, j, :], in0=bank(2 + s)[:, 0, k * D:(k + 1) * D], scalar=ri[:, s, k:k + 1],
                                in1=xn[:, q, t, j, :],
                                op0=ALU.mult, op1=ALU.add)
                    i.then_inc(ln3[0], 1)

            layer3(0, True)
            layer3(1, False, True)
            with dve.Fori(2, IT) as p:
                layer3(p, False)
            norm3(IT - 1, False)

        @block.scalar
        def _(act):
            act.wait_ge(gr, LOG_STEP)
            act.activation(log_a[:], prod[:, 0, :], ACT.Ln).then_inc(s_log, 1)
            act.wait_ge(s_log, 1)

            def pass1(p):
                for s in range(2):
                    q = 2 * p + s
                    act.wait_ge(h_done, q + 1)
                    act.activation(hraw[:, :, q, :], bank(2 + 2 * s, 2), ACT.Copy).then_inc(h_out, 1)

            with act.Fori(0, IT) as p:
                pass1(p)
            act.wait_ge(bn1_ready, 1)
            with act.Fori(0, Q) as q:
                for k in range(H0 // P):
                    i = act.activation(hraw[:, k, q, :], hraw[:, k, q, :], ACT.Relu, bias=bco[:, k, 3:4], scale=bco[:, k, 2:3])
                i.then_inc(relu_ready, 1)

            act.wait_ge(bn2_ready, 1)

            def layer1a(p, first):
                for s in range(2):
                    q = 2 * p + s
                    if not first:
                        act.wait_ge(t1_done, q - 1)
                    act.activation(bnt[:, s, :], oraw[:, q, :], ACT.Identity, bias=bco[:, 2, 3:4], scale=bco[:, 2, 2:3]).then_inc(bnt_ready, 1)
                for s in range(2):
                    q = 2 * p + s
                    act.wait_ge(t2_done, q + 1)
                    act.activation(xt[0][:, s, :], bank(2 + s)[:, 0, :], ACT.Copy).then_inc(xt_hi, 1)
                for s in range(2):
                    q = 2 * p + s
                    act.wait_ge(vq_done, q + 1)
                    act.activation(vq[0][:, s], vq_bank(s), ACT.Copy).then_inc(vq_hi_ok, 1)
                for s in range(2):
                    q = 2 * p + s
                    act.wait_ge(g_done, q + 1)
                    act.activation(z1[:, s, :], bank(2 + s)[:, 0, :], ACT.Copy).then_inc(z_ready, 1)
                for s in range(2):
                    q = 2 * p + s
                    act.wait_ge(ve_done, q + 1)
                    act.activation(vall[:, :, bass.ds(2 * q, 2), :],
                                   bank(4 + s)[:, 0, :].rearrange("p (t j d) -> p t j d", t=ET, j=2), ACT.Copy).then_inc(ve_out, 1)

            act.wait_ge(o_done, Q)
            layer1a(0, True)
            with act.Fori(1, IT) as p:
                layer1a(p, False)
            act.wait_ge(sm, 5)
            act.activation(sc[:, 5, :], sc[:, 0, :], ACT.Exp).then_inc(sm_exp, 1)
            with act.Fori(0, IT) as p:
                for s in range(2):
                    q = 2 * p + s
                    act.wait_ge(y1_done, q + 1)
                    act.activation(y1t[:, s, :], bank(s)[:, 0, :], ACT.Copy).then_inc(y1_out, 1)

            with act.Fori(0, IT) as p:
                for s in range(2):
                    act.wait_ge(pt_done, 2 * p + s + 1)
                    act.activation(pt[0][:, s, :], bank(4 + s)[:, 0, :], ACT.Copy).then_inc(pt_hi, 1)
                for s in range(2):
                    act.wait_ge(h1_done, 2 * p + s + 1)
                    act.activation(h1[0][:, s].rearrange("p j t f -> p (j t f)"), bank(2 * s, 2).rearrange("p k c -> p (k c)"),
                                   ACT.Relu).then_inc(h1_hi, 1)
                for s in range(2):
                    act.wait_ge(qt_done, 2 * p + s + 1)
                    act.activation(qt[0][:, s], bank(2 * s, 2), ACT.Copy).then_inc(qt_hi, 1)
                for s in range(2):
                    for g in range(GB):
                        act.wait_ge(h2_done, GB * (2 * p + s) + g + 1)
                        act.activation(h2[:, s, g, :], bank(4 + g)[:, 0, :], ACT.Relu).then_inc(h2_out, 1)
                for s in range(2):
                    act.wait_ge(s3_done, 2 * p + s + 1)
                    act.activation(s3[0][:, s], bank(s)[:, 0, :].rearrange("p (t j d) -> p t j d", t=T, j=2),
                                   ACT.Copy).then_inc(s3_hi, 1)

            act.wait_ge(o2_done, Q)
            with act.Fori(0, IT) as p:
                for s in range(2):
                    act.wait_ge(t3_done, 2 * p + s + 1)
                    act.activation(xt3[:, s, :], bank(s)[:, 0, :], ACT.Copy).then_inc(xt3_out, 1)
                for s in range(2):
                    act.wait_ge(tm_done, 2 * p + s + 1)
                    act.wait_ge(s1_out, 2 * p + s + 1)
                    for k in range(4):
                        i = act.activation(zt[:, s, k, :], tm[:, s, k, :], ACT.Identity, bias=s1c[:, s, k:k + 1])
                    i.then_inc(zt_ready, 1)
                for s in range(2):
                    act.wait_ge(lk_ready, 2 * p + s + 1)
                    act.wait_ge(m_step, 3 * (2 * p + s) + 3)
                    for k in range(4):
                        i = act.activation(ex[:, s, k, :], lk[:, s, k, :], ACT.Exp, bias=zm[:, s, 2, k:k + 1],
                                           accum_out=rs[:, s, k:k + 1])
                    i.then_inc(ex_ready, 1)
                for s in range(2):
                    act.wait_ge(ax_done, 2 * p + s + 1)
                    act.activation(axt[:, s, :], bank(s)[:, 0, :], ACT.Copy).then_inc(ax_out, 1)

        @block.tensor
        def _(pe):
            pe.wait_ge(gr, 4)
            for t in range(T):
                pe.matmul(bank(0)[:, 0, 0:N], ones[:], degm[:, t, :], start=(t == 0), stop=(t == T - 1))
            for m in range(T):
                for t in range(T):
                    i = pe.matmul(bank(1)[:, 0, m:m + 1], degm[:, t, m * P:(m + 1) * P], ones[:, 0:1],
                                  start=(t == 0), stop=(t == T - 1))
            i.then_inc(s_setup_pe, 1)
            pe.wait_ge(gr, RANK_STEP)
            for k in range(2):
                for t in range(ET):
                    pe.matmul(bank(0)[:, 0, k * E:(k + 1) * E], ecol_bc[:, k, t, :], perm[:, t, :], start=(t == 0), stop=(t == ET - 1))
            for m in range(ET):
                for t in range(ET):
                    i = pe.matmul(bank(1)[:, 0, m:m + 1], perm[:, t, m * P:(m + 1) * P], ecol_f[:, 0, t:t + 1],
                                  start=(t == 0), stop=(t == ET - 1))
            i.then_inc(s_setup_pe, 1)
            pe.wait_ge(gr, RANK_STEP + 3)
            for n in range(T):
                for t in range(T):
                    i = pe.matmul(bank(2)[:, 0, n * E:(n + 1) * E], adjt_sb[:, t, n * P:(n + 1) * P], sdst[:, t, :],
                                  start=(t == 0), stop=(t == T - 1))
            i.then_inc(s_setup_pe, 1)
            pe.wait_ge(gr, LOG_STEP - 1)
            for t in range(T):
                i = pe.matmul(bank(0)[:, 0, 0:E], ones[:], prod[:, t, :], start=(t == 0), stop=(t == T - 1))
            i.then_inc(s_setup_pe, 1)
            pe.wait_ge(s_wts, 16 * 12)
            pe.wait_ge(s_small, 16 * SMALL)
            pe.matmul(bank(1)[:, 0, 0:2], l3wt_s[:], l3a_s[:], start=True, stop=True).then_inc(s_setup_pe, 1)
            pe.wait_ge(gr, LAST_STEP)
            pe.wait_ge(s_ahat, 1)

            def pass1(p, first):
                for s in range(2):
                    pe.wait_ge(x_in[s], 32 * (p + 1))
                    for j in range(2):
                        for t in range(T):
                            i = pe.matmul(bank(s)[:, 0, j * N:(j + 1) * N], xin[:, s, t, j, :], a_hat_t[:, t, :],
                                          start=(t == 0), stop=(t == T - 1))
                    i.then_inc(agg_done, 1)
                for s in range(2):
                    q = 2 * p + s
                    pe.wait_ge(agg_out, q + 1)
                    if not first:
                        pe.wait_ge(h_out, q - 1)
                    for k in range(H0 // P):
                        i = pe.matmul(bank(2 + 2 * s + k)[:, 0, :], w1t[:, k * P:(k + 1) * P], aggt[:, s, :], start=True, stop=True)
                    i.then_inc(h_done, 1)

            pass1(0, True)
            with pe.Fori(1, IT) as p:
                pass1(p, False)

            def pass2(p, first):
                for s in range(2):
                    q = 2 * p + s
                    pe.wait_ge(relu_ready, q + 1)
                    if not first:
                        pe.wait_ge(o_out, q - 1)
                    for k in range(H0 // P):
                        i = pe.matmul(bank(s)[:, 0, :], w2t[:, k, :], hraw[:, k, q, :], start=(k == 0), stop=(k == 1))
                    i.then_inc(o_done, 1)

            pass2(0, True)
            with pe.Fori(1, IT) as p:
                pass2(p, False)

            pe.wait_ge(s_wsplit, 3)
            pe.wait_ge(o_out, Q)

            def layer1a(p, first):
                for s in range(2):
                    q = 2 * p + s
                    pe.wait_ge(bnt_ready, q + 1)
                    if not first:
                        pe.wait_ge(vq_lo_ok, 2 * p)
                    for t in range(T):
                        for j in range(2):
                            k = 2 * t + j
                            i = pe.transpose(bank(s)[:, 0, k * P:(k + 1) * P], bnt[:, s, j * N + t * P:j * N + (t + 1) * P], ident[:])
                    i.then_inc(t1_done, 1)
                for s in range(2):
                    q = 2 * p + s
                    pe.wait_ge(ln0[5], q + 1)
                    if not first:
                        pe.wait_ge(z_ready, q - 1)
                    for j in range(2):
                        for t in range(T):
                            k = 2 * j + t
                            i = pe.transpose(bank(2 + s)[:, 0, k * P:(k + 1) * P], x1r[:, s, t, j, :], ident[:])
                    i.then_inc(t2_done, 1)
                for s in range(2):
                    q = 2 * p + s
                    pe.wait_ge(xt_lo, q + 1)
                    if not first and s == 0:
                        pe.wait_ge(ve_out, 2 * p)
                    for t in range(T):
                        for j in range(2):
                            c = j * N + t * P
                            i = three(pe, vq_bank(s)[:, t, j, :], [h[:, s, c:c + P] for h in xt], [h[:] for h in wvq], True, True)
                    i.then_inc(vq_done, 1)
                for s in range(2):
                    q = 2 * p + s
                    pe.wait_ge(vq_lo_ok, q + 1)
                    for j in range(2):
                        for n, (t, h) in enumerate((t, h) for t in range(T) for h in range(2)):
                            i = pe.matmul(bank(2 + s)[:, 0, j * E:(j + 1) * E], vq[h][:, s, t, j, D:2 * D], sel_sum[:, t, :],
                                          start=(n == 0), stop=(n == 3))
                    i.then_inc(g_done, 1)
                for s in range(2):
                    for e in range(ET):
                        for n, (t, h) in enumerate((t, h) for t in range(T) for h in range(2)):
                            i = pe.matmul(bank(4 + s)[:, 0, e * 2 * D:(e + 1) * 2 * D], sel_dst[:, t, e * P:(e + 1) * P],
                                          vq[h][:, s, t, :, 0:D], start=(n == 0), stop=(n == 3))
                    i.then_inc(ve_done, 1)
                for s in range(2):
                    q = 2 * p + s
                    pe.wait_ge(l_ready, q + 1)
                    for e in range(ET):
                        for j in range(2):
                            i = pe.matmul(bank(7)[:, 0, bass.ds(e * P + HEADS * (2 * q + j), HEADS)],
                                          l1[:, s, j * E + e * P:j * E + (e + 1) * P], head_a[:], start=True, stop=True)
                    i.then_inc(e_done, 1)

            layer1a(0, True)
            with pe.Fori(1, IT) as p:
                layer1a(p, False)

            pe.wait_ge(sm, 1)
            for t in range(ET):
                i = pe.transpose(bank(6)[:, 0, t * P:(t + 1) * P], esb[:, t, :], ident[:])
            i.then_inc(sm_t1, 1)
            pe.wait_ge(sm, 9)
            for t in range(ET):
                i = pe.transpose(bank(6)[:, 0, t * P:(t + 1) * P], sc[:, 0, t * P:(t + 1) * P], ident[:])
            i.then_inc(sm_t2, 1)

            def layer1b(p, first):
                for s in range(2):
                    q = 2 * p + s
                    pe.wait_ge(wv_ready, q + 1)
                    for j in range(2):
                        for e in range(ET):
                            i = pe.matmul(bank(s)[:, 0, j * N:(j + 1) * N], wv[:, s, e, j, :], sel_src_t[:, e, :],
                                          start=(e == 0), stop=(e == ET - 1))
                    i.then_inc(y1_done, 1)
                for s in range(2):
                    q = 2 * p + s
                    pe.wait_ge(y1_out, q + 1)
                    if not first:
                        pe.wait_ge(ln1[0], q - 1)
                    for t in range(T):
                        for j in range(2):
                            k = 2 * t + j
                            c = j * N + t * P
                            i = pe.matmul(bank(2 + s)[:, 0, k * D:(k + 1) * D], y1t[:, s, c:c + P], wot[:], start=True, stop=True)
                    i.then_inc(o1_done, 1)

            layer1b(0, True)
            with pe.Fori(1, IT) as p:
                layer1b(p, False)

            def layer2(p, first):
                for s in range(2):
                    q = 2 * p + s
                    pe.wait_ge(xs_lo, q + 1)
                    if not first:
                        pe.wait_ge(h2_out, GB * (2 * p - 1) + s + 1)
                    for j in range(2):
                        for t in range(T):
                            i = three(pe, bank(4 + s)[:, 0, j * N:(j + 1) * N], [h[:, s, t, j, :] for h in xs],
                                      [h[:, t, :] for h in wgt], t == 0, t == T - 1)
                    i.then_inc(pt_done, 1)
                for s in range(2):
                    q = 2 * p + s
                    pe.wait_ge(pt_lo, q + 1)
                    if not first:
                        if s == 0:
                            pe.wait_ge(s3_lo, 2 * p)
                        else:
                            pe.wait_ge(ln2[0], 2 * p)
                    for j in range(2):
                        for t in range(T):
                            c = j * N + t * P
                            i = three(pe, bank(2 * s + j)[:, 0, t * H2A:(t + 1) * H2A], [h[:, s, c:c + P] for h in pt],
                                      [h[:] for h in l2w1_s], True, True)
                    i.then_inc(h1_done, 1)
                for s in range(2):
                    q = 2 * p + s
                    pe.wait_ge(h1_lo, q + 1)
                    for f in range(GA):
                        for j in range(2):
                            for t in range(T):
                                i = three(pe, bank(2 * s + f)[:, 0, j * N:(j + 1) * N],
                                          [h[:, s, j, t, f * P:(f + 1) * P] for h in h1], [h[:, t, :] for h in wgt],
                                          t == 0, t == T - 1)
                    i.then_inc(qt_done, 1)
                for s in range(2):
                    q = 2 * p + s
                    pe.wait_ge(qt_lo, q + 1)
                    for g in range(GB):
                        if s == 0:
                            if not first:
                                pe.wait_ge(h2_out, GB * (q - 1) + g + 1)
                        else:
                            pe.wait_ge(h2_out, GB * (q - 1) + g + 1)
                        for f in range(GA):
                            i = three(pe, bank(4 + g)[:, 0, :], [h[:, f, g * P:(g + 1) * P] for h in l2w2_s],
                                      [h[:, s, f, :] for h in qt], f == 0, f == GA - 1)
                        i.then_inc(h2_done, 1)
                for s in range(2):
                    q = 2 * p + s
                    pe.wait_ge(h2_out, GB * (q + 1))
                    for t in range(T):
                        for j in range(2):
                            k = 2 * t + j
                            for g in range(GB):
                                i = pe.matmul(bank(s)[:, 0, k * D:(k + 1) * D], h2[:, s, g, j * N + t * P:j * N + (t + 1) * P],
                                              l2w3_s[:, g, :], start=(g == 0), stop=(g == GB - 1))
                    i.then_inc(s3_done, 1)
                for s in range(2):
                    q = 2 * p + s
                    pe.wait_ge(s3_lo, q + 1)
                    for n in range(T):
                        for t in range(T):
                            i = three(pe, bank(2 + s)[:, 0, n * 2 * D:(n + 1) * 2 * D], [h[:, t, n * P:(n + 1) * P] for h in wgt],
                                      [h[:, s, t, :, :] for h in s3], t == 0, t == T - 1)
                    i.then_inc(o2_done, 1)

            layer2(0, True)
            with pe.Fori(1, IT) as p:
                layer2(p, False)

            pe.wait_ge(ln2[0], Q)

            def layer3(p, first):
                for s in range(2):
                    q = 2 * p + s
                    pe.wait_ge(x3_ready, q + 1)
                    if not first:
                        pe.wait_ge(ax_out, q - 1)
                    for j in range(2):
                        for t in range(T):
                            k = 2 * j + t
                            i = pe.transpose(bank(s)[:, 0, k * P:(k + 1) * P], x3r[:, s, t, j, :], ident[:])
                    i.then_inc(t3_done, 1)
                for s in range(2):
                    q = 2 * p + s
                    pe.wait_ge(xt3_out, q + 1)
                    if not first:
                        pe.wait_ge(ln3[0], q - 1)
                    pe.matmul(bank(2 + s)[:, 0, :], wa2_bc[:], xt3[:, s, :], start=True, stop=True)
                    for t in range(T):
                        for j in range(2):
                            k = 2 * t + j
                            i = pe.matmul(bank(s)[:, 0, k:k + 1], xt3[:, s, j * N + t * P:j * N + (t + 1) * P], wa[:, 0:1],
                                          start=True, stop=True)
                    i.then_inc(s2_done, 1)
                for s in range(2):
                    q = 2 * p + s
                    pe.wait_ge(ex_ready, q + 1)
                    if not first:
                        pe.wait_ge(ext_out, q - 1)
                    for j in range(2):
                        for c in range(T):
                            for t in range(T):
                                i = pe.transpose(bank(4 + 2 * s + j)[:, 0, c * N + t * P:c * N + (t + 1) * P],
                                                 ex[:, s, 2 * t + j, c * P:(c + 1) * P], ident[:])
                    i.then_inc(exr_done, 1)
                for s in range(2):
                    q = 2 * p + s
                    pe.wait_ge(ext_out, q + 1)
                    pe.wait_ge(s1_out, q + 1)
                    for j in range(2):
                        for c in range(T):
                            i = pe.matmul(bank(s)[:, 0, j * N:(j + 1) * N], x3r[:, s, c, j, :], ext[:, s, j, c, :],
                                          start=(c == 0), stop=(c == T - 1))
                    i.then_inc(ax_done, 1)
                for s in range(2):
                    q = 2 * p + s
                    pe.wait_ge(ax_out, q + 1)
                    pe.wait_ge(tm_done, q + 1)
                    for t in range(T):
                        for j in range(2):
                            k = 2 * t + j
                            i = pe.matmul(bank(2 + s)[:, 0, k * D:(k + 1) * D], axt[:, s, j * N + t * P:j * N + (t + 1) * P],
                                          l3w_s[:], start=True, stop=True)
                    i.then_inc(o3_done, 1)

            layer3(0, True)
            with pe.Fori(1, IT) as p:
                layer3(p, False)


RANK_STEP = 11
LOG_STEP = 17
LAST_STEP = 22


def kernel(**inputs):
    import numpy as np
    import concourse.bacc as bacc
    from concourse.bass_utils import run_bass_kernel_spmd

    a = {k: np.ascontiguousarray(v) for k, v in inputs.items()}
    arrays = {
        "x": a["x"], "adj": a["adj"], "adj_t": np.ascontiguousarray(a["adj"].T),
        "w1_t": np.ascontiguousarray(a["L0_gnn_W1"].T),
        "w2_t": np.ascontiguousarray(a["L0_gnn_W2"].T),
        "bn_cols": np.ascontiguousarray(np.concatenate(
            [a["L0_gnn_" + k].reshape(-1, P) for k in ("b1", "g1", "be1", "b2", "g2", "be2")]).T),
        "wv_t": np.ascontiguousarray(a["L1_gnn_W_val"].T), "wq_t": np.ascontiguousarray(a["L1_gnn_W_lin"].T),
        "a_head": a["L1_gnn_a"].reshape(D, 1), "wo_t": np.ascontiguousarray(a["L1_gnn_W_out"].T),
        "src": a["L1_gnn_src"], "dst": a["L1_gnn_dst"],
        "edge_cols": np.ascontiguousarray(np.concatenate([a[k].reshape(ET, P) for k in ("L1_gnn_src", "L1_gnn_dst")]).T),
        "l2w1": a["L2_gnn_W1"], "l2w2": a["L2_gnn_W2"], "l2w3": a["L2_gnn_W3"],
        "l3w": a["L3_gnn_W"], "l3a": np.ascontiguousarray(a["L3_gnn_a"].reshape(2, D).T), "l3w_t": np.ascontiguousarray(a["L3_gnn_W"].T),
    }
    nc = bacc.Bacc("TRN2", target_bir_lowering=False, num_devices=1)
    aps = {k: nc.dram_tensor("in_" + k, v.shape, mybir.dt.from_np(v.dtype), kind="ExternalInput").ap() for k, v in arrays.items()}
    out = nc.dram_tensor("out_x", (B, N, D), F32, kind="ExternalOutput").ap()
    build(nc, *aps.values(), out)
    r = run_bass_kernel_spmd(nc, [{"in_" + k: v for k, v in arrays.items()}], core_ids=[0])
    return r.results[0]["out_x"]
```

```python
from contextlib import ExitStack

import concourse.bass as bass
from concourse import mybir

F32 = mybir.dt.float32
F32R = mybir.dt.float32r
I32 = mybir.dt.int32
ALU = mybir.AluOpType
ACT = mybir.ActivationFunctionType
AX_X = mybir.AxisListType.X

P = 128
B, N, D = 32, 256, 128
T = N // P
E = 256
ET = E // P
HEADS = 4
DH = D // HEADS
H0 = 256
H2A, H2B = 256, 512
GA, GB = H2A // P, H2B // P
Q = B // 2
IT = Q // 2
W = 2 * N
BN_EPS = 1e-5
LN_EPS = 1e-5
LOG_EPS = 1e-8
SLOPE = 0.2
BIG = 1e30


def build(nc, x, adj, adj_t, w1_t, w2_t, bn_cols, wv_t, wq_t, a_head, wo_t, src,
          dst, edge_cols, l2w1, l2w2, l2w3, l3w, l3a, l3w_t, out):
    ctx = ExitStack()
    with ctx:
        def sb(name, shape, dt=F32, scope=ctx):
            return scope.enter_context(nc.sbuf_tensor(name, shape, dt))

        def sem(name):
            return ctx.enter_context(nc.semaphore(name))

        def hilo(name, shape, scope=ctx):
            return sb(name + "_hi", shape, F32R, scope), sb(name + "_lo", shape, F32R, scope)

        psum = ctx.enter_context(nc.psum_tensor("psum", [P, 8, 512], F32))

        def bank(k, n=1):
            return psum[:, k:k + n, :]

        def vq_bank(s):
            return bank(2 + 2 * s, 2).rearrange("p t (j c) -> p t j c", j=2)

        ident = sb("ident", [P, P])
        ones = sb("ones", [P, P])
        iota_row = sb("iota_row", [P, N])
        iota_col = sb("iota_col", [P, T])
        adj_sb = sb("adj_sb", [P, T, N])
        adjt_sb = sb("adjt_sb", [P, T, N])
        a_hat = hilo("a_hat", [P, T, N])
        wgt = hilo("wgt", [P, T, N])
        mask = sb("mask", [P, T, N])
        w1_raw = sb("w1_raw", [P, H0])
        w1t = hilo("w1t", [P, H0])
        w2t = sb("w2t", [P, H0 // P, D])
        wvq_raw = sb("wvq_raw", [P, 2, D])
        wvq = hilo("wvq", [P, 2 * D])
        wot = sb("wot", [P, D])
        head_a = sb("head_a", [P, HEADS])
        l2w1_raw = sb("l2w1_raw", [P, H2A])
        l2w1_s = hilo("l2w1_s", [P, H2A])
        l2w2_raw = sb("l2w2_raw", [P, GA, H2B])
        l2w2_s = hilo("l2w2_s", [P, GA, H2B])
        l2w3_s = sb("l2w3_s", [P, GB, D])
        l3w_s = sb("l3w_s", [P, D])
        l3wt_s = sb("l3wt_s", [P, D])
        l3a_s = sb("l3a_s", [P, 2])
        wa = sb("wa", [P, 2])
        wa2_bc = sb("wa2_bc", [P, P])
        bnp = sb("bnp", [P, 9])
        sel_sum = sb("sel_sum", [P, T, E], F32R)
        sel_dst = sb("sel_dst", [P, T, E], F32R)
        sel_src_t = sb("sel_src_t", [P, ET, N])
        reset = sb("reset", [P, 2, E])
        same = sb("same", [P, 2, E])
        log_a = sb("log_a", [P, E])
        scope_x = ExitStack()
        x0 = hilo("x0", [P, 2, T, 2, D], scope_x)
        scope_x.close()
        keep_x = sb("keep_x", [P, Q, W])
        xn = keep_x[:].rearrange("p q (t j d) -> p q t j d", t=T, j=2)
        oraw = keep_x
        s_adj, s_small, s_edge, s_wts = sem("in_adj"), sem("in_small"), sem("in_edge"), sem("in_weights")
        pz = sem("constants")
        dc, pc = sem("setup_chain_vector"), sem("setup_chain_pool")
        deg_ready, deg_done, deg_root, a_hat_ready = sem("deg_ready"), sem("deg_done"), sem("deg_root"), sem("a_hat_ready")
        keys_compared, ranks_ready = sem("keys_compared"), sem("ranks_ready")
        edges_ranked, edges_sorted, sorted_out = sem("edges_ranked"), sem("edges_sorted"), sem("sorted_out")
        sel_ready, adj_dst_done, adj_dst_out = sem("sel_ready"), sem("adj_dst_done"), sem("adj_dst_out")
        picked, a_edge_done, log_ready = sem("picked"), sem("a_edge_done"), sem("log_ready")
        weights_split, wgt_ready, wa2_ready = sem("weights_split"), sem("wgt_ready"), sem("wa2_ready")

        bst1 = sb("bst1", [P, H0 // P, Q, 6])
        bst2 = sb("bst2", [P, Q, 6])
        bagg = sb("bagg", [P, 3, 2])
        bco = sb("bco", [P, 4, 3])
        xin = sb("xin", [P, 2, T, 2, D])
        x_in = [sem("x_in0"), sem("x_in1")]
        agg_done, agg_hi, agg_lo = sem("agg_done"), sem("agg_hi"), sem("agg_lo")
        x0_hi, x0_lo = sem("x0_hi"), sem("x0_lo")
        h_done, h_out = sem("h_done"), sem("h_out")
        h_stat, bn1_ready = sem("h_stat"), sem("bn1_ready")
        relu_ready, o_done, o_out = sem("relu_ready"), sem("o_done"), sem("o_out")
        o_stat, bn2_ready = sem("o_stat"), sem("bn2_ready")
        bn_chain, bn_var, bn_root = sem("bn_chain"), sem("bn_var"), sem("bn_root")

        def wait_apart(dve, signal, value):
            if not isinstance(value, int):
                value = dve.snap(value)
            dve.wait_ge(dc, 1)
            dve.wait_ge(signal, value)

        def ln_sems(tag):
            return [sem(f"ln_{tag}_{k}") for k in ("y", "stats", "aggr", "root", "rstd", "done")]

        lnst = sb("lnst", [P, 2, 4, 6])
        lnag = sb("lnag", [P, 2, 4, 2])
        lnr = sb("lnr", [P, 2, 4])
        lnv = sb("lnv", [P, 2, 4])
        eps = sb("eps", [P, 1])
        log_eps = sb("log_eps", [P, 1])
        mhalf = sb("mhalf", [P, 8])

        def ln_stats(dve, y, p, sems):
            y_ok, stats, aggr = sems[:3]
            wait_apart(dve, y_ok, 2 * p + 2)
            for s in range(2):
                for k in range(4):
                    i = dve.bn_stats(lnst[:, s, k, :], y(s, k // 2, k % 2))
            i.then_inc(stats, 2)
            wait_apart(dve, stats, 2 * p + 2)
            for s in range(2):
                for k in range(4):
                    i = dve.bn_aggr(lnag[:, s, k, :], lnst[:, s, k, :])
            i.then_inc(aggr, 1)

        def ln_root(act, p, sems):
            act.wait_ge(sems[2], p + 1)
            act.activation(lnv[:].rearrange("p s k -> p (s k)"), lnag[:].rearrange("p s k c -> p (s k) c")[:, :, 1],
                           ACT.Sqrt, bias=eps[:]).then_inc(sems[3], 1)

        def var_eps(dve, p, sems):
            dve.wait_ge(sems[2], p + 1)
            dve.tensor_scalar(lnv[:].rearrange("p s k -> p (s k)"), lnag[:].rearrange("p s k c -> p (s k) c")[:, :, 1],
                              LN_EPS, None, ALU.add).then_inc(sems[3], 1)

        def ln_rstd(dve, p, sems):
            dve.wait_ge(sems[3], p + 1)
            dve.reciprocal(lnr[:], lnv[:]).then_inc(sems[4], 1)

        def ln_apply(dve, y, dst_of, p, s, sems):
            dve.wait_ge(sems[4], p + 1)
            for k in range(4):
                i = dve.tensor_scalar(dst_of(k // 2, k % 2), y(s, k // 2, k % 2), lnag[:, s, k, 0:1],
                                      lnr[:, s, k:k + 1], ALU.subtract, ALU.mult)
            i.then_inc(sems[5], 1)

        def three(pe, o, lhs, rhs, start, stop):
            pe.matmul(o, lhs[0], rhs[0], start=start, stop=False)
            pe.matmul(o, lhs[0], rhs[1], start=False, stop=False)
            return pe.matmul(o, lhs[1], rhs[0], start=False, stop=stop)

        scope_a = ExitStack()
        aggt = hilo("aggt", [P, 2, W], scope_a)
        scope_a.close()
        xt = hilo("xt", [P, 2, W])
        l1 = sb("l1", [P, 2, W])
        ln0 = ln_sems("0")
        bnt_ready, t1_done, x1_kept = sem("bnt_ready"), sem("t1_done"), sem("x1_kept")
        t2_done, xt_hi, xt_lo = sem("t2_done"), sem("xt_hi"), sem("xt_lo")
        vq_done, vq_hi_ok, vq_lo_ok = sem("vq_done"), sem("vq_hi"), sem("vq_lo")
        g_done, z_ready, l_ready, e_done = sem("g_done"), sem("z_ready"), sem("l_ready"), sem("e_done")
        ve_done, ve_out = sem("ve_done"), sem("ve_out")
        x_in2 = [sem("x_again0"), sem("x_again1")]
        sm = sem("softmax_chain")
        sm_exp, sm_t1, sm_t2 = sem("softmax_exp"), sem("scores_turned"), sem("attn_turned")
        wv_ready, y1_done, y1_out, o1_done = sem("wv_ready"), sem("y1_done"), sem("y1_out"), sem("o1_done")
        ln1 = ln_sems("1")
        xs_hi, xs_lo = sem("xs_hi"), sem("xs_lo")
        pt_done, pt_hi, pt_lo = sem("pt_done"), sem("pt_hi"), sem("pt_lo")
        h1_done, h1_hi, h1_lo = sem("h1_done"), sem("h1_hi"), sem("h1_lo")
        qt_done, qt_hi, qt_lo = sem("qt_done"), sem("qt_hi"), sem("qt_lo")
        h2_done, h2_out = sem("h2_done"), sem("h2_out")
        s3_done, s3_hi, s3_lo = sem("s3_done"), sem("s3_hi"), sem("s3_lo")
        o2_done = sem("o2_done")
        ln2 = ln_sems("2")
        x3t_ready, x3r_ready, t3_done, xt3_out = sem("x3t_ready"), sem("x3r_ready"), sem("t3_done"), sem("xt3_out")
        s2_done, s1_out, tm_done, m_step = sem("s2_done"), sem("s1_out"), sem("tm_done"), sem("m_step")
        zt_ready, lk_ready, ex_ready = sem("zt_ready"), sem("lk_ready"), sem("ex_ready")
        exr_done, ext_out = sem("ex_turned"), sem("ext_out")
        ax_done, ax_out, o3_done, r_step = sem("ax_done"), sem("ax_out"), sem("o3_done"), sem("r_step")
        ln3 = ln_sems("3")
        stored = [sem("stored0"), sem("stored1")]

        x_nat = x.rearrange("b (t n) d -> n t b d", n=P)
        out_nat = out.rearrange("b (t n) d -> n t b d", n=P)

        setup1 = ExitStack()
        edge_i = sb("edge_i", [P, 2, E], I32, scope=setup1)
        edge_f = sb("edge_f", [P, 2, E], scope=setup1)
        key_row = sb("key_row", [P, E], scope=setup1)
        less = sb("less", [P, ET, E], scope=setup1)
        ecol_bc = sb("ecol_bc", [P, 2, ET, P], scope=setup1)
        degm = sb("degm", [P, T, N], scope=setup1)
        dinv_bc = sb("dinv_bc", [P, N], scope=setup1)
        root_bc = sb("root_bc", [P, N], scope=setup1)
        at1 = sb("at1", [P, T, N], scope=setup1)
        setup1.close()
        bnt = sb("bnt", [P, 2, W])
        y0 = sb("y0", [P, 2, T, 2, D])
        x1r = sb("x1r", [P, 2, T, 2, D])
        z1 = sb("z1", [P, 2, W])
        setup2 = ExitStack()
        perm = sb("perm", [P, ET, E], scope=setup2)
        sorted_bc = sb("sorted_bc", [P, 2, E], scope=setup2)
        ssrc = sb("ssrc", [P, T, E], scope=setup2)
        sdst = sb("sdst", [P, T, E], scope=setup2)
        prod = sb("prod", [P, T, E], scope=setup2)
        diff = sb("diff", [P, 2, E], scope=setup2)
        sq = sb("sq", [P, T, N], scope=setup2)
        adj_dst = sb("adj_dst", [P, T, E], scope=setup2)
        setup2.close()
        xs = hilo("xs", [P, 2, T, 2, D])
        x3t = sb("x3t", [P, 2, T, 2, D])
        x3r = sb("x3r", [P, 2, T, 2, D])
        ecol_i = sb("ecol_i", [P, 2, ET], I32)
        ecol_f = sb("ecol_f", [P, 2, ET], F32)
        key_col = sb("key_col", [P, ET], F32)
        rank = sb("rank", [P, ET], F32)
        sorted_col = sb("sorted_col", [P, ET], F32)
        dinv = sb("dinv", [P, T], F32)
        root = sb("root", [P, T], F32)
        scope0 = ExitStack()
        hraw = sb("hraw", [P, H0 // P, Q, W], scope=scope0)
        scope0.close()
        scope3 = ExitStack()
        vall = sb("vall", [P, ET, B, D], scope=scope3)
        vq = hilo("vq", [P, 2, T, 2, 2 * D], scope3)
        esb = sb("esb", [P, ET, P], scope=scope3)
        sc = sb("sc", [P, 6, E], scope=scope3)
        attn_t = sb("attn_t", [P, ET, P], scope=scope3)
        wv = sb("wv", [P, 2, ET, 2, D], scope=scope3)
        y1t = sb("y1t", [P, 2, W], scope=scope3)
        scope3.close()
        scope4 = ExitStack()
        pt = hilo("pt", [P, 2, W], scope4)
        h1 = hilo("h1", [P, 2, 2, T, H2A], scope4)
        qt = hilo("qt", [P, 2, GA, W], scope4)
        h2 = sb("h2", [P, 2, GB, W], scope=scope4)
        s3 = hilo("s3", [P, 2, T, 2, D], scope4)
        scope4.close()
        scope5 = ExitStack()
        xt3 = sb("xt3", [P, 2, W], scope=scope5)
        tm = sb("tm", [P, 2, 4, N], scope=scope5)
        zt = sb("zt", [P, 2, 4, N], scope=scope5)
        lk = sb("lk", [P, 2, 4, N], scope=scope5)
        ex = sb("ex", [P, 2, 4, N], scope=scope5)
        m3 = sb("m3", [P, 2, 4], scope=scope5)
        s1c = sb("s1c", [P, 2, 4], scope=scope5)
        zm = sb("zm", [P, 3, 2, 4], scope=scope5)
        rs = sb("rs", [P, 2, 4], scope=scope5)
        ri = sb("ri", [P, 2, 4], scope=scope5)
        ext = sb("ext", [P, 2, 2, 2, N], scope=scope5)
        axt = sb("axt", [P, 2, W], scope=scope5)
        y3 = sb("y3", [P, 2, T, 2, D], scope=scope5)
        ob = sb("ob", [P, 2, T, 2, D], scope=scope5)
        scope5.close()

        SMALL = 4
        block = ctx.enter_context(nc.Block())

        @block.sync
        def _(sp):
            sp.dma_start(adj_sb[:], adj.rearrange("(t p) m -> p t m", p=P)).then_inc(s_adj, 16)
            sp.dma_start(adjt_sb[:], adj_t.rearrange("(t p) m -> p t m", p=P)).then_inc(s_adj, 16)

            def load_x(s, q, to):
                sp.dma_start(xin[:, s, 0, :, :], x_nat[:, 0, bass.ds(2 * q, 2), :]).then_inc(to[s], 16)
                sp.dma_start(xin[:, s, 1, :, :], x_nat[:, 1, bass.ds(2 * q, 2), :]).then_inc(to[s], 16)

            load_x(0, 0, x_in)
            load_x(1, 1, x_in)
            sp.dma_start(w1_raw[:], w1_t).then_inc(s_small, 16)
            sp.dma_start(w2t[:], w2_t.rearrange("(k p) o -> p k o", p=P)).then_inc(s_small, 16)
            sp.dma_start(bnp[:], bn_cols).then_inc(s_small, 16)
            sp.dma_start(l3a_s[:], l3a).then_inc(s_small, 16)
            for k, v in enumerate((src, dst)):
                sp.dma_start(edge_i[:, k, :], v.partition_broadcast(P)).then_inc(s_edge, 16)
            sp.dma_start(ecol_i[:].rearrange("p a t -> p (a t)"), edge_cols).then_inc(s_edge, 16)
            with sp.Fori(1, IT) as p:
                for s in range(2):
                    sp.wait_ge(x0_lo, 2 * p + s - 1)
                    load_x(s, 2 * p + s, x_in)
            sp.wait_ge(x0_lo, Q)
            load_x(0, 0, x_in2)
            load_x(1, 1, x_in2)
            with sp.Fori(1, IT) as p:
                for s in range(2):
                    sp.wait_ge(ln0[0], 2 * p + s - 1)
                    load_x(s, 2 * p + s, x_in2)
            with sp.Fori(0, IT) as p:
                for s in range(2):
                    sp.wait_ge(ln3[5], 2 * p + s + 1)
                    for t in range(T):
                        sp.dma_start(out_nat[:, t, bass.ds(4 * p + 2 * s, 2), :], ob[:, s, t, :, :]).then_inc(stored[s], 16)
            for s in range(2):
                sp.wait_ge(stored[s], 32 * IT)

        @block.gpsimd
        def _(pool):
            steps = [0]

            def link(ins):
                steps[0] += 1
                ins.then_inc(pc, 1)
                pool.wait_ge(pc, steps[0])

            pool.memset(ident[:], 0.0).then_inc(pz, 1)
            pool.memset(ones[:], 1.0).then_inc(pz, 1)
            pool.memset(eps[:], LN_EPS).then_inc(pz, 1)
            pool.wait_ge(pz, 3)
            pool.affine_select(out=ident[:], in_=ident[:], compare_op=ALU.not_equal, fill=1.0, base=0,
                               pattern=[[-1, P]], channel_multiplier=1).then_inc(pz, 1)
            pool.memset(head_a[:], 0.0).then_inc(pz, 1)
            pool.iota(iota_row[:], pattern=[[1, N]], base=0, channel_multiplier=0,
                      allow_small_or_imprecise_dtypes=True).then_inc(pz, 1)
            pool.iota(iota_col[:], pattern=[[P, T]], base=0, channel_multiplier=1,
                      allow_small_or_imprecise_dtypes=True).then_inc(pz, 1)
            pool.memset(log_eps[:], LOG_EPS).then_inc(pz, 1)
            pool.memset(mhalf[:], -0.5).then_inc(pz, 1)
            pool.wait_ge(pz, 9)
            for h in range(HEADS):
                pool.dma_start(head_a[h * DH:(h + 1) * DH, h:h + 1],
                               a_head[h * DH:(h + 1) * DH, :]).then_inc(s_wts, 16)
            for to, frm in ((wvq_raw[:, 0, :], wv_t), (wvq_raw[:, 1, :], wq_t), (wot[:], wo_t),
                            (l2w1_raw[:], l2w1), (l2w2_raw[:], l2w2.rearrange("(k p) g -> p k g", p=P)),
                            (l2w3_s[:], l2w3.rearrange("(k p) g -> p k g", p=P)), (l3w_s[:], l3w), (l3wt_s[:], l3w_t)):
                pool.dma_start(to, frm).then_inc(s_wts, 16)

            pool.wait_ge(s_edge, 48)
            pool.tensor_copy(edge_f[:], edge_i[:])
            link(pool.tensor_copy(ecol_f[:], ecol_i[:]))
            pool.tensor_scalar(key_row[:], edge_f[:, 0, :], float(E), None, ALU.mult)
            link(pool.tensor_scalar(key_col[:], ecol_f[:, 0, :], float(E), None, ALU.mult))
            pool.tensor_tensor(key_row[:], key_row[:], iota_row[:, 0:E], ALU.add)
            link(pool.tensor_tensor(key_col[:], key_col[:], iota_col[:, 0:ET], ALU.add))
            for t in range(ET):
                i = pool.tensor_scalar(less[:, t, :], key_row[:], key_col[:, t:t + 1], None, ALU.is_lt)
            i.then_inc(keys_compared, 1)
            pool.wait_ge(ranks_ready, 1)
            for t in range(ET):
                i = pool.tensor_scalar(perm[:, t, :], iota_row[:, 0:E], rank[:, t:t + 1], None, ALU.is_equal)
            for k in range(2):
                for t in range(ET):
                    i = pool.tensor_scalar(ecol_bc[:, k, t, :], ones[:], ecol_f[:, k, t:t + 1], None, ALU.mult)
            i.then_inc(edges_ranked, 1)

            pool.wait_ge(s_wts, 16 * 12)
            pairs = ((wvq, wvq_raw[:].rearrange("p a b -> p (a b)")), (l2w1_s, l2w1_raw[:]), (l2w2_s, l2w2_raw[:]))
            for hl, raw in pairs:
                i = pool.tensor_copy(hl[0][:], raw)
            link(i)
            for hl, raw in pairs:
                i = pool.tensor_tensor(hl[1][:], raw, hl[0][:], ALU.subtract)
            i.then_inc(weights_split, 1)
            pool.wait_ge(s_adj, 32)
            link(pool.tensor_tensor(sq[:], adjt_sb[:], adjt_sb[:], ALU.mult))
            link(pool.tensor_copy(wgt[0][:], sq[:]))
            pool.tensor_scalar(mask[:], adj_sb[:], 0.0, -BIG, ALU.is_equal, ALU.mult)
            pool.tensor_tensor(wgt[1][:], sq[:], wgt[0][:], ALU.subtract).then_inc(wgt_ready, 1)

            pool.wait_ge(sorted_out, 1)
            for t in range(T):
                pool.tensor_scalar(ssrc[:, t, :], sorted_bc[:, 0, :], iota_col[:, t:t + 1], None, ALU.is_equal)
                pool.tensor_scalar(sdst[:, t, :], sorted_bc[:, 1, :], iota_col[:, t:t + 1], None, ALU.is_equal)
            for t in range(ET):
                pool.tensor_scalar(sel_src_t[:, t, :], iota_row[:], sorted_col[:, t:t + 1], None, ALU.is_equal)
            link(pool.memset(diff[:], 1.0))
            pool.tensor_tensor(sel_sum[:], ssrc[:], sdst[:], ALU.add)
            pool.tensor_copy(sel_dst[:], sdst[:]).then_inc(sel_ready, 1)
            pool.tensor_tensor(diff[:, 0, 1:E], sorted_bc[:, 0, 1:E], sorted_bc[:, 0, 0:E - 1], ALU.subtract)
            link(pool.tensor_tensor(diff[:, 1, 0:E - 1], sorted_bc[:, 0, 1:E], sorted_bc[:, 0, 0:E - 1], ALU.subtract))
            link(pool.tensor_scalar(same[:], diff[:], 0.0, None, ALU.is_equal))
            pool.tensor_scalar(reset[:], same[:], 1.0, BIG, ALU.subtract, ALU.mult)
            pool.tensor_scalar(wa2_bc[:], ones[:], wa[:, 1:2], None, ALU.mult).then_inc(wa2_ready, 1)
            pool.wait_ge(adj_dst_out, 1)
            pool.tensor_tensor(prod[:], adj_dst[:], ssrc[:], ALU.mult).then_inc(picked, 1)

            with pool.Fori(0, IT) as p:
                for s in range(2):
                    pool.wait_ge(ln0[5], 2 * p + s + 1)
                    pool.tensor_copy(xn[:, 2 * p + s], x1r[:, s]).then_inc(x1_kept, 1)

            def weigh(s, q, first):
                if not first:
                    pool.wait_ge(y1_done, q - 1)
                v = vall[:, :, bass.ds(2 * q, 2), :].rearrange("p t j (h c) -> p t (j h) c", c=DH)
                w = wv[:, s].rearrange("p t j (h c) -> p t (j h) c", c=DH)
                for t in range(ET):
                    a = attn_t[:, t, bass.ds(2 * HEADS * q, 2 * HEADS)].unsqueeze(2).broadcast_to([P, 2 * HEADS, DH])
                    i = pool.tensor_tensor(w[:, t], v[:, t], a, ALU.mult)
                i.then_inc(wv_ready, 1)

            def split_x(s, q, first):
                pool.wait_ge(ln1[5], q + 1)
                if not first:
                    pool.wait_ge(pt_done, q - 1)
                pool.tensor_copy(xs[0][:, s], xn[:, q]).then_inc(xs_hi, 1)
                pool.wait_ge(pz, 1)
                pool.wait_ge(xs_hi, q + 1)
                pool.tensor_tensor(xs[1][:, s], xn[:, q], xs[0][:, s], ALU.subtract).then_inc(xs_lo, 1)

            def power(p, sems):
                pool.wait_ge(sems[3], p + 1)
                pool.tensor_tensor(lnr[:].rearrange("p s k -> p (s k)"), lnv[:].rearrange("p s k -> p (s k)"), mhalf[:],
                                   ALU.pow).then_inc(sems[4], 1)

            pool.wait_ge(ve_out, Q)
            pool.wait_ge(sm, 10)
            weigh(0, 0, True)
            weigh(1, 1, True)
            weigh(0, 2, False)
            weigh(1, 3, False)
            with pool.Fori(1, IT - 1) as p:
                power(p - 1, ln1)
                for s in range(2):
                    weigh(s, 2 * p + s + 2, False)
            power(IT - 2, ln1)
            split_x(0, 0, True)
            split_x(1, 1, True)
            power(IT - 1, ln1)
            with pool.Fori(1, IT) as p:
                for s in range(2):
                    split_x(s, 2 * p + s, False)

            def take_turned(s, q, first):
                pool.wait_ge(ln2[5], q + 1)
                if not first:
                    pool.wait_ge(t3_done, q - 1)
                pool.tensor_copy(x3t[:, s], xn[:, q]).then_inc(x3t_ready, 1)

            def take_values(s, q, first):
                if not first:
                    pool.wait_ge(ax_done, q - 1)
                pool.tensor_copy(x3r[:, s], xn[:, q]).then_inc(x3r_ready, 1)

            for s in range(2):
                take_turned(s, s, True)
            for s in range(2):
                take_turned(s, 2 + s, False)
            for s in range(2):
                take_values(s, s, True)
            for i in (2, 3):
                for s in range(2):
                    take_turned(s, 2 * i + s, False)
            for s in range(2):
                take_values(s, 2 + s, False)
            with pool.Fori(1, IT - 3) as p:
                power(p - 1, ln3)
                for s in range(2):
                    take_turned(s, 2 * p + s + 6, False)
                for s in range(2):
                    take_values(s, 2 * p + s + 2, False)
            for p in (IT - 3, IT - 2):
                power(p - 1, ln3)
                for s in range(2):
                    take_values(s, 2 * p + s + 2, False)
            power(IT - 2, ln3)
            power(IT - 1, ln3)

        @block.vector
        def _(dve):
            steps = [0]

            def link(ins):
                steps[0] += 1
                ins.then_inc(dc, 1)
                dve.wait_ge(dc, steps[0])

            dve.wait_ge(pz, 4)
            dve.wait_ge(s_adj, 32)
            dve.tensor_tensor(degm[:], adj_sb[:], adjt_sb[:], ALU.add)
            for t in range(T):
                blk = slice(t * P, (t + 1) * P)
                i = dve.tensor_tensor(prod[:, t, blk], adj_sb[:, t, blk], ident[:], ALU.mult)
            link(i)
            for t in range(T):
                blk = slice(t * P, (t + 1) * P)
                i = dve.tensor_tensor(degm[:, t, blk], degm[:, t, blk], prod[:, t, blk], ALU.subtract)
            link(i)
            for t in range(T):
                blk = slice(t * P, (t + 1) * P)
                i = dve.tensor_tensor(degm[:, t, blk], degm[:, t, blk], ident[:], ALU.add)
            i.then_inc(deg_ready, 1)
            link(dve.tensor_copy(at1[:], adjt_sb[:]))
            for t in range(T):
                blk = slice(t * P, (t + 1) * P)
                i = dve.tensor_tensor(at1[:, t, blk], at1[:, t, blk], ident[:], ALU.add)
            link(i)
            dve.wait_ge(s_small, 16 * SMALL)
            link(dve.tensor_copy(w1t[0][:], w1_raw[:]))
            dve.tensor_tensor(w1t[1][:], w1_raw[:], w1t[0][:], ALU.subtract)
            dve.wait_ge(deg_root, 1)
            dve.reciprocal(dinv_bc[:], root_bc[:])
            link(dve.reciprocal(dinv[:], root[:]))
            for t in range(T):
                i = dve.scalar_tensor_tensor(out=at1[:, t, :], in0=at1[:, t, :], scalar=dinv[:, t:t + 1],
                                             in1=dinv_bc[:], op0=ALU.mult, op1=ALU.mult)
            link(i)
            link(dve.tensor_copy(a_hat[0][:], at1[:]))
            dve.tensor_tensor(a_hat[1][:], at1[:], a_hat[0][:], ALU.subtract).then_inc(a_hat_ready, 1)
            def x0_low(p):
                for s in range(2):
                    dve.wait_ge(x0_hi, 2 * p + s + 1)
                    dve.tensor_tensor(x0[1][:, s], xin[:, s], x0[0][:, s], ALU.subtract).then_inc(x0_lo, 1)

            def agg_low(p):
                for s in range(2):
                    dve.wait_ge(agg_hi, 2 * p + s + 1)
                    dve.tensor_tensor(aggt[1][:, s, :], bank(s)[:, 0, :], aggt[0][:, s, :], ALU.subtract).then_inc(agg_lo, 1)

            def h_stats(p):
                for s in range(2):
                    q = 2 * p + s
                    wait_apart(dve, h_out, q + 1)
                    for k in range(H0 // P):
                        i = dve.bn_stats(bst1[:, k, q, :], hraw[:, k, q, :])
                    i.then_inc(h_stat, 1)

            x0_low(0)
            agg_low(0)
            dve.wait_ge(keys_compared, 1)
            dve.tensor_reduce(rank[:], less[:], AX_X, ALU.add).then_inc(ranks_ready, 1)
            x0_low(1)
            with dve.Fori(1, IT - 1) as p:
                agg_low(p)
                x0_low(p + 1)
                h_stats(p - 1)
            agg_low(IT - 1)
            h_stats(IT - 2)
            h_stats(IT - 1)
            dve.wait_ge(h_stat, Q)

            cs = [0]

            def bn_link(ins):
                cs[0] += 1
                ins.then_inc(bn_chain, 1)
                dve.wait_ge(bn_chain, cs[0])

            def coefficients(ks, stats, bias, gamma, beta, turn):
                mean, rstd, scale, shift = (bco[:, c, ks] for c in range(4))
                for n, k in enumerate(range(ks.start, ks.stop)):
                    i = dve.bn_aggr(bagg[:, k, :], stats[n])
                i.then_inc(bn_var, 1)
                dve.wait_ge(bn_var, turn)
                bn_link(dve.tensor_tensor(mean, bagg[:, ks, 0], bias, ALU.add))
                dve.wait_ge(bn_root, turn)
                bn_link(dve.reciprocal(rstd, rstd))
                dve.tensor_tensor(shift, bias, mean, ALU.subtract)
                bn_link(dve.tensor_tensor(scale, rstd, gamma, ALU.mult))
                bn_link(dve.tensor_tensor(shift, shift, scale, ALU.mult))
                return dve.tensor_tensor(shift, shift, beta, ALU.add)

            coefficients(slice(0, 2), [bst1[:, k].rearrange("p q c -> p (q c)") for k in range(2)],
                         bnp[:, 0:2], bnp[:, 2:4], bnp[:, 4:6], 1).then_inc(bn1_ready, 1)

            with dve.Fori(0, IT) as p:
                for s in range(2):
                    q = 2 * p + s
                    dve.wait_ge(o_done, q + 1)
                    dve.tensor_copy(oraw[:, q, :], bank(s)[:, 0, :]).then_inc(o_out, 1)
                    wait_apart(dve, o_out, q + 1)
                    dve.bn_stats(bst2[:, q, :], oraw[:, q, :]).then_inc(o_stat, 1)
            dve.wait_ge(o_stat, Q)
            coefficients(slice(2, 3), [bst2[:].rearrange("p q c -> p (q c)")],
                         bnp[:, 6:7], bnp[:, 7:8], bnp[:, 8:9], 2).then_inc(bn2_ready, 1)

            def y0_of(s, t, j):
                return y0[:, s, t, j, :]

            def sum0(p):
                for s in range(2):
                    q = 2 * p + s
                    dve.wait_ge(t1_done, q + 1)
                    dve.wait_ge(x_in2[s], 32 * (p + 1))
                    dve.tensor_tensor(y0[:, s], bank(s)[:, 0, :].rearrange("p (t j d) -> p t j d", t=T, j=2),
                                      xin[:, s], ALU.add).then_inc(ln0[0], 1)
                ln_stats(dve, y0_of, p, ln0)

            def norm0(p, first):
                ln_rstd(dve, p, ln0)
                for s in range(2):
                    if not first:
                        dve.wait_ge(x1_kept, 2 * p + s - 1)
                        dve.wait_ge(t2_done, 2 * p + s - 1)
                    ln_apply(dve, y0_of, lambda t, j: x1r[:, s, t, j, :], p, s, ln0)

            def x1_low(p):
                for s in range(2):
                    q = 2 * p + s
                    dve.wait_ge(xt_hi, q + 1)
                    dve.tensor_tensor(xt[1][:, s, :], bank(s)[:, 0, :], xt[0][:, s, :], ALU.subtract).then_inc(xt_lo, 1)

            def vq_low(p):
                for s in range(2):
                    q = 2 * p + s
                    dve.wait_ge(vq_hi_ok, q + 1)
                    dve.tensor_tensor(vq[1][:, s], vq_bank(s), vq[0][:, s], ALU.subtract).then_inc(vq_lo_ok, 1)

            def leaky(p):
                for s in range(2):
                    q = 2 * p + s
                    dve.wait_ge(z_ready, q + 1)
                    dve.scalar_tensor_tensor(out=l1[:, s, :], in0=z1[:, s, :], scalar=SLOPE, in1=z1[:, s, :],
                                             op0=ALU.mult, op1=ALU.max).then_inc(l_ready, 1)

            dve.wait_ge(o_done, Q)
            sum0(0)
            norm0(0, True)
            x1_low(0)
            with dve.Fori(0, IT - 1) as p:
                sum0(p + 1)
                vq_low(p)
                norm0(p + 1, False)
                leaky(p)
                x1_low(p + 1)
            vq_low(IT - 1)
            leaky(IT - 1)

            ss = [0]

            def sm_link(ins):
                ss[0] += 1
                ins.then_inc(sm, 1)
                dve.wait_ge(sm, ss[0])

            dve.wait_ge(e_done, Q)
            sm_link(dve.tensor_copy(esb[:], bank(7)[:, 0, 0:2 * P].rearrange("p (t c) -> p t c", t=ET)))
            dve.wait_ge(sm_t1, 1)
            dve.wait_ge(log_ready, 1)
            score, fwd, top, ssum, total = (sc[:, k, :] for k in range(5))
            rev = slice(None, None, -1)
            sm_link(dve.tensor_tensor(score, bank(5)[:, 0, 0:E], log_a[:], ALU.add))
            sm_link(dve.tensor_tensor_scan(fwd, reset[:, 0, :], score, -BIG, ALU.add, ALU.max))
            sm_link(dve.tensor_tensor_scan(top[:, rev], reset[:, 1, rev], fwd[:, rev], -BIG, ALU.add, ALU.max))
            sm_link(dve.tensor_tensor(score, score, top, ALU.subtract))
            dve.wait_ge(sm_exp, 1)
            sm_link(dve.tensor_tensor_scan(fwd, same[:, 0, :], sc[:, 5, :], 0.0, ALU.mult, ALU.add))
            sm_link(dve.tensor_tensor_scan(total[:, rev], reset[:, 1, rev], fwd[:, rev], -BIG, ALU.add, ALU.max))
            sm_link(dve.reciprocal(ssum, total))
            sm_link(dve.tensor_tensor(score, sc[:, 5, :], ssum, ALU.mult))
            dve.wait_ge(sm_t2, 1)
            sm_link(dve.tensor_copy(attn_t[:], bank(6)[:, 0, 0:2 * P].rearrange("p (t c) -> p t c", t=ET)))

            def add_ln(s, q, done, psum_bank, sems):
                dve.wait_ge(done, q + 1)
                xq = xn[:, q]
                dve.tensor_tensor(xq, bank(psum_bank)[:, 0, :].rearrange("p (t j d) -> p t j d", t=T, j=2), xq,
                                  ALU.add).then_inc(sems[0], 1)

            def row(p):
                return lambda s, t, j: xn[:, 2 * p + s, t, j, :]

            def apply(p, sems):
                for s in range(2):
                    ln_apply(dve, row(p), lambda t, j: row(p)(s, t, j), p, s, sems)

            def norm(p, sems):
                ln_stats(dve, row(p), p, sems)
                ln_rstd(dve, p, sems)
                apply(p, sems)

            def layer1(p, first):
                for s in range(2):
                    add_ln(s, 2 * p + s, o1_done, 2 + s, ln1)
                if not first:
                    apply(p - 1, ln1)

            def variance1(p, first):
                if not first:
                    wait_apart(dve, ln1[5], 2 * p)
                ln_stats(dve, row(p), p, ln1)
                var_eps(dve, p, ln1)

            layer1(0, True)
            variance1(0, True)
            with dve.Fori(1, IT - 1) as p:
                layer1(p, False)
                variance1(p, False)
            layer1(IT - 1, False)

            def layer2(p, first, last):
                for s in range(2):
                    dve.wait_ge(pt_hi, 2 * p + s + 1)
                    dve.tensor_tensor(pt[1][:, s, :], bank(4 + s)[:, 0, :], pt[0][:, s, :], ALU.subtract).then_inc(pt_lo, 1)
                for s in range(2):
                    dve.wait_ge(h1_hi, 2 * p + s + 1)
                    dve.scalar_tensor_tensor(out=h1[1][:, s].rearrange("p j t f -> p (j t f)"),
                                             in0=bank(2 * s, 2).rearrange("p k c -> p (k c)"), scalar=0.0,
                                             in1=h1[0][:, s].rearrange("p j t f -> p (j t f)"),
                                             op0=ALU.max, op1=ALU.subtract).then_inc(h1_lo, 1)
                for s in range(2):
                    dve.wait_ge(qt_hi, 2 * p + s + 1)
                    dve.tensor_tensor(qt[1][:, s], bank(2 * s, 2), qt[0][:, s], ALU.subtract).then_inc(qt_lo, 1)
                if first:
                    variance1(IT - 1, False)
                    apply(IT - 1, ln1)
                else:
                    norm(p - 1, ln2)
                for s in range(2):
                    dve.wait_ge(s3_hi, 2 * p + s + 1)
                    dve.tensor_tensor(s3[1][:, s], bank(s)[:, 0, :].rearrange("p (t j d) -> p t j d", t=T, j=2),
                                      s3[0][:, s], ALU.subtract).then_inc(s3_lo, 1)
                if last:
                    scores3(0)
                for s in range(2):
                    add_ln(s, 2 * p + s, o2_done, 2 + s, ln2)

            def scores3(p):
                for s in range(2):
                    q = 2 * p + s
                    dve.wait_ge(s2_done, q + 1)
                    dve.tensor_copy(s1c[:, s, :], bank(6 + s)[:, 0, 0:4]).then_inc(s1_out, 1)
                    for k in range(4):
                        i = dve.tensor_tensor_reduce(out=tm[:, s, k, :], in0=bank(4 + s)[:, 0, (k % 2) * N:(k % 2 + 1) * N],
                                                     in1=mask[:, k // 2, :], scale=1.0, scalar=-2 * BIG, op0=ALU.add,
                                                     op1=ALU.max, accum_out=m3[:, s, k:k + 1])
                    i.then_inc(tm_done, 1)
                dve.wait_ge(tm_done, 2 * p + 2)
                dve.wait_ge(s1_out, 2 * p + 2)
                dve.tensor_tensor(zm[:, 0], m3[:], s1c[:], ALU.add).then_inc(m_step, 1)
                dve.wait_ge(m_step, 3 * p + 1)
                dve.scalar_tensor_tensor(out=zm[:, 1], in0=zm[:, 0], scalar=SLOPE, in1=zm[:, 0],
                                         op0=ALU.mult, op1=ALU.max).then_inc(m_step, 1)
                dve.wait_ge(m_step, 3 * p + 2)
                dve.tensor_scalar(zm[:, 2], zm[:, 1], -1.0, None, ALU.mult).then_inc(m_step, 1)

            def leaky3(p):
                for s in range(2):
                    dve.wait_ge(zt_ready, 2 * p + s + 1)
                    dve.scalar_tensor_tensor(out=lk[:, s].rearrange("p k n -> p (k n)"),
                                             in0=zt[:, s].rearrange("p k n -> p (k n)"), scalar=SLOPE,
                                             in1=zt[:, s].rearrange("p k n -> p (k n)"),
                                             op0=ALU.mult, op1=ALU.max).then_inc(lk_ready, 1)

            def weights3(p, first):
                if not first:
                    dve.wait_ge(ln3[0], 2 * p)
                dve.wait_ge(ex_ready, 2 * p + 2)
                dve.reciprocal(ri[:], rs[:]).then_inc(r_step, 1)

            def sum3(p, first):
                if not first:
                    dve.wait_ge(ln3[5], 2 * p)
                dve.wait_ge(r_step, p + 1)
                for s in range(2):
                    q = 2 * p + s
                    dve.wait_ge(o3_done, q + 1)
                    for t in range(T):
                        for j in range(2):
                            k = 2 * t + j
                            i = dve.scalar_tensor_tensor(
                                out=y3[:, s, t, j, :], in0=bank(2 * s + 1)[:, 0, k * D:(k + 1) * D], scalar=ri[:, s, k:k + 1],
                                in1=xn[:, q, t, j, :], op0=ALU.mult, op1=ALU.add)
                    i.then_inc(ln3[0], 1)

            def y3_of(s, t, j):
                return y3[:, s, t, j, :]

            def norm3(p, first):
                for s in range(2):
                    if not first:
                        dve.wait_ge(stored[s], 32 * p)
                    ln_apply(dve, y3_of, lambda t, j: ob[:, s, t, j, :], p, s, ln3)

            layer2(0, True, False)
            with dve.Fori(1, IT - 1) as p:
                layer2(p, False, False)
            layer2(IT - 1, False, True)
            leaky3(0)
            ln_stats(dve, row(IT - 1), IT - 1, ln2)
            weights3(0, True)
            scores3(1)
            ln_rstd(dve, IT - 1, ln2)
            apply(IT - 1, ln2)
            leaky3(1)
            sum3(0, True)

            def step3(p, first, last):
                weights3(p, False)
                if not last:
                    scores3(p + 1)
                ln_stats(dve, y3_of, p - 1, ln3)
                var_eps(dve, p - 1, ln3)
                if not last:
                    leaky3(p + 1)
                norm3(p - 1, first)
                sum3(p, False)

            step3(1, True, False)
            with dve.Fori(2, IT - 1) as p:
                step3(p, False, False)
            step3(IT - 1, False, True)
            ln_stats(dve, y3_of, IT - 1, ln3)
            var_eps(dve, IT - 1, ln3)
            norm3(IT - 1, False)

        @block.scalar
        def _(act):
            def x0_high(p):
                for s in range(2):
                    act.wait_ge(x_in[s], 32 * (p + 1))
                    act.activation(x0[0][:, s], xin[:, s], ACT.Copy).then_inc(x0_hi, 1)

            def agg_high(p):
                for s in range(2):
                    act.wait_ge(agg_done, 2 * p + s + 1)
                    act.activation(aggt[0][:, s, :], bank(s)[:, 0, :], ACT.Copy).then_inc(agg_hi, 1)

            def h_raw(p):
                for s in range(2):
                    q = 2 * p + s
                    act.wait_ge(h_done, q + 1)
                    act.activation(hraw[:, :, q, :], bank(2 + 2 * s, 2), ACT.Copy).then_inc(h_out, 1)

            act.wait_ge(deg_done, 1)
            act.activation(root_bc[:], bank(0)[:, 0, 0:N], ACT.Sqrt)
            act.activation(root[:], bank(1)[:, 0, 0:T], ACT.Sqrt).then_inc(deg_root, 1)
            x0_high(0)
            with act.Fori(0, IT - 1) as p:
                agg_high(p)
                x0_high(p + 1)
                h_raw(p)
            agg_high(IT - 1)
            h_raw(IT - 1)
            act.wait_ge(edges_sorted, 1)
            act.activation(sorted_bc[:], bank(6)[:, 0, :].rearrange("p (a e) -> p a e", a=2), ACT.Copy)
            act.activation(wa[:], bank(7)[:, 0, 4:6], ACT.Copy)
            act.activation(sorted_col[:], bank(7)[:, 0, 0:ET], ACT.Copy).then_inc(sorted_out, 1)

            def bn_sqrt(ks, turn):
                act.wait_ge(bn_var, turn)
                act.activation(bco[:, 1, ks], bagg[:, ks, 1], ACT.Sqrt, bias=eps[:]).then_inc(bn_root, 1)

            bn_sqrt(slice(0, 2), 1)
            act.wait_ge(bn1_ready, 1)
            with act.Fori(0, Q) as q:
                for k in range(H0 // P):
                    i = act.activation(hraw[:, k, q, :], hraw[:, k, q, :], ACT.Relu, bias=bco[:, 3, k:k + 1], scale=bco[:, 2, k:k + 1])
                i.then_inc(relu_ready, 1)

            act.wait_ge(adj_dst_done, 1)
            act.activation(adj_dst[:], bank(6)[:, 0, :].rearrange("p (t e) -> p t e", t=T), ACT.Copy).then_inc(adj_dst_out, 1)
            bn_sqrt(slice(2, 3), 2)
            act.wait_ge(bn2_ready, 1)

            def bn_out(p, first):
                for s in range(2):
                    q = 2 * p + s
                    if not first:
                        act.wait_ge(t1_done, q - 1)
                    act.activation(bnt[:, s, :], oraw[:, q, :], ACT.Identity, bias=bco[:, 3, 2:3], scale=bco[:, 2, 2:3]).then_inc(bnt_ready, 1)

            def x1_high(p):
                for s in range(2):
                    q = 2 * p + s
                    act.wait_ge(t2_done, q + 1)
                    act.activation(xt[0][:, s, :], bank(s)[:, 0, :], ACT.Copy).then_inc(xt_hi, 1)

            def vq_high(p):
                for s in range(2):
                    q = 2 * p + s
                    act.wait_ge(vq_done, q + 1)
                    act.activation(vq[0][:, s], vq_bank(s), ACT.Copy).then_inc(vq_hi_ok, 1)

            def gathered(p):
                for s in range(2):
                    q = 2 * p + s
                    act.wait_ge(g_done, q + 1)
                    act.activation(z1[:, s, :], bank(2 + 2 * s)[:, 0, :], ACT.Copy).then_inc(z_ready, 1)
                for s in range(2):
                    q = 2 * p + s
                    act.wait_ge(ve_done, q + 1)
                    act.activation(vall[:, :, bass.ds(2 * q, 2), :],
                                   bank(3 + 2 * s)[:, 0, :].rearrange("p (t j d) -> p t j d", t=ET, j=2), ACT.Copy).then_inc(ve_out, 1)

            bn_out(0, True)
            ln_root(act, 0, ln0)
            bn_out(1, False)
            x1_high(0)
            with act.Fori(0, IT - 2) as p:
                vq_high(p)
                ln_root(act, p + 1, ln0)
                gathered(p)
                bn_out(p + 2, False)
                x1_high(p + 1)
            vq_high(IT - 2)
            ln_root(act, IT - 1, ln0)
            gathered(IT - 2)
            x1_high(IT - 1)
            vq_high(IT - 1)
            gathered(IT - 1)
            act.wait_ge(a_edge_done, 1)
            act.activation(log_a[:], bank(6)[:, 0, 0:E], ACT.Ln, bias=log_eps[:]).then_inc(log_ready, 1)
            act.wait_ge(sm, 5)
            act.activation(sc[:, 5, :], sc[:, 0, :], ACT.Exp).then_inc(sm_exp, 1)
            with act.Fori(0, IT) as p:
                for s in range(2):
                    q = 2 * p + s
                    act.wait_ge(y1_done, q + 1)
                    act.activation(y1t[:, s, :], bank(s)[:, 0, :], ACT.Copy).then_inc(y1_out, 1)

            def layer2(p, first):
                for s in range(2):
                    act.wait_ge(pt_done, 2 * p + s + 1)
                    act.activation(pt[0][:, s, :], bank(4 + s)[:, 0, :], ACT.Copy).then_inc(pt_hi, 1)
                for s in range(2):
                    act.wait_ge(h1_done, 2 * p + s + 1)
                    act.activation(h1[0][:, s].rearrange("p j t f -> p (j t f)"), bank(2 * s, 2).rearrange("p k c -> p (k c)"),
                                   ACT.Relu).then_inc(h1_hi, 1)
                for s in range(2):
                    act.wait_ge(qt_done, 2 * p + s + 1)
                    act.activation(qt[0][:, s], bank(2 * s, 2), ACT.Copy).then_inc(qt_hi, 1)
                for s in range(2):
                    for g in range(GB):
                        act.wait_ge(h2_done, GB * (2 * p + s) + g + 1)
                        act.activation(h2[:, s, g, :], bank(4 + g)[:, 0, :], ACT.Relu).then_inc(h2_out, 1)
                        if s == 0 and g == 2 and not first:
                            ln_root(act, p - 1, ln2)
                for s in range(2):
                    act.wait_ge(s3_done, 2 * p + s + 1)
                    act.activation(s3[0][:, s], bank(s)[:, 0, :].rearrange("p (t j d) -> p t j d", t=T, j=2),
                                   ACT.Copy).then_inc(s3_hi, 1)

            def turned3(p):
                for s in range(2):
                    act.wait_ge(t3_done, 2 * p + s + 1)
                    act.activation(xt3[:, s, :], bank(4 + s)[:, 0, :], ACT.Copy).then_inc(xt3_out, 1)

            def sum_scores(p, s):
                act.wait_ge(tm_done, 2 * p + s + 1)
                act.wait_ge(s1_out, 2 * p + s + 1)
                for k in range(4):
                    i = act.activation(zt[:, s, k, :], tm[:, s, k, :], ACT.Identity, bias=s1c[:, s, k:k + 1])
                i.then_inc(zt_ready, 1)

            def exps(p, s, first):
                act.wait_ge(m_step, 3 * p + 3)
                act.wait_ge(lk_ready, 2 * p + s + 1)
                if not first:
                    act.wait_ge(r_step, p)
                    act.wait_ge(exr_done, 2 * p + s - 1)
                for k in range(4):
                    i = act.activation(ex[:, s, k, :], lk[:, s, k, :], ACT.Exp, bias=zm[:, 2, s, k:k + 1],
                                       accum_out=rs[:, s, k:k + 1])
                i.then_inc(ex_ready, 1)

            def turned_exps(p, s):
                act.wait_ge(exr_done, 2 * p + s + 1)
                act.activation(ext[:, s].rearrange("p j t n -> p (j t n)"),
                               bank(2 * s, 2).rearrange("p k c -> p (k c)"), ACT.Copy).then_inc(ext_out, 1)

            def attended(p, s):
                act.wait_ge(ax_done, 2 * p + s + 1)
                act.activation(axt[:, s, :], bank(2 * s)[:, 0, :], ACT.Copy).then_inc(ax_out, 1)

            def step3(p, turn, soft):
                if soft:
                    sum_scores(p + 1, 0)
                turned_exps(p, 0)
                turned_exps(p, 1)
                if soft:
                    sum_scores(p + 1, 1)
                if turn:
                    turned3(p + 2)
                if soft:
                    exps(p + 1, 0, False)
                attended(p, 0)
                if soft:
                    exps(p + 1, 1, False)
                attended(p, 1)

            layer2(0, True)
            with act.Fori(1, IT) as p:
                layer2(p, False)
            turned3(0)
            for s in range(2):
                sum_scores(0, s)
            turned3(1)
            for s in range(2):
                exps(0, s, True)
            ln_root(act, IT - 1, ln2)
            with act.Fori(0, IT - 2) as p:
                step3(p, True, True)
            step3(IT - 2, False, True)
            step3(IT - 1, False, False)

        @block.tensor
        def _(pe):
            pe.wait_ge(deg_ready, 1)
            for t in range(T):
                pe.matmul(bank(0)[:, 0, 0:N], ones[:], degm[:, t, :], start=(t == 0), stop=(t == T - 1))
            for m in range(T):
                for t in range(T):
                    i = pe.matmul(bank(1)[:, 0, m:m + 1], degm[:, t, m * P:(m + 1) * P], ones[:, 0:1],
                                  start=(t == 0), stop=(t == T - 1))
            i.then_inc(deg_done, 1)
            pe.wait_ge(a_hat_ready, 1)

            def pass1(p, first):
                for s in range(2):
                    pe.wait_ge(x0_lo, 2 * p + s + 1)
                    for j in range(2):
                        for t in range(T):
                            i = three(pe, bank(s)[:, 0, j * N:(j + 1) * N], [h[:, s, t, j, :] for h in x0],
                                      [h[:, t, :] for h in a_hat], t == 0, t == T - 1)
                    i.then_inc(agg_done, 1)
                for s in range(2):
                    q = 2 * p + s
                    pe.wait_ge(agg_lo, q + 1)
                    if not first:
                        pe.wait_ge(h_out, q - 1)
                    for k in range(H0 // P):
                        i = three(pe, bank(2 + 2 * s + k)[:, 0, :], [h[:, k * P:(k + 1) * P] for h in w1t],
                                  [h[:, s, :] for h in aggt], True, True)
                    i.then_inc(h_done, 1)

            pass1(0, True)
            with pe.Fori(1, IT) as p:
                pass1(p, False)

            pe.wait_ge(edges_ranked, 1)
            for k in range(2):
                for t in range(ET):
                    pe.matmul(bank(6)[:, 0, k * E:(k + 1) * E], ecol_bc[:, k, t, :], perm[:, t, :], start=(t == 0), stop=(t == ET - 1))
            pe.wait_ge(s_wts, 16 * 12)
            pe.wait_ge(s_small, 16 * SMALL)
            pe.matmul(bank(7)[:, 0, 4:6], l3wt_s[:], l3a_s[:], start=True, stop=True)
            for m in range(ET):
                for t in range(ET):
                    i = pe.matmul(bank(7)[:, 0, m:m + 1], perm[:, t, m * P:(m + 1) * P], ecol_f[:, 0, t:t + 1],
                                  start=(t == 0), stop=(t == ET - 1))
            i.then_inc(edges_sorted, 1)

            def pass2(p, first):
                for s in range(2):
                    q = 2 * p + s
                    pe.wait_ge(relu_ready, q + 1)
                    if not first:
                        pe.wait_ge(o_out, q - 1)
                    for k in range(H0 // P):
                        i = pe.matmul(bank(s)[:, 0, :], w2t[:, k, :], hraw[:, k, q, :], start=(k == 0), stop=(k == 1))
                    i.then_inc(o_done, 1)

            pass2(0, True)
            with pe.Fori(1, IT) as p:
                pass2(p, False)

            pe.wait_ge(sel_ready, 1)
            for n in range(T):
                for t in range(T):
                    i = pe.matmul(bank(6)[:, 0, n * E:(n + 1) * E], adjt_sb[:, t, n * P:(n + 1) * P], sdst[:, t, :],
                                  start=(t == 0), stop=(t == T - 1))
            i.then_inc(adj_dst_done, 1)

            pe.wait_ge(weights_split, 1)
            pe.wait_ge(o_out, Q)

            def turn_out(p, first):
                for s in range(2):
                    q = 2 * p + s
                    pe.wait_ge(bnt_ready, q + 1)
                    if not first:
                        pe.wait_ge(xt_lo, q - 1)
                    for t in range(T):
                        for j in range(2):
                            k = 2 * t + j
                            i = pe.transpose(bank(s)[:, 0, k * P:(k + 1) * P], bnt[:, s, j * N + t * P:j * N + (t + 1) * P], ident[:])
                    i.then_inc(t1_done, 1)

            def turn_x1(p):
                for s in range(2):
                    q = 2 * p + s
                    pe.wait_ge(ln0[5], q + 1)
                    for j in range(2):
                        for t in range(T):
                            k = 2 * j + t
                            i = pe.transpose(bank(s)[:, 0, k * P:(k + 1) * P], x1r[:, s, t, j, :], ident[:])
                    i.then_inc(t2_done, 1)

            def project(p, first):
                for s in range(2):
                    q = 2 * p + s
                    pe.wait_ge(xt_lo, q + 1)
                    if not first:
                        pe.wait_ge(z_ready, q - 1)
                        pe.wait_ge(ve_out, q - 1)
                    for t in range(T):
                        for j in range(2):
                            c = j * N + t * P
                            i = three(pe, vq_bank(s)[:, t, j, :], [h[:, s, c:c + P] for h in xt], [h[:] for h in wvq], True, True)
                    i.then_inc(vq_done, 1)

            def gather(p):
                for s in range(2):
                    q = 2 * p + s
                    pe.wait_ge(vq_lo_ok, q + 1)
                    for j in range(2):
                        for n, (t, h) in enumerate((t, h) for t in range(T) for h in range(2)):
                            i = pe.matmul(bank(2 + 2 * s)[:, 0, j * E:(j + 1) * E], vq[h][:, s, t, j, D:2 * D], sel_sum[:, t, :],
                                          start=(n == 0), stop=(n == 3))
                    i.then_inc(g_done, 1)
                for s in range(2):
                    for e in range(ET):
                        for n, (t, h) in enumerate((t, h) for t in range(T) for h in range(2)):
                            i = pe.matmul(bank(3 + 2 * s)[:, 0, e * 2 * D:(e + 1) * 2 * D], sel_dst[:, t, e * P:(e + 1) * P],
                                          vq[h][:, s, t, :, 0:D], start=(n == 0), stop=(n == 3))
                    i.then_inc(ve_done, 1)

            def score(p):
                for s in range(2):
                    q = 2 * p + s
                    pe.wait_ge(l_ready, q + 1)
                    for e in range(ET):
                        for j in range(2):
                            i = pe.matmul(bank(7)[:, 0, bass.ds(e * P + HEADS * (2 * q + j), HEADS)],
                                          l1[:, s, j * E + e * P:j * E + (e + 1) * P], head_a[:], start=True, stop=True)
                    i.then_inc(e_done, 1)

            turn_out(0, True)
            turn_x1(0)
            turn_out(1, False)
            project(0, True)
            gather(0)
            turn_x1(1)
            score(0)
            with pe.Fori(1, IT - 1) as p:
                turn_out(p + 1, False)
                project(p, False)
                gather(p)
                turn_x1(p + 1)
                score(p)
            project(IT - 1, False)
            gather(IT - 1)
            score(IT - 1)
            pe.wait_ge(picked, 1)
            for t in range(T):
                i = pe.matmul(bank(6)[:, 0, 0:E], ones[:], prod[:, t, :], start=(t == 0), stop=(t == T - 1))
            i.then_inc(a_edge_done, 1)

            pe.wait_ge(ve_out, Q)
            pe.wait_ge(sm, 1)
            for t in range(ET):
                i = pe.transpose(bank(5)[:, 0, t * P:(t + 1) * P], esb[:, t, :], ident[:])
            i.then_inc(sm_t1, 1)
            pe.wait_ge(sm, 9)
            for t in range(ET):
                i = pe.transpose(bank(6)[:, 0, t * P:(t + 1) * P], sc[:, 0, t * P:(t + 1) * P], ident[:])
            i.then_inc(sm_t2, 1)

            def layer1b(p, first):
                for s in range(2):
                    q = 2 * p + s
                    pe.wait_ge(wv_ready, q + 1)
                    for j in range(2):
                        for e in range(ET):
                            i = pe.matmul(bank(s)[:, 0, j * N:(j + 1) * N], wv[:, s, e, j, :], sel_src_t[:, e, :],
                                          start=(e == 0), stop=(e == ET - 1))
                    i.then_inc(y1_done, 1)
                for s in range(2):
                    q = 2 * p + s
                    pe.wait_ge(y1_out, q + 1)
                    if not first:
                        pe.wait_ge(ln1[0], q - 1)
                    for t in range(T):
                        for j in range(2):
                            k = 2 * t + j
                            c = j * N + t * P
                            i = pe.matmul(bank(2 + s)[:, 0, k * D:(k + 1) * D], y1t[:, s, c:c + P], wot[:], start=True, stop=True)
                    i.then_inc(o1_done, 1)

            layer1b(0, True)
            with pe.Fori(1, IT) as p:
                layer1b(p, False)

            pe.wait_ge(wgt_ready, 1)

            def layer2(p, first, last):
                for s in range(2):
                    q = 2 * p + s
                    pe.wait_ge(xs_lo, q + 1)
                    if not first:
                        pe.wait_ge(h2_out, GB * (2 * p - 1) + s + 1)
                    for j in range(2):
                        for t in range(T):
                            i = three(pe, bank(4 + s)[:, 0, j * N:(j + 1) * N], [h[:, s, t, j, :] for h in xs],
                                      [h[:, t, :] for h in wgt], t == 0, t == T - 1)
                    i.then_inc(pt_done, 1)
                for s in range(2):
                    q = 2 * p + s
                    pe.wait_ge(pt_lo, q + 1)
                    if not first:
                        if s == 0:
                            pe.wait_ge(s3_lo, 2 * p)
                        else:
                            pe.wait_ge(ln2[0], 2 * p)
                    for j in range(2):
                        for t in range(T):
                            c = j * N + t * P
                            i = three(pe, bank(2 * s + j)[:, 0, t * H2A:(t + 1) * H2A], [h[:, s, c:c + P] for h in pt],
                                      [h[:] for h in l2w1_s], True, True)
                    i.then_inc(h1_done, 1)
                for s in range(2):
                    q = 2 * p + s
                    pe.wait_ge(h1_lo, q + 1)
                    for f in range(GA):
                        for j in range(2):
                            for t in range(T):
                                i = three(pe, bank(2 * s + f)[:, 0, j * N:(j + 1) * N],
                                          [h[:, s, j, t, f * P:(f + 1) * P] for h in h1], [h[:, t, :] for h in wgt],
                                          t == 0, t == T - 1)
                    i.then_inc(qt_done, 1)
                for s in range(2):
                    q = 2 * p + s
                    pe.wait_ge(qt_lo, q + 1)
                    for g in range(GB):
                        if s == 0:
                            if not first:
                                pe.wait_ge(h2_out, GB * (q - 1) + g + 1)
                        else:
                            pe.wait_ge(h2_out, GB * (q - 1) + g + 1)
                        for f in range(GA):
                            i = three(pe, bank(4 + g)[:, 0, :], [h[:, f, g * P:(g + 1) * P] for h in l2w2_s],
                                      [h[:, s, f, :] for h in qt], f == 0, f == GA - 1)
                        i.then_inc(h2_done, 1)
                for s in range(2):
                    q = 2 * p + s
                    pe.wait_ge(h2_out, GB * (q + 1))
                    for t in range(T):
                        for j in range(2):
                            k = 2 * t + j
                            for g in range(GB):
                                i = pe.matmul(bank(s)[:, 0, k * D:(k + 1) * D], h2[:, s, g, j * N + t * P:j * N + (t + 1) * P],
                                              l2w3_s[:, g, :], start=(g == 0), stop=(g == GB - 1))
                    i.then_inc(s3_done, 1)
                if last:
                    turn3(0, True)
                for s in range(2):
                    q = 2 * p + s
                    if last and s == 1:
                        scores3(0)
                    pe.wait_ge(s3_lo, q + 1)
                    for n in range(T):
                        for t in range(T):
                            i = three(pe, bank(2 + s)[:, 0, n * 2 * D:(n + 1) * 2 * D], [h[:, t, n * P:(n + 1) * P] for h in wgt],
                                      [h[:, s, t, :, :] for h in s3], t == 0, t == T - 1)
                    i.then_inc(o2_done, 1)

            def turn3(p, first):
                for s in range(2):
                    q = 2 * p + s
                    pe.wait_ge(x3t_ready, q + 1)
                    if not first:
                        pe.wait_ge(tm_done, q - 1)
                    for j in range(2):
                        for t in range(T):
                            k = 2 * j + t
                            i = pe.transpose(bank(4 + s)[:, 0, k * P:(k + 1) * P], x3t[:, s, t, j, :], ident[:])
                    i.then_inc(t3_done, 1)

            def scores3(p):
                for s in range(2):
                    q = 2 * p + s
                    pe.wait_ge(xt3_out, q + 1)
                    for t in range(T):
                        for j in range(2):
                            k = 2 * t + j
                            pe.matmul(bank(6 + s)[:, 0, k:k + 1], xt3[:, s, j * N + t * P:j * N + (t + 1) * P], wa[:, 0:1],
                                      start=True, stop=True)
                    pe.matmul(bank(4 + s)[:, 0, :], wa2_bc[:], xt3[:, s, :], start=True, stop=True).then_inc(s2_done, 1)

            def turn_exps(p, first):
                for s in range(2):
                    q = 2 * p + s
                    pe.wait_ge(ex_ready, q + 1)
                    if not first:
                        pe.wait_ge(ax_out, q - 1)
                        pe.wait_ge(ln3[0], q - 1)
                    for j in range(2):
                        for c in range(T):
                            for t in range(T):
                                i = pe.transpose(bank(2 * s + j)[:, 0, c * N + t * P:c * N + (t + 1) * P],
                                                 ex[:, s, 2 * t + j, c * P:(c + 1) * P], ident[:])
                    i.then_inc(exr_done, 1)

            def attend(p):
                for s in range(2):
                    q = 2 * p + s
                    pe.wait_ge(ext_out, q + 1)
                    pe.wait_ge(x3r_ready, q + 1)
                    for j in range(2):
                        for c in range(T):
                            i = pe.matmul(bank(2 * s)[:, 0, j * N:(j + 1) * N], x3r[:, s, c, j, :], ext[:, s, j, c, :],
                                          start=(c == 0), stop=(c == T - 1))
                    i.then_inc(ax_done, 1)

            def output3(p):
                for s in range(2):
                    q = 2 * p + s
                    pe.wait_ge(ax_out, q + 1)
                    for t in range(T):
                        for j in range(2):
                            k = 2 * t + j
                            i = pe.matmul(bank(2 * s + 1)[:, 0, k * D:(k + 1) * D], axt[:, s, j * N + t * P:j * N + (t + 1) * P],
                                          l3w_s[:], start=True, stop=True)
                    i.then_inc(o3_done, 1)

            def step3(p, first, last):
                turn_exps(p, first)
                if not last:
                    turn3(p + 2, False)
                attend(p)
                if not last:
                    scores3(p + 2)
                output3(p)

            layer2(0, True, False)
            with pe.Fori(1, IT - 1) as p:
                layer2(p, False, False)
            pe.wait_ge(wa2_ready, 1)
            layer2(IT - 1, False, True)
            turn3(1, False)
            scores3(1)
            pe.wait_ge(ln2[0], Q)
            step3(0, True, False)
            with pe.Fori(1, IT - 2) as p:
                step3(p, False, False)
            step3(IT - 2, False, True)
            step3(IT - 1, False, True)


def kernel(**inputs):
    import numpy as np
    import concourse.bacc as bacc
    from concourse.bass_utils import run_bass_kernel_spmd

    a = {k: np.ascontiguousarray(v) for k, v in inputs.items()}
    arrays = {
        "x": a["x"], "adj": a["adj"], "adj_t": np.ascontiguousarray(a["adj"].T),
        "w1_t": np.ascontiguousarray(a["L0_gnn_W1"].T),
        "w2_t": np.ascontiguousarray(a["L0_gnn_W2"].T),
        "bn_cols": np.ascontiguousarray(np.concatenate(
            [a["L0_gnn_" + k].reshape(-1, P) for k in ("b1", "g1", "be1", "b2", "g2", "be2")]).T),
        "wv_t": np.ascontiguousarray(a["L1_gnn_W_val"].T), "wq_t": np.ascontiguousarray(a["L1_gnn_W_lin"].T),
        "a_head": a["L1_gnn_a"].reshape(D, 1), "wo_t": np.ascontiguousarray(a["L1_gnn_W_out"].T),
        "src": a["L1_gnn_src"], "dst": a["L1_gnn_dst"],
        "edge_cols": np.ascontiguousarray(np.concatenate([a[k].reshape(ET, P) for k in ("L1_gnn_src", "L1_gnn_dst")]).T),
        "l2w1": a["L2_gnn_W1"], "l2w2": a["L2_gnn_W2"], "l2w3": a["L2_gnn_W3"],
        "l3w": a["L3_gnn_W"], "l3a": np.ascontiguousarray(a["L3_gnn_a"].reshape(2, D).T), "l3w_t": np.ascontiguousarray(a["L3_gnn_W"].T),
    }
    nc = bacc.Bacc("TRN2", target_bir_lowering=False, num_devices=1)
    aps = {k: nc.dram_tensor("in_" + k, v.shape, mybir.dt.from_np(v.dtype), kind="ExternalInput").ap() for k, v in arrays.items()}
    out = nc.dram_tensor("out_x", (B, N, D), F32, kind="ExternalOutput").ap()
    build(nc, *aps.values(), out)
    r = run_bass_kernel_spmd(nc, [{"in_" + k: v for k, v in arrays.items()}], core_ids=[0])
    return r.results[0]["out_x"]
```

```python
from contextlib import ExitStack

import concourse.bass as bass
from concourse import mybir

F32 = mybir.dt.float32
F32R = mybir.dt.float32r
I32 = mybir.dt.int32
ALU = mybir.AluOpType
ACT = mybir.ActivationFunctionType
AX_X = mybir.AxisListType.X

P = 128
B, N, D = 32, 256, 128
T = N // P
E = 256
ET = E // P
HEADS = 4
DH = D // HEADS
H0 = 256
H2A, H2B = 256, 512
GA, GB = H2A // P, H2B // P
Q = B // 2
IT = Q // 2
W = 2 * N
BN_EPS = 1e-5
LN_EPS = 1e-5
LOG_EPS = 1e-8
SLOPE = 0.2
BIG = 1e30


def build(nc, x, adj, adj_t, w1_t, w2_t, bn_cols, wv_t, wq_t, a_head, wo_t, src,
          dst, edge_cols, l2w1, l2w2, l2w3, l3w, l3a, l3w_t, out):
    ctx = ExitStack()
    with ctx:
        def sb(name, shape, dt=F32, scope=ctx):
            return scope.enter_context(nc.sbuf_tensor(name, shape, dt))

        def sem(name):
            return ctx.enter_context(nc.semaphore(name))

        def hilo(name, shape, scope=ctx):
            return sb(name + "_hi", shape, F32R, scope), sb(name + "_lo", shape, F32R, scope)

        psum = ctx.enter_context(nc.psum_tensor("psum", [P, 8, 512], F32))

        def bank(k, n=1):
            return psum[:, k:k + n, :]

        def vq_bank(s):
            return bank(2 + 2 * s, 2).rearrange("p t (j c) -> p t j c", j=2)

        def in_turn(*makers):
            made = []
            for k, make in enumerate(makers):
                scope = ctx if k == len(makers) - 1 else ExitStack()
                made.append(make(scope))
                if scope is not ctx:
                    scope.close()
            return made

        ident = sb("ident", [P, P])
        ones = sb("ones", [P, P])
        iota_row = sb("iota_row", [P, N])
        iota_col = sb("iota_col", [P, T])
        adjs, wv_lo = in_turn(lambda c: sb("adjs", [P, 2, T, N], scope=c), lambda c: sb("wv_lo", [P, 2, ET, 2, D], F32R, c))
        adj_sb, adjt_sb = adjs[:, 0], adjs[:, 1]
        a_hat, wv_hi = in_turn(lambda c: hilo("a_hat", [P, T, N], c), lambda c: sb("wv_hi", [P, 2, ET, 2, D], F32R, c))
        wgt = hilo("wgt", [P, T, N])
        mask = sb("mask", [P, T, N])
        w1_raw, attn_t = in_turn(lambda c: sb("w1_raw", [P, H0], scope=c), lambda c: sb("attn_t", [P, ET, P], scope=c))
        x3_hi, (w1t, w2t, wvq) = in_turn(
            lambda c: sb("x3_hi", [P, 2, T, 2, D], F32R, c),
            lambda c: (hilo("w1t", [P, H0], c), sb("w2t", [P, H0 // P, D], scope=c), hilo("wvq", [P, 2 * D], c)))
        wot = sb("wot", [P, D])
        head_a = sb("head_a", [P, HEADS])
        l2w1_raw, esb = in_turn(lambda c: sb("l2w1_raw", [P, H2A], scope=c), lambda c: sb("esb", [P, 2, ET, P // 2], scope=c))
        l2w1_s = hilo("l2w1_s", [P, H2A])
        l2w2_raw, xt3 = in_turn(lambda c: sb("l2w2_raw", [P, GA, H2B], scope=c), lambda c: sb("xt3", [P, 2, W], scope=c))
        l2w2_s = hilo("l2w2_s", [P, GA, H2B])
        l2w3_s = sb("l2w3_s", [P, GB, D])
        l3w_s = sb("l3w_s", [P, D])
        l3wt_s = sb("l3wt_s", [P, D])
        l3a_s = sb("l3a_s", [P, 2])
        wa = sb("wa", [P, 2])
        wa2_bc = sb("wa2_bc", [P, P])
        bnp = sb("bnp", [P, 9])
        ext_lo, (sel_sum, sel_dst, reset, same) = in_turn(
            lambda c: sb("ext_lo", [P, 2, 2, 2, N], F32R, c),
            lambda c: (sb("sel_sum", [P, T, E], F32R, c), sb("sel_dst", [P, T, E], F32R, c),
                       sb("reset", [P, 2, E], scope=c), sb("same", [P, 2, E], scope=c)))
        sel_src_t = sb("sel_src_t", [P, ET, N], F32R)
        wvq_raw, log_a = in_turn(lambda c: sb("wvq_raw", [P, 2, D], scope=c), lambda c: sb("log_a", [P, E], scope=c))
        x0, keep_x = in_turn(lambda c: hilo("x0", [P, 2, T, 2, D], c), lambda c: sb("keep_x", [P, Q, W], scope=c))
        xn = keep_x[:].rearrange("p q (t j d) -> p q t j d", t=T, j=2)
        oraw = keep_x
        s_adj, s_small, s_edge, s_wts = sem("in_adj"), sem("in_small"), sem("in_edge"), sem("in_weights")
        pz = sem("constants")
        dc, pc = sem("setup_chain_vector"), sem("setup_chain_pool")
        deg_ready, deg_done, deg_root, a_hat_ready = sem("deg_ready"), sem("deg_done"), sem("deg_root"), sem("a_hat_ready")
        keys_compared, ranks_ready = sem("keys_compared"), sem("ranks_ready")
        edges_ranked, edges_sorted, sorted_out = sem("edges_ranked"), sem("edges_sorted"), sem("sorted_out")
        sel_ready, adj_dst_done, adj_dst_out = sem("sel_ready"), sem("adj_dst_done"), sem("adj_dst_out")
        picked, a_edge_done, log_ready = sem("picked"), sem("a_edge_done"), sem("log_ready")
        weights_split, wgt_ready, wa2_ready = sem("weights_split"), sem("wgt_ready"), sem("wa2_ready")

        bst1 = sb("bst1", [P, H0 // P, Q, 6])
        bst2 = sb("bst2", [P, Q, 6])
        bagg = sb("bagg", [P, 3, 2])
        bco = sb("bco", [P, 4, 3])
        ob, xin = in_turn(lambda c: sb("ob", [P, 2, T, 2, D], scope=c), lambda c: sb("xin", [P, 2, T, 2, D], scope=c))
        x_in = [sem("x_in0"), sem("x_in1")]
        agg_done, agg_hi, agg_lo = sem("agg_done"), sem("agg_hi"), sem("agg_lo")
        x0_hi, x0_lo = sem("x0_hi"), sem("x0_lo")
        h_done, h_out = sem("h_done"), sem("h_out")
        h_stat, bn1_ready = sem("h_stat"), sem("bn1_ready")
        relu_ready, o_done, o_out = sem("relu_ready"), sem("o_done"), sem("o_out")
        o_stat, bn2_ready = sem("o_stat"), sem("bn2_ready")
        bn_chain, bn_var, bn_root = sem("bn_chain"), sem("bn_var"), sem("bn_root")

        def wait_apart(eng, own, signal, value):
            if not isinstance(value, int):
                value = eng.snap(value)
            eng.wait_ge(own, 1)
            eng.wait_ge(signal, value)

        eps = sb("eps", [P, 1])
        log_eps = sb("log_eps", [P, 1])
        mhalf = sb("mhalf", [P, 8])

        class LayerNorm:
            def __init__(self, tag):
                names = ("added", "stats", "mean", "var", "rstd", "done")
                self.added, self.stats, self.mean, self.var, self.rstd, self.done = (sem(f"ln{tag}_{k}") for k in names)
                self.st = sb(f"ln{tag}_st", [P, 2, 4, 6])
                self.ag = sb(f"ln{tag}_ag", [P, 2, 4, 2])
                self.v = sb(f"ln{tag}_v", [P, 2, 4])
                self.r = sb(f"ln{tag}_r", [P, 2, 4])

        ln0, ln1, ln2, ln3 = (LayerNorm(k) for k in range(4))

        def ln_stats(dve, y, p, ln):
            wait_apart(dve, dc, ln.added, 2 * p + 2)
            for s in range(2):
                for k in range(4):
                    i = dve.bn_stats(ln.st[:, s, k, :], y(s, k // 2, k % 2))
            i.then_inc(ln.stats, 2)
            wait_apart(dve, dc, ln.stats, 2 * p + 2)
            for s in range(2):
                for k in range(4):
                    i = dve.bn_aggr(ln.ag[:, s, k, :], ln.st[:, s, k, :])
            i.then_inc(ln.mean, 1)

        def ln_var_eps(dve, p, ln):
            dve.wait_ge(ln.mean, p + 1)
            dve.tensor_scalar(ln.v[:].rearrange("p s k -> p (s k)"), ln.ag[:].rearrange("p s k c -> p (s k) c")[:, :, 1],
                              LN_EPS, None, ALU.add).then_inc(ln.var, 1)

        def ln_power(pool, p, ln):
            pool.wait_ge(ln.var, p + 1)
            pool.tensor_tensor(ln.r[:].rearrange("p s k -> p (s k)"), ln.v[:].rearrange("p s k -> p (s k)"), mhalf[:],
                               ALU.pow).then_inc(ln.rstd, 1)

        def ln_root(act, p, ln):
            act.wait_ge(ln.mean, p + 1)
            act.activation(ln.v[:].rearrange("p s k -> p (s k)"), ln.ag[:].rearrange("p s k c -> p (s k) c")[:, :, 1],
                           ACT.Sqrt, bias=eps[:]).then_inc(ln.var, 1)

        def ln_rstd(dve, p, ln):
            dve.wait_ge(ln.var, p + 1)
            dve.reciprocal(ln.r[:], ln.v[:]).then_inc(ln.rstd, 1)

        def ln_apply(dve, y, dst_of, p, s, ln):
            dve.wait_ge(ln.rstd, p + 1)
            for k in range(4):
                i = dve.tensor_scalar(dst_of(k // 2, k % 2), y(s, k // 2, k % 2), ln.ag[:, s, k, 0:1],
                                      ln.r[:, s, k:k + 1], ALU.subtract, ALU.mult)
            i.then_inc(ln.done, 1)

        def three(pe, o, lhs, rhs, start, stop):
            pe.matmul(o, lhs[0], rhs[0], start=start, stop=False)
            pe.matmul(o, lhs[0], rhs[1], start=False, stop=False)
            return pe.matmul(o, lhs[1], rhs[0], start=False, stop=stop)

        bnt_ready, t1_done, x1_kept = sem("bnt_ready"), sem("t1_done"), sem("x1_kept")
        t2_done, xt_hi, xt_lo = sem("t2_done"), sem("xt_hi"), sem("xt_lo")
        vq_done, vq_hi_ok, vq_lo_ok = sem("vq_done"), sem("vq_hi"), sem("vq_lo")
        g_done, z_ready, l_ready, e_done = sem("g_done"), sem("z_ready"), sem("l_ready"), sem("e_done")
        ve_done, ve_out = sem("ve_done"), sem("ve_out")
        x_in2 = [sem("x_again0"), sem("x_again1")]
        sm = sem("softmax_chain")
        sm_exp, sm_t1, sm_t2 = sem("softmax_exp"), sem("scores_turned"), sem("attn_turned")
        wv_ready, wv_hi_ok, wv_lo_ok = sem("wv_ready"), sem("wv_hi_ok"), sem("wv_lo_ok")
        y1_done, y1_out, o1_done = sem("y1_done"), sem("y1_out"), sem("o1_done")
        xs_hi, xs_lo = sem("xs_hi"), sem("xs_lo")
        pt_done, pt_hi, pt_lo = sem("pt_done"), sem("pt_hi"), sem("pt_lo")
        h1_done, h1_hi, h1_lo = sem("h1_done"), sem("h1_hi"), sem("h1_lo")
        qt_done, qt_hi, qt_lo = sem("qt_done"), sem("qt_hi"), sem("qt_lo")
        h2_done, h2_out = sem("h2_done"), sem("h2_out")
        s3_done, s3_hi, s3_lo = sem("s3_done"), sem("s3_hi"), sem("s3_lo")
        o2_done = sem("o2_done")
        x3_ready, t3_done, xt3_out = sem("x3_ready"), sem("t3_done"), sem("xt3_out")
        s2_done, s1_out, tm_done, m_step = sem("s2_done"), sem("s1_out"), sem("tm_done"), sem("m_step")
        zt_ready, lk_ready, ex_ready = sem("zt_ready"), sem("lk_ready"), sem("ex_ready")
        exr_done, ext_hi_ok, ext_lo_ok = sem("ex_turned"), sem("ext_hi_ok"), sem("ext_lo_ok")
        x3_hi_ok, x3_lo_ok = sem("x3_hi_ok"), sem("x3_lo_ok")
        ax_done, ax_out, o3_done, r_step = sem("ax_done"), sem("ax_out"), sem("o3_done"), sem("r_step")
        stored = [sem("stored0"), sem("stored1")]

        x_nat = x.rearrange("b (t n) d -> n t b d", n=P)
        out_nat = out.rearrange("b (t n) d -> n t b d", n=P)

        aggt, xt, pt, s3 = in_turn(lambda c: hilo("aggt", [P, 2, W], c), lambda c: hilo("xt", [P, 2, W], c),
                                   lambda c: hilo("pt", [P, 2, W], c), lambda c: hilo("s3", [P, 2, T, 2, D], c))
        x3_lo, l1 = in_turn(lambda c: sb("x3_lo", [P, 2, T, 2, D], F32R, c), lambda c: sb("l1", [P, 2, W], scope=c))

        setup1 = ExitStack()
        edge_i = sb("edge_i", [P, 2, E], I32, scope=setup1)
        edge_f = sb("edge_f", [P, 2, E], scope=setup1)
        key_row = sb("key_row", [P, E], scope=setup1)
        less = sb("less", [P, ET, E], scope=setup1)
        ecol_bc = sb("ecol_bc", [P, 2, ET, P], scope=setup1)
        degm = sb("degm", [P, T, N], scope=setup1)
        dinv_bc = sb("dinv_bc", [P, N], scope=setup1)
        root_bc = sb("root_bc", [P, N], scope=setup1)
        at1 = sb("at1", [P, T, N], scope=setup1)
        setup1.close()
        late1 = ExitStack()
        y1t = sb("y1t", [P, 2, W], scope=late1)
        ext_hi = sb("ext_hi", [P, 2, 2, 2, N], F32R, late1)
        axt = sb("axt", [P, 2, W], scope=late1)
        late1.close()
        bnt = sb("bnt", [P, 2, W])
        y0 = sb("y0", [P, 2, T, 2, D])
        x1r = sb("x1r", [P, 2, T, 2, D])
        z1 = sb("z1", [P, 2, W])
        setup2 = ExitStack()
        perm = sb("perm", [P, ET, E], scope=setup2)
        sorted_bc = sb("sorted_bc", [P, 2, E], scope=setup2)
        ssrc = sb("ssrc", [P, T, E], scope=setup2)
        sdst = sb("sdst", [P, T, E], scope=setup2)
        prod = sb("prod", [P, T, E], scope=setup2)
        diff = sb("diff", [P, 2, E], scope=setup2)
        sq = sb("sq", [P, T, N], scope=setup2)
        adj_dst = sb("adj_dst", [P, T, E], scope=setup2)
        setup2.close()
        xs = hilo("xs", [P, 2, T, 2, D])
        wv = sb("wv", [P, 2, ET, 2, D])
        sc, x3 = in_turn(lambda c: sb("sc", [P, 4, E], scope=c), lambda c: sb("x3", [P, 2, T, 2, D], scope=c))
        ecol_i = sb("ecol_i", [P, 2, ET], I32)
        ecol_f = sb("ecol_f", [P, 2, ET])
        key_col = sb("key_col", [P, ET])
        rank = sb("rank", [P, ET])
        sorted_col = sb("sorted_col", [P, ET])
        dinv = sb("dinv", [P, T])
        root = sb("root", [P, T])
        soft = sb("soft", [P, 2, 4, N])
        m3 = sb("m3", [P, 2, 4])
        s1c = sb("s1c", [P, 2, 4])
        zm = sb("zm", [P, 3, 2, 4])
        rs = sb("rs", [P, 2, 4])
        ri = sb("ri", [P, 2, 4])
        scope0 = ExitStack()
        hraw = sb("hraw", [P, H0 // P, Q, W], scope=scope0)
        scope0.close()
        vall = sb("vall", [P, ET, B, D])
        scope3 = ExitStack()
        vq = hilo("vq", [P, 2, T, 2, 2 * D], scope3)
        scope3.close()
        qt = hilo("qt", [P, 2, GA, W])
        h1, h2 = in_turn(lambda c: hilo("h1", [P, 2, 2, T, H2A], c), lambda c: sb("h2", [P, 2, GB, W], scope=c))

        SMALL = 4
        HALF = P // 2
        SM_STEPS, SM_EXP, SM_RESULT = 10, 5, 9
        block = ctx.enter_context(nc.Block())

        @block.sync
        def _(sp):
            sp.dma_start(adj_sb, adj.rearrange("(t p) m -> p t m", p=P)).then_inc(s_adj, 16)
            sp.dma_start(adjt_sb, adj_t.rearrange("(t p) m -> p t m", p=P)).then_inc(s_adj, 16)

            def load_x(s, q, to):
                sp.dma_start(xin[:, s, 0, :, :], x_nat[:, 0, bass.ds(2 * q, 2), :]).then_inc(to[s], 16)
                sp.dma_start(xin[:, s, 1, :, :], x_nat[:, 1, bass.ds(2 * q, 2), :]).then_inc(to[s], 16)

            load_x(0, 0, x_in)
            load_x(1, 1, x_in)
            sp.dma_start(w1_raw[:], w1_t).then_inc(s_small, 16)
            sp.dma_start(w2t[:], w2_t.rearrange("(k p) o -> p k o", p=P)).then_inc(s_small, 16)
            sp.dma_start(bnp[:], bn_cols).then_inc(s_small, 16)
            sp.dma_start(l3a_s[:], l3a).then_inc(s_small, 16)
            for k, v in enumerate((src, dst)):
                sp.dma_start(edge_i[:, k, :], v.partition_broadcast(P)).then_inc(s_edge, 16)
            sp.dma_start(ecol_i[:].rearrange("p a t -> p (a t)"), edge_cols).then_inc(s_edge, 16)
            with sp.Fori(1, IT) as p:
                for s in range(2):
                    sp.wait_ge(x0_lo, 2 * p + s - 1)
                    load_x(s, 2 * p + s, x_in)
            sp.wait_ge(x0_lo, Q)
            load_x(0, 0, x_in2)
            load_x(1, 1, x_in2)
            with sp.Fori(1, IT) as p:
                for s in range(2):
                    sp.wait_ge(ln0.added, 2 * p + s - 1)
                    load_x(s, 2 * p + s, x_in2)
            with sp.Fori(0, IT) as p:
                for s in range(2):
                    sp.wait_ge(ln3.done, 2 * p + s + 1)
                    for t in range(T):
                        sp.dma_start(out_nat[:, t, bass.ds(4 * p + 2 * s, 2), :], ob[:, s, t, :, :]).then_inc(stored[s], 16)
            for s in range(2):
                sp.wait_ge(stored[s], 32 * IT)

        @block.gpsimd
        def _(pool):
            steps = [0]

            def link(ins):
                steps[0] += 1
                ins.then_inc(pc, 1)
                pool.wait_ge(pc, steps[0])

            pool.memset(ident[:], 0.0).then_inc(pz, 1)
            pool.memset(ones[:], 1.0).then_inc(pz, 1)
            pool.memset(eps[:], LN_EPS).then_inc(pz, 1)
            pool.wait_ge(pz, 3)
            pool.affine_select(out=ident[:], in_=ident[:], compare_op=ALU.not_equal, fill=1.0, base=0,
                               pattern=[[-1, P]], channel_multiplier=1).then_inc(pz, 1)
            pool.memset(head_a[:], 0.0).then_inc(pz, 1)
            pool.iota(iota_row[:], pattern=[[1, N]], base=0, channel_multiplier=0,
                      allow_small_or_imprecise_dtypes=True).then_inc(pz, 1)
            pool.iota(iota_col[:], pattern=[[P, T]], base=0, channel_multiplier=1,
                      allow_small_or_imprecise_dtypes=True).then_inc(pz, 1)
            pool.memset(log_eps[:], LOG_EPS).then_inc(pz, 1)
            pool.memset(mhalf[:], -0.5).then_inc(pz, 1)
            pool.wait_ge(pz, 9)
            for h in range(HEADS):
                pool.dma_start(head_a[h * DH:(h + 1) * DH, h:h + 1],
                               a_head[h * DH:(h + 1) * DH, :]).then_inc(s_wts, 16)
            for to, frm in ((wvq_raw[:, 0, :], wv_t), (wvq_raw[:, 1, :], wq_t), (wot[:], wo_t),
                            (l2w1_raw[:], l2w1), (l2w2_raw[:], l2w2.rearrange("(k p) g -> p k g", p=P)),
                            (l2w3_s[:], l2w3.rearrange("(k p) g -> p k g", p=P)), (l3w_s[:], l3w), (l3wt_s[:], l3w_t)):
                pool.dma_start(to, frm).then_inc(s_wts, 16)

            pool.wait_ge(s_edge, 48)
            pool.tensor_copy(edge_f[:], edge_i[:])
            link(pool.tensor_copy(ecol_f[:], ecol_i[:]))
            pool.tensor_scalar(key_row[:], edge_f[:, 0, :], float(E), None, ALU.mult)
            link(pool.tensor_scalar(key_col[:], ecol_f[:, 0, :], float(E), None, ALU.mult))
            pool.tensor_tensor(key_row[:], key_row[:], iota_row[:, 0:E], ALU.add)
            link(pool.tensor_tensor(key_col[:], key_col[:], iota_col[:, 0:ET], ALU.add))
            for t in range(ET):
                i = pool.tensor_scalar(less[:, t, :], key_row[:], key_col[:, t:t + 1], None, ALU.is_lt)
            i.then_inc(keys_compared, 1)
            pool.wait_ge(ranks_ready, 1)
            for t in range(ET):
                i = pool.tensor_scalar(perm[:, t, :], iota_row[:, 0:E], rank[:, t:t + 1], None, ALU.is_equal)
            for k in range(2):
                for t in range(ET):
                    i = pool.tensor_scalar(ecol_bc[:, k, t, :], ones[:], ecol_f[:, k, t:t + 1], None, ALU.mult)
            i.then_inc(edges_ranked, 1)

            pool.wait_ge(s_wts, 16 * 12)
            pairs = ((wvq, wvq_raw[:].rearrange("p a b -> p (a b)")), (l2w1_s, l2w1_raw[:]), (l2w2_s, l2w2_raw[:]))
            for hl, raw in pairs:
                i = pool.tensor_copy(hl[0][:], raw)
            link(i)
            for hl, raw in pairs:
                i = pool.tensor_tensor(hl[1][:], raw, hl[0][:], ALU.subtract)
            i.then_inc(weights_split, 1)
            pool.wait_ge(s_adj, 32)
            link(pool.tensor_tensor(sq[:], adjt_sb, adjt_sb, ALU.mult))
            link(pool.tensor_copy(wgt[0][:], sq[:]))
            pool.tensor_scalar(mask[:], adj_sb, 0.0, -BIG, ALU.is_equal, ALU.mult)
            pool.tensor_tensor(wgt[1][:], sq[:], wgt[0][:], ALU.subtract).then_inc(wgt_ready, 1)

            pool.wait_ge(sorted_out, 1)
            for t in range(T):
                pool.tensor_scalar(ssrc[:, t, :], sorted_bc[:, 0, :], iota_col[:, t:t + 1], None, ALU.is_equal)
                pool.tensor_scalar(sdst[:, t, :], sorted_bc[:, 1, :], iota_col[:, t:t + 1], None, ALU.is_equal)
            for t in range(ET):
                pool.tensor_scalar(sel_src_t[:, t, :], iota_row[:], sorted_col[:, t:t + 1], None, ALU.is_equal)
            link(pool.memset(diff[:], 1.0))
            pool.tensor_tensor(sel_sum[:], ssrc[:], sdst[:], ALU.add)
            pool.tensor_copy(sel_dst[:], sdst[:]).then_inc(sel_ready, 1)
            pool.tensor_tensor(diff[:, 0, 1:E], sorted_bc[:, 0, 1:E], sorted_bc[:, 0, 0:E - 1], ALU.subtract)
            link(pool.tensor_tensor(diff[:, 1, 0:E - 1], sorted_bc[:, 0, 1:E], sorted_bc[:, 0, 0:E - 1], ALU.subtract))
            link(pool.tensor_scalar(same[:], diff[:], 0.0, None, ALU.is_equal))
            pool.tensor_scalar(reset[:], same[:], 1.0, BIG, ALU.subtract, ALU.mult)
            pool.tensor_scalar(wa2_bc[:], ones[:], wa[:, 1:2], None, ALU.mult).then_inc(wa2_ready, 1)
            pool.wait_ge(adj_dst_out, 1)
            pool.tensor_tensor(prod[:], adj_dst[:], ssrc[:], ALU.mult).then_inc(picked, 1)

            def keep_x1(p):
                for s in range(2):
                    pool.wait_ge(ln0.done, 2 * p + s + 1)
                    pool.tensor_copy(xn[:, 2 * p + s], x1r[:, s]).then_inc(x1_kept, 1)

            with pool.Fori(0, IT - 1) as p:
                keep_x1(p)

            def weigh(s, q, first):
                if not first:
                    pool.wait_ge(wv_lo_ok, q - 1)
                v = vall[:, :, bass.ds(2 * q, 2), :].rearrange("p t j (h c) -> p t (j h) c", c=DH)
                w = wv[:, s].rearrange("p t j (h c) -> p t (j h) c", c=DH)
                for t in range(ET):
                    a = attn_t[:, t, bass.ds(2 * HEADS * q, 2 * HEADS)].unsqueeze(2).broadcast_to([P, 2 * HEADS, DH])
                    i = pool.tensor_tensor(w[:, t], v[:, t], a, ALU.mult)
                i.then_inc(wv_ready, 1)

            def split_x(p, s, first):
                q = 2 * p + s
                pool.wait_ge(ln1.done, q + 1)
                if not first:
                    pool.wait_ge(pt_done, q - 1)
                pool.tensor_copy(xs[0][:, s], xn[:, q]).then_inc(xs_hi, 1)
                wait_apart(pool, pz, xs_hi, q + 1)
                pool.tensor_tensor(xs[1][:, s], xn[:, q], xs[0][:, s], ALU.subtract).then_inc(xs_lo, 1)

            def take_x3(p, first):
                for s in range(2):
                    q = 2 * p + s
                    pool.wait_ge(ln2.done, q + 1)
                    if not first:
                        pool.wait_ge(t3_done, q - 1)
                    pool.tensor_copy(x3[:, s], xn[:, q]).then_inc(x3_ready, 1)

            def split_x3(p, first):
                for s in range(2):
                    q = 2 * p + s
                    if not first:
                        wait_apart(pool, pz, ax_done, q - 1)
                    pool.tensor_copy(x3_hi[:, s], xn[:, q]).then_inc(x3_hi_ok, 1)
                    wait_apart(pool, pz, x3_hi_ok, q + 1)
                    pool.tensor_tensor(x3_lo[:, s], xn[:, q], x3_hi[:, s], ALU.subtract).then_inc(x3_lo_ok, 1)

            def step(p, two_ahead=True, ahead=True, behind=True, two_behind=True):
                if two_ahead:
                    for s in range(2):
                        weigh(s, 2 * (p + 2) + s, False)
                if behind:
                    ln_power(pool, p - 1, ln2)
                if ahead:
                    ln_power(pool, p + 1, ln1)
                if behind:
                    take_x3(p - 1, not two_behind)
                if ahead:
                    split_x(p + 1, 0, False)
                if two_behind:
                    ln_power(pool, p - 2, ln3)
                if ahead:
                    split_x(p + 1, 1, False)
                if behind:
                    split_x3(p - 1, not two_behind)

            pool.wait_ge(ve_out, Q // 2)
            pool.wait_ge(sm, SM_STEPS)
            for s in range(2):
                weigh(s, s, True)
            keep_x1(IT - 1)
            for s in range(2):
                weigh(s, 2 + s, False)
            ln_power(pool, 0, ln1)
            for s in range(2):
                split_x(0, s, True)
            step(0, behind=False, two_behind=False)
            step(1, two_behind=False)
            pool.wait_ge(ve_out, Q)
            pool.wait_ge(sm, 2 * SM_STEPS)
            with pool.Fori(2, IT - 2) as p:
                step(p)
            step(IT - 2, two_ahead=False)
            step(IT - 1, two_ahead=False, ahead=False)
            ln_power(pool, IT - 1, ln2)
            take_x3(IT - 1, False)
            split_x3(IT - 1, False)
            ln_power(pool, IT - 2, ln3)
            ln_power(pool, IT - 1, ln3)

        @block.vector
        def _(dve):
            steps = [0]

            def link(ins):
                steps[0] += 1
                ins.then_inc(dc, 1)
                dve.wait_ge(dc, steps[0])

            dve.wait_ge(pz, 4)
            dve.wait_ge(s_adj, 32)
            dve.tensor_tensor(degm[:], adj_sb, adjt_sb, ALU.add)
            for t in range(T):
                blk = slice(t * P, (t + 1) * P)
                i = dve.tensor_tensor(prod[:, t, blk], adj_sb[:, t, blk], ident[:], ALU.mult)
            link(i)
            for t in range(T):
                blk = slice(t * P, (t + 1) * P)
                i = dve.tensor_tensor(degm[:, t, blk], degm[:, t, blk], prod[:, t, blk], ALU.subtract)
            link(i)
            for t in range(T):
                blk = slice(t * P, (t + 1) * P)
                i = dve.tensor_tensor(degm[:, t, blk], degm[:, t, blk], ident[:], ALU.add)
            i.then_inc(deg_ready, 1)
            link(dve.tensor_copy(at1[:], adjt_sb))
            for t in range(T):
                blk = slice(t * P, (t + 1) * P)
                i = dve.tensor_tensor(at1[:, t, blk], at1[:, t, blk], ident[:], ALU.add)
            link(i)
            dve.wait_ge(s_small, 16 * SMALL)
            link(dve.tensor_copy(w1t[0][:], w1_raw[:]))
            dve.tensor_tensor(w1t[1][:], w1_raw[:], w1t[0][:], ALU.subtract)
            dve.wait_ge(deg_root, 1)
            dve.reciprocal(dinv_bc[:], root_bc[:])
            link(dve.reciprocal(dinv[:], root[:]))
            for t in range(T):
                i = dve.scalar_tensor_tensor(out=at1[:, t, :], in0=at1[:, t, :], scalar=dinv[:, t:t + 1],
                                             in1=dinv_bc[:], op0=ALU.mult, op1=ALU.mult)
            link(i)
            link(dve.tensor_copy(a_hat[0][:], at1[:]))
            dve.tensor_tensor(a_hat[1][:], at1[:], a_hat[0][:], ALU.subtract).then_inc(a_hat_ready, 1)
            def x0_low(p):
                for s in range(2):
                    dve.wait_ge(x0_hi, 2 * p + s + 1)
                    dve.tensor_tensor(x0[1][:, s], xin[:, s], x0[0][:, s], ALU.subtract).then_inc(x0_lo, 1)

            def agg_low(p):
                for s in range(2):
                    dve.wait_ge(agg_hi, 2 * p + s + 1)
                    dve.tensor_tensor(aggt[1][:, s, :], bank(s)[:, 0, :], aggt[0][:, s, :], ALU.subtract).then_inc(agg_lo, 1)

            def h_stats(p):
                for s in range(2):
                    q = 2 * p + s
                    wait_apart(dve, dc, h_out, q + 1)
                    for k in range(H0 // P):
                        i = dve.bn_stats(bst1[:, k, q, :], hraw[:, k, q, :])
                    i.then_inc(h_stat, 1)

            x0_low(0)
            agg_low(0)
            dve.wait_ge(keys_compared, 1)
            dve.tensor_reduce(rank[:], less[:], AX_X, ALU.add).then_inc(ranks_ready, 1)
            x0_low(1)
            with dve.Fori(1, IT - 1) as p:
                agg_low(p)
                x0_low(p + 1)
                h_stats(p - 1)
            agg_low(IT - 1)
            h_stats(IT - 2)
            h_stats(IT - 1)
            dve.wait_ge(h_stat, Q)

            cs = [0]

            def bn_link(ins):
                cs[0] += 1
                ins.then_inc(bn_chain, 1)
                dve.wait_ge(bn_chain, cs[0])

            def coefficients(ks, stats, bias, gamma, beta, turn):
                mean, rstd, scale, shift = (bco[:, c, ks] for c in range(4))
                for n, k in enumerate(range(ks.start, ks.stop)):
                    i = dve.bn_aggr(bagg[:, k, :], stats[n])
                i.then_inc(bn_var, 1)
                dve.wait_ge(bn_var, turn)
                bn_link(dve.tensor_tensor(mean, bagg[:, ks, 0], bias, ALU.add))
                dve.wait_ge(bn_root, turn)
                bn_link(dve.reciprocal(rstd, rstd))
                dve.tensor_tensor(shift, bias, mean, ALU.subtract)
                bn_link(dve.tensor_tensor(scale, rstd, gamma, ALU.mult))
                bn_link(dve.tensor_tensor(shift, shift, scale, ALU.mult))
                return dve.tensor_tensor(shift, shift, beta, ALU.add)

            coefficients(slice(0, 2), [bst1[:, k].rearrange("p q c -> p (q c)") for k in range(2)],
                         bnp[:, 0:2], bnp[:, 2:4], bnp[:, 4:6], 1).then_inc(bn1_ready, 1)

            with dve.Fori(0, IT) as p:
                for s in range(2):
                    q = 2 * p + s
                    dve.wait_ge(o_done, q + 1)
                    dve.tensor_copy(oraw[:, q, :], bank(s)[:, 0, :]).then_inc(o_out, 1)
                    wait_apart(dve, dc, o_out, q + 1)
                    dve.bn_stats(bst2[:, q, :], oraw[:, q, :]).then_inc(o_stat, 1)
            dve.wait_ge(o_stat, Q)
            coefficients(slice(2, 3), [bst2[:].rearrange("p q c -> p (q c)")],
                         bnp[:, 6:7], bnp[:, 7:8], bnp[:, 8:9], 2).then_inc(bn2_ready, 1)

            def y0_of(s, t, j):
                return y0[:, s, t, j, :]

            def sum0(p):
                for s in range(2):
                    q = 2 * p + s
                    dve.wait_ge(t1_done, q + 1)
                    dve.wait_ge(x_in2[s], 32 * (p + 1))
                    dve.tensor_tensor(y0[:, s], bank(s)[:, 0, :].rearrange("p (t j d) -> p t j d", t=T, j=2),
                                      xin[:, s], ALU.add).then_inc(ln0.added, 1)
                ln_stats(dve, y0_of, p, ln0)

            def norm0(p, first):
                ln_rstd(dve, p, ln0)
                for s in range(2):
                    if not first:
                        dve.wait_ge(x1_kept, 2 * p + s - 1)
                        dve.wait_ge(t2_done, 2 * p + s - 1)
                    ln_apply(dve, y0_of, lambda t, j: x1r[:, s, t, j, :], p, s, ln0)

            def x1_low(p):
                for s in range(2):
                    q = 2 * p + s
                    dve.wait_ge(xt_hi, q + 1)
                    dve.tensor_tensor(xt[1][:, s, :], bank(s)[:, 0, :], xt[0][:, s, :], ALU.subtract).then_inc(xt_lo, 1)

            def vq_low(p):
                for s in range(2):
                    q = 2 * p + s
                    dve.wait_ge(vq_hi_ok, q + 1)
                    dve.tensor_tensor(vq[1][:, s], vq_bank(s), vq[0][:, s], ALU.subtract).then_inc(vq_lo_ok, 1)

            def leaky(p):
                for s in range(2):
                    q = 2 * p + s
                    dve.wait_ge(z_ready, q + 1)
                    dve.scalar_tensor_tensor(out=l1[:, s, :], in0=z1[:, s, :], scalar=SLOPE, in1=z1[:, s, :],
                                             op0=ALU.mult, op1=ALU.max).then_inc(l_ready, 1)

            dve.wait_ge(o_done, Q)
            sum0(0)
            norm0(0, True)
            x1_low(0)
            ss = [0]

            def sm_link(ins):
                ss[0] += 1
                ins.then_inc(sm, 1)
                dve.wait_ge(sm, ss[0])

            score, fwd, top, expo = (sc[0:HALF, k, :] for k in range(4))
            rev = slice(None, None, -1)

            def take_scores(half):
                dve.wait_ge(e_done, (half + 1) * Q // 2)
                sm_link(dve.tensor_copy(esb[:, half], bank(7)[:, 0, 0:2 * P].rearrange(
                    "p (t c) -> p t c", t=ET)[:, :, half * HALF:(half + 1) * HALF]))

            def maxima(half):
                dve.wait_ge(sm_t1, half + 1)
                dve.wait_ge(log_ready, 1)
                sm_link(dve.tensor_tensor(score, bank(6)[0:HALF, 0, 0:E], log_a[0:HALF], ALU.add))
                sm_link(dve.tensor_tensor_scan(fwd, reset[0:HALF, 0, :], score, -BIG, ALU.add, ALU.max))
                sm_link(dve.tensor_tensor_scan(top[:, rev], reset[0:HALF, 1, rev], fwd[:, rev], -BIG, ALU.add, ALU.max))
                sm_link(dve.tensor_tensor(score, score, top, ALU.subtract))

            def normalize(half):
                dve.wait_ge(sm_exp, half + 1)
                sm_link(dve.tensor_tensor_scan(fwd, same[0:HALF, 0, :], expo, 0.0, ALU.mult, ALU.add))
                sm_link(dve.tensor_tensor_scan(top[:, rev], reset[0:HALF, 1, rev], fwd[:, rev], -BIG, ALU.add, ALU.max))
                sm_link(dve.reciprocal(fwd, top))
                sm_link(dve.tensor_tensor(score, expo, fwd, ALU.mult))

            def take_attention(half):
                dve.wait_ge(sm_t2, half + 1)
                sm_link(dve.tensor_copy(attn_t[:, :, half * HALF:(half + 1) * HALF],
                                        bank(6)[:, 0, 0:ET * HALF].rearrange("p (t c) -> p t c", t=ET)))

            def body(p, between=None, after=None):
                sum0(p + 1)
                vq_low(p)
                if between:
                    between()
                norm0(p + 1, False)
                leaky(p)
                x1_low(p + 1)
                if after:
                    after()

            with dve.Fori(0, IT // 2) as p:
                body(p)
            body(IT // 2, lambda: take_scores(0), lambda: maxima(0))
            body(IT // 2 + 1, lambda: normalize(0), lambda: take_attention(0))

            def weighted_low(p, s):
                dve.wait_ge(wv_hi_ok, 2 * p + s + 1)
                dve.tensor_tensor(wv_lo[:, s], wv[:, s], wv_hi[:, s], ALU.subtract).then_inc(wv_lo_ok, 1)

            def both_low(p):
                for s in range(2):
                    weighted_low(p, s)

            body(IT // 2 + 2, lambda: both_low(0))
            vq_low(IT - 1)

            def row(p):
                return lambda s, t, j: xn[:, 2 * p + s, t, j, :]

            def add(p, s, done, psum_bank, ln):
                q = 2 * p + s
                dve.wait_ge(done, q + 1)
                dve.tensor_tensor(xn[:, q], bank(psum_bank)[:, 0, :].rearrange("p (t j d) -> p t j d", t=T, j=2), xn[:, q],
                                  ALU.add).then_inc(ln.added, 1)

            def variance(p, ln, first):
                if not first:
                    wait_apart(dve, dc, ln.done, 2 * p)
                ln_stats(dve, row(p), p, ln)
                ln_var_eps(dve, p, ln)

            def apply(p, ln):
                for s in range(2):
                    ln_apply(dve, row(p), lambda t, j: row(p)(s, t, j), p, s, ln)

            def pt_low(p, s):
                dve.wait_ge(pt_hi, 2 * p + s + 1)
                dve.tensor_tensor(pt[1][:, s, :], bank(4 + s)[:, 0, :], pt[0][:, s, :], ALU.subtract).then_inc(pt_lo, 1)

            def h1_low(p, s):
                dve.wait_ge(h1_hi, 2 * p + s + 1)
                dve.scalar_tensor_tensor(out=h1[1][:, s].rearrange("p j t f -> p (j t f)"),
                                         in0=bank(2 * s, 2).rearrange("p k c -> p (k c)"), scalar=0.0,
                                         in1=h1[0][:, s].rearrange("p j t f -> p (j t f)"),
                                         op0=ALU.max, op1=ALU.subtract).then_inc(h1_lo, 1)

            def qt_low(p, s):
                dve.wait_ge(qt_hi, 2 * p + s + 1)
                dve.tensor_tensor(qt[1][:, s], bank(2 * s, 2), qt[0][:, s], ALU.subtract).then_inc(qt_lo, 1)

            def s3_low(p, s):
                dve.wait_ge(s3_hi, 2 * p + s + 1)
                dve.tensor_tensor(s3[1][:, s], bank(s)[:, 0, :].rearrange("p (t j d) -> p t j d", t=T, j=2),
                                  s3[0][:, s], ALU.subtract).then_inc(s3_lo, 1)

            def scores3(p):
                for s in range(2):
                    q = 2 * p + s
                    dve.wait_ge(s2_done, q + 1)
                    dve.tensor_copy(s1c[:, s, :], bank(6 + s)[:, 0, 0:4]).then_inc(s1_out, 1)
                    for k in range(4):
                        i = dve.tensor_tensor_reduce(out=soft[:, s, k, :], in0=bank(4 + s)[:, 0, (k % 2) * N:(k % 2 + 1) * N],
                                                     in1=mask[:, k // 2, :], scale=1.0, scalar=-2 * BIG, op0=ALU.add,
                                                     op1=ALU.max, accum_out=m3[:, s, k:k + 1])
                    i.then_inc(tm_done, 1)
                dve.wait_ge(tm_done, 2 * p + 2)
                dve.wait_ge(s1_out, 2 * p + 2)
                dve.tensor_tensor(zm[:, 0], m3[:], s1c[:], ALU.add).then_inc(m_step, 1)
                dve.wait_ge(m_step, 3 * p + 1)
                dve.scalar_tensor_tensor(out=zm[:, 1], in0=zm[:, 0], scalar=SLOPE, in1=zm[:, 0],
                                         op0=ALU.mult, op1=ALU.max).then_inc(m_step, 1)
                dve.wait_ge(m_step, 3 * p + 2)
                dve.tensor_scalar(zm[:, 2], zm[:, 1], -1.0, None, ALU.mult).then_inc(m_step, 1)

            def leaky3(p):
                for s in range(2):
                    dve.wait_ge(zt_ready, 2 * p + s + 1)
                    z = soft[:, s].rearrange("p k n -> p (k n)")
                    dve.scalar_tensor_tensor(out=z, in0=z, scalar=SLOPE, in1=z, op0=ALU.mult, op1=ALU.max).then_inc(lk_ready, 1)

            def turned_low(p, slots=(0, 1)):
                for s in slots:
                    dve.wait_ge(ext_hi_ok, 2 * p + s + 1)
                    dve.tensor_tensor(ext_lo[:, s].rearrange("p j t n -> p (j t n)"),
                                      bank(2 * s, 2).rearrange("p k c -> p (k c)"),
                                      ext_hi[:, s].rearrange("p j t n -> p (j t n)"), ALU.subtract).then_inc(ext_lo_ok, 1)

            def weights3(p, first):
                if not first:
                    dve.wait_ge(ln3.added, 2 * p)
                dve.wait_ge(ex_ready, 2 * p + 2)
                dve.reciprocal(ri[:], rs[:]).then_inc(r_step, 1)

            def sum3(p, first):
                dve.wait_ge(r_step, p + 1)
                for s in range(2):
                    q = 2 * p + s
                    if not first:
                        dve.wait_ge(stored[s], 32 * p)
                    dve.wait_ge(o3_done, q + 1)
                    for t in range(T):
                        for j in range(2):
                            k = 2 * t + j
                            i = dve.scalar_tensor_tensor(
                                out=ob[:, s, t, j, :], in0=bank(2 * s + 1)[:, 0, k * D:(k + 1) * D], scalar=ri[:, s, k:k + 1],
                                in1=xn[:, q, t, j, :], op0=ALU.mult, op1=ALU.add)
                    i.then_inc(ln3.added, 1)

            def last_sum(s, t, j):
                return ob[:, s, t, j, :]

            def step(p, two_ahead=True, ahead=True, behind=True, two_behind=True, first3=False, beside=None):
                for s in range(2):
                    pt_low(p, s)
                if beside:
                    beside()
                for s in range(2):
                    h1_low(p, s)
                for s in range(2):
                    if ahead:
                        add(p + 1, s, o1_done, 4 + s, ln1)
                    qt_low(p, s)
                if two_ahead:
                    for s in range(2):
                        weighted_low(p + 2, s)
                if behind:
                    variance(p - 1, ln2, not two_behind)
                if two_behind:
                    turned_low(p - 2)
                    weights3(p - 2, first3)
                if ahead:
                    variance(p + 1, ln1, False)
                if behind:
                    apply(p - 1, ln2)
                if ahead:
                    apply(p + 1, ln1)
                if two_behind:
                    sum3(p - 2, first3)
                    ln_stats(dve, last_sum, p - 2, ln3)
                    ln_var_eps(dve, p - 2, ln3)
                s3_low(p, 0)
                if two_behind:
                    norm3(p - 2)
                s3_low(p, 1)
                if behind:
                    scores3(p - 1)
                    leaky3(p - 1)
                for s in range(2):
                    add(p, s, o2_done, 2 + s, ln2)

            def norm3(p):
                for s in range(2):
                    ln_apply(dve, last_sum, lambda t, j: last_sum(s, t, j), p, s, ln3)

            for s in range(2):
                add(0, s, o1_done, s, ln1)
            leaky(IT - 1)
            variance(0, ln1, True)
            take_scores(1)
            apply(0, ln1)
            maxima(1)
            both_low(1)
            normalize(1)
            step(0, behind=False, two_behind=False, beside=lambda: take_attention(1))
            step(1, two_behind=False)
            step(2, first3=True)
            with dve.Fori(3, IT - 2) as p:
                step(p)
            step(IT - 2, two_ahead=False)
            step(IT - 1, two_ahead=False, ahead=False)
            variance(IT - 1, ln2, False)
            turned_low(IT - 2, (0,))
            apply(IT - 1, ln2)
            turned_low(IT - 2, (1,))
            scores3(IT - 1)
            weights3(IT - 2, False)
            leaky3(IT - 1)
            sum3(IT - 2, False)
            ln_stats(dve, last_sum, IT - 2, ln3)
            ln_var_eps(dve, IT - 2, ln3)
            weights3(IT - 1, False)
            turned_low(IT - 1)
            norm3(IT - 2)
            sum3(IT - 1, False)
            ln_stats(dve, last_sum, IT - 1, ln3)
            ln_var_eps(dve, IT - 1, ln3)
            norm3(IT - 1)

        @block.scalar
        def _(act):
            def x0_high(p):
                for s in range(2):
                    act.wait_ge(x_in[s], 32 * (p + 1))
                    act.activation(x0[0][:, s], xin[:, s], ACT.Copy).then_inc(x0_hi, 1)

            def agg_high(p):
                for s in range(2):
                    act.wait_ge(agg_done, 2 * p + s + 1)
                    act.activation(aggt[0][:, s, :], bank(s)[:, 0, :], ACT.Copy).then_inc(agg_hi, 1)

            def h_raw(p):
                for s in range(2):
                    q = 2 * p + s
                    act.wait_ge(h_done, q + 1)
                    act.activation(hraw[:, :, q, :], bank(2 + 2 * s, 2), ACT.Copy).then_inc(h_out, 1)

            act.wait_ge(deg_done, 1)
            act.activation(root_bc[:], bank(0)[:, 0, 0:N], ACT.Sqrt)
            act.activation(root[:], bank(1)[:, 0, 0:T], ACT.Sqrt).then_inc(deg_root, 1)
            x0_high(0)
            with act.Fori(0, IT - 1) as p:
                agg_high(p)
                x0_high(p + 1)
                h_raw(p)
            agg_high(IT - 1)
            h_raw(IT - 1)
            act.wait_ge(edges_sorted, 1)
            act.activation(sorted_bc[:], bank(6)[:, 0, :].rearrange("p (a e) -> p a e", a=2), ACT.Copy)
            act.activation(wa[:], bank(7)[:, 0, 4:6], ACT.Copy)
            act.activation(sorted_col[:], bank(7)[:, 0, 0:ET], ACT.Copy).then_inc(sorted_out, 1)

            def bn_sqrt(ks, turn):
                act.wait_ge(bn_var, turn)
                act.activation(bco[:, 1, ks], bagg[:, ks, 1], ACT.Sqrt, bias=eps[:]).then_inc(bn_root, 1)

            bn_sqrt(slice(0, 2), 1)
            act.wait_ge(bn1_ready, 1)
            with act.Fori(0, Q) as q:
                for k in range(H0 // P):
                    i = act.activation(hraw[:, k, q, :], hraw[:, k, q, :], ACT.Relu, bias=bco[:, 3, k:k + 1], scale=bco[:, 2, k:k + 1])
                i.then_inc(relu_ready, 1)

            act.wait_ge(adj_dst_done, 1)
            act.activation(adj_dst[:], bank(6)[:, 0, :].rearrange("p (t e) -> p t e", t=T), ACT.Copy).then_inc(adj_dst_out, 1)
            bn_sqrt(slice(2, 3), 2)
            act.wait_ge(bn2_ready, 1)

            def bn_out(p, first):
                for s in range(2):
                    q = 2 * p + s
                    if not first:
                        act.wait_ge(t1_done, q - 1)
                    act.activation(bnt[:, s, :], oraw[:, q, :], ACT.Identity, bias=bco[:, 3, 2:3], scale=bco[:, 2, 2:3]).then_inc(bnt_ready, 1)

            def x1_high(p):
                for s in range(2):
                    q = 2 * p + s
                    act.wait_ge(t2_done, q + 1)
                    act.activation(xt[0][:, s, :], bank(s)[:, 0, :], ACT.Copy).then_inc(xt_hi, 1)

            def vq_high(p):
                for s in range(2):
                    q = 2 * p + s
                    act.wait_ge(vq_done, q + 1)
                    act.activation(vq[0][:, s], vq_bank(s), ACT.Copy).then_inc(vq_hi_ok, 1)

            def gathered(p):
                for s in range(2):
                    q = 2 * p + s
                    act.wait_ge(g_done, q + 1)
                    act.activation(z1[:, s, :], bank(2 + 2 * s)[:, 0, :], ACT.Copy).then_inc(z_ready, 1)
                for s in range(2):
                    q = 2 * p + s
                    act.wait_ge(ve_done, q + 1)
                    act.activation(vall[:, :, bass.ds(2 * q, 2), :],
                                   bank(3 + 2 * s)[:, 0, :].rearrange("p (t j d) -> p t j d", t=ET, j=2), ACT.Copy).then_inc(ve_out, 1)

            bn_out(0, True)
            ln_root(act, 0, ln0)
            bn_out(1, False)
            x1_high(0)
            act.wait_ge(a_edge_done, 1)
            act.activation(log_a[:], bank(6)[:, 0, 0:E], ACT.Ln, bias=log_eps[:]).then_inc(log_ready, 1)

            def softmax_exp(half):
                act.wait_ge(sm, half * SM_STEPS + SM_EXP)
                act.activation(sc[0:HALF, 3, :], sc[0:HALF, 0, :], ACT.Exp).then_inc(sm_exp, 1)

            def weighted_high(p, s, first):
                act.wait_ge(wv_ready, 2 * p + s + 1)
                if not first:
                    act.wait_ge(y1_done, 2 * p + s - 1)
                act.activation(wv_hi[:, s], wv[:, s], ACT.Copy).then_inc(wv_hi_ok, 1)

            def y1_turned(p, s, psum_bank):
                act.wait_ge(y1_done, 2 * p + s + 1)
                act.activation(y1t[:, s, :], bank(psum_bank)[:, 0, :], ACT.Copy).then_inc(y1_out, 1)

            with act.Fori(0, IT // 2 + 1) as p:
                vq_high(p)
                ln_root(act, p + 1, ln0)
                gathered(p)
                x1_high(p + 1)
                bn_out(p + 2, False)
            softmax_exp(0)
            vq_high(IT - 3)
            ln_root(act, IT - 2, ln0)
            gathered(IT - 3)
            x1_high(IT - 2)
            bn_out(IT - 1, False)
            vq_high(IT - 2)
            for s in range(2):
                weighted_high(0, s, True)
            ln_root(act, IT - 1, ln0)
            gathered(IT - 2)
            x1_high(IT - 1)
            y1_turned(0, 0, 6)
            vq_high(IT - 1)
            y1_turned(0, 1, 6)
            gathered(IT - 1)
            for s in range(2):
                weighted_high(1, s, False)
            softmax_exp(1)

            def pt_high(p, s):
                act.wait_ge(pt_done, 2 * p + s + 1)
                act.activation(pt[0][:, s, :], bank(4 + s)[:, 0, :], ACT.Copy).then_inc(pt_hi, 1)

            def h1_high(p, s):
                act.wait_ge(h1_done, 2 * p + s + 1)
                act.activation(h1[0][:, s].rearrange("p j t f -> p (j t f)"), bank(2 * s, 2).rearrange("p k c -> p (k c)"),
                               ACT.Relu).then_inc(h1_hi, 1)

            def qt_high(p, s):
                act.wait_ge(qt_done, 2 * p + s + 1)
                act.activation(qt[0][:, s], bank(2 * s, 2), ACT.Copy).then_inc(qt_hi, 1)

            def h2_relu(p, s, g):
                act.wait_ge(h2_done, GB * (2 * p + s) + g + 1)
                act.activation(h2[:, s, g, :], bank(4 + g)[:, 0, :], ACT.Relu).then_inc(h2_out, 1)

            def s3_high(p, s):
                act.wait_ge(s3_done, 2 * p + s + 1)
                act.activation(s3[0][:, s], bank(s)[:, 0, :].rearrange("p (t j d) -> p t j d", t=T, j=2),
                               ACT.Copy).then_inc(s3_hi, 1)

            def turned3(p):
                for s in range(2):
                    act.wait_ge(t3_done, 2 * p + s + 1)
                    act.activation(xt3[:, s, :], bank(4 + s)[:, 0, :], ACT.Copy).then_inc(xt3_out, 1)

            def sum_scores(p):
                for s in range(2):
                    act.wait_ge(tm_done, 2 * p + s + 1)
                    act.wait_ge(s1_out, 2 * p + s + 1)
                    for k in range(4):
                        i = act.activation(soft[:, s, k, :], soft[:, s, k, :], ACT.Identity, bias=s1c[:, s, k:k + 1])
                    i.then_inc(zt_ready, 1)

            def exps(p, s):
                act.wait_ge(m_step, 3 * p + 3)
                act.wait_ge(lk_ready, 2 * p + s + 1)
                for k in range(4):
                    i = act.activation(soft[:, s, k, :], soft[:, s, k, :], ACT.Exp, bias=zm[:, 2, s, k:k + 1],
                                       accum_out=rs[:, s, k:k + 1])
                i.then_inc(ex_ready, 1)

            def turned_exps(p, s):
                act.wait_ge(exr_done, 2 * p + s + 1)
                act.activation(ext_hi[:, s].rearrange("p j t n -> p (j t n)"),
                               bank(2 * s, 2).rearrange("p k c -> p (k c)"), ACT.Copy).then_inc(ext_hi_ok, 1)

            def attended(p, s):
                act.wait_ge(ax_done, 2 * p + s + 1)
                act.activation(axt[:, s, :], bank(2 * s)[:, 0, :], ACT.Copy).then_inc(ax_out, 1)

            def step(p, two_ahead=True, ahead=True, behind=True, two_behind=True):
                for s in range(2):
                    pt_high(p, s)
                for s in range(2):
                    if two_behind:
                        exps(p - 2, s)
                    if ahead:
                        y1_turned(p + 1, s, 6 + s)
                    h1_high(p, s)
                for s in range(2):
                    qt_high(p, s)
                if two_ahead:
                    for s in range(2):
                        weighted_high(p + 2, s, False)
                for s in range(2):
                    if two_behind:
                        turned_exps(p - 2, s)
                    for g in range(2):
                        h2_relu(p, 0, 2 * s + g)
                for s in range(2):
                    h2_relu(p, 1, s)
                    if two_behind:
                        attended(p - 2, s)
                for g in range(2, GB):
                    h2_relu(p, 1, g)
                s3_high(p, 0)
                if behind:
                    turned3(p - 1)
                s3_high(p, 1)
                if behind:
                    sum_scores(p - 1)

            step(0, behind=False, two_behind=False)
            step(1, two_behind=False)
            with act.Fori(2, IT - 2) as p:
                step(p)
            step(IT - 2, two_ahead=False)
            step(IT - 1, two_ahead=False, ahead=False)
            for p in (IT - 2, IT - 1):
                for s in range(2):
                    exps(p, s)
                for s in range(2):
                    turned_exps(p, s)
                attended(p, 0)
                if p == IT - 2:
                    turned3(IT - 1)
                    sum_scores(IT - 1)
                attended(p, 1)

        @block.tensor
        def _(pe):
            pe.wait_ge(deg_ready, 1)
            for t in range(T):
                pe.matmul(bank(0)[:, 0, 0:N], ones[:], degm[:, t, :], start=(t == 0), stop=(t == T - 1))
            for m in range(T):
                for t in range(T):
                    i = pe.matmul(bank(1)[:, 0, m:m + 1], degm[:, t, m * P:(m + 1) * P], ones[:, 0:1],
                                  start=(t == 0), stop=(t == T - 1))
            i.then_inc(deg_done, 1)
            pe.wait_ge(a_hat_ready, 1)

            def pass1(p, first):
                for s in range(2):
                    pe.wait_ge(x0_lo, 2 * p + s + 1)
                    for j in range(2):
                        for t in range(T):
                            i = three(pe, bank(s)[:, 0, j * N:(j + 1) * N], [h[:, s, t, j, :] for h in x0],
                                      [h[:, t, :] for h in a_hat], t == 0, t == T - 1)
                    i.then_inc(agg_done, 1)
                for s in range(2):
                    q = 2 * p + s
                    pe.wait_ge(agg_lo, q + 1)
                    if not first:
                        pe.wait_ge(h_out, q - 1)
                    for k in range(H0 // P):
                        i = three(pe, bank(2 + 2 * s + k)[:, 0, :], [h[:, k * P:(k + 1) * P] for h in w1t],
                                  [h[:, s, :] for h in aggt], True, True)
                    i.then_inc(h_done, 1)

            pass1(0, True)
            with pe.Fori(1, IT) as p:
                pass1(p, False)

            pe.wait_ge(edges_ranked, 1)
            for k in range(2):
                for t in range(ET):
                    pe.matmul(bank(6)[:, 0, k * E:(k + 1) * E], ecol_bc[:, k, t, :], perm[:, t, :], start=(t == 0), stop=(t == ET - 1))
            pe.wait_ge(s_wts, 16 * 12)
            pe.wait_ge(s_small, 16 * SMALL)
            pe.matmul(bank(7)[:, 0, 4:6], l3wt_s[:], l3a_s[:], start=True, stop=True)
            for m in range(ET):
                for t in range(ET):
                    i = pe.matmul(bank(7)[:, 0, m:m + 1], perm[:, t, m * P:(m + 1) * P], ecol_f[:, 0, t:t + 1],
                                  start=(t == 0), stop=(t == ET - 1))
            i.then_inc(edges_sorted, 1)

            def pass2(p, first):
                for s in range(2):
                    q = 2 * p + s
                    pe.wait_ge(relu_ready, q + 1)
                    if not first:
                        pe.wait_ge(o_out, q - 1)
                    for k in range(H0 // P):
                        i = pe.matmul(bank(s)[:, 0, :], w2t[:, k, :], hraw[:, k, q, :], start=(k == 0), stop=(k == 1))
                    i.then_inc(o_done, 1)

            pass2(0, True)
            with pe.Fori(1, IT) as p:
                pass2(p, False)

            pe.wait_ge(sel_ready, 1)
            for n in range(T):
                for t in range(T):
                    i = pe.matmul(bank(6)[:, 0, n * E:(n + 1) * E], adjt_sb[:, t, n * P:(n + 1) * P], sdst[:, t, :],
                                  start=(t == 0), stop=(t == T - 1))
            i.then_inc(adj_dst_done, 1)

            pe.wait_ge(weights_split, 1)
            pe.wait_ge(o_out, Q)

            def turn_out(p, first):
                for s in range(2):
                    q = 2 * p + s
                    pe.wait_ge(bnt_ready, q + 1)
                    if not first:
                        pe.wait_ge(xt_lo, q - 1)
                    for t in range(T):
                        for j in range(2):
                            k = 2 * t + j
                            i = pe.transpose(bank(s)[:, 0, k * P:(k + 1) * P], bnt[:, s, j * N + t * P:j * N + (t + 1) * P], ident[:])
                    i.then_inc(t1_done, 1)

            def turn_x1(p):
                for s in range(2):
                    q = 2 * p + s
                    pe.wait_ge(ln0.done, q + 1)
                    for j in range(2):
                        for t in range(T):
                            k = 2 * j + t
                            i = pe.transpose(bank(s)[:, 0, k * P:(k + 1) * P], x1r[:, s, t, j, :], ident[:])
                    i.then_inc(t2_done, 1)

            def project(p, first):
                for s in range(2):
                    q = 2 * p + s
                    pe.wait_ge(xt_lo, q + 1)
                    if not first:
                        pe.wait_ge(z_ready, q - 1)
                        pe.wait_ge(ve_out, q - 1)
                    for t in range(T):
                        for j in range(2):
                            c = j * N + t * P
                            i = three(pe, vq_bank(s)[:, t, j, :], [h[:, s, c:c + P] for h in xt], [h[:] for h in wvq], True, True)
                    i.then_inc(vq_done, 1)

            def gather(p):
                for s in range(2):
                    q = 2 * p + s
                    pe.wait_ge(vq_lo_ok, q + 1)
                    for j in range(2):
                        for n, (t, h) in enumerate((t, h) for t in range(T) for h in range(2)):
                            i = pe.matmul(bank(2 + 2 * s)[:, 0, j * E:(j + 1) * E], vq[h][:, s, t, j, D:2 * D], sel_sum[:, t, :],
                                          start=(n == 0), stop=(n == 3))
                    i.then_inc(g_done, 1)
                for s in range(2):
                    for e in range(ET):
                        for n, (t, h) in enumerate((t, h) for t in range(T) for h in range(2)):
                            i = pe.matmul(bank(3 + 2 * s)[:, 0, e * 2 * D:(e + 1) * 2 * D], sel_dst[:, t, e * P:(e + 1) * P],
                                          vq[h][:, s, t, :, 0:D], start=(n == 0), stop=(n == 3))
                    i.then_inc(ve_done, 1)

            def score(p):
                for s in range(2):
                    q = 2 * p + s
                    pe.wait_ge(l_ready, q + 1)
                    for e in range(ET):
                        for j in range(2):
                            i = pe.matmul(bank(7)[:, 0, bass.ds(e * P + HEADS * (2 * q + j), HEADS)],
                                          l1[:, s, j * E + e * P:j * E + (e + 1) * P], head_a[:], start=True, stop=True)
                    i.then_inc(e_done, 1)

            turn_out(0, True)
            turn_x1(0)
            turn_out(1, False)
            pe.wait_ge(picked, 1)
            for t in range(T):
                i = pe.matmul(bank(6)[:, 0, 0:E], ones[:], prod[:, t, :], start=(t == 0), stop=(t == T - 1))
            i.then_inc(a_edge_done, 1)
            project(0, True)
            gather(0)
            turn_x1(1)
            score(0)
            def turn_scores(half):
                pe.wait_ge(sm, half * SM_STEPS + 1)
                pe.wait_ge(log_ready, 1)
                for t in range(ET):
                    i = pe.transpose(bank(6)[0:HALF, 0, t * P:(t + 1) * P], esb[:, half, t, :], ident[:])
                i.then_inc(sm_t1, 1)

            def turn_attention(half):
                pe.wait_ge(sm, half * SM_STEPS + SM_RESULT)
                for t in range(ET):
                    i = pe.transpose(bank(6)[:, 0, t * HALF:(t + 1) * HALF], sc[0:HALF, 0, t * P:(t + 1) * P],
                                     ident[0:HALF, 0:HALF])
                i.then_inc(sm_t2, 1)

            def body(p, beside=None):
                turn_out(p + 1, False)
                project(p, False)
                gather(p)
                if beside:
                    beside()
                turn_x1(p + 1)
                score(p)

            with pe.Fori(1, IT // 2) as p:
                body(p)
            body(IT // 2, lambda: turn_scores(0))
            body(IT // 2 + 1, lambda: turn_attention(0))

            def attend1(p, s, psum_bank):
                pe.wait_ge(wv_lo_ok, 2 * p + s + 1)
                for j in range(2):
                    for n, (e, h) in enumerate((e, h) for e in range(ET) for h in (wv_hi, wv_lo)):
                        i = pe.matmul(bank(psum_bank)[:, 0, j * N:(j + 1) * N], h[:, s, e, j, :], sel_src_t[:, e, :],
                                      start=(n == 0), stop=(n == 3))
                i.then_inc(y1_done, 1)

            def output1(p, s, psum_bank):
                pe.wait_ge(y1_out, 2 * p + s + 1)
                for t in range(T):
                    for j in range(2):
                        k = 2 * t + j
                        c = j * N + t * P
                        i = pe.matmul(bank(psum_bank)[:, 0, k * D:(k + 1) * D], y1t[:, s, c:c + P], wot[:], start=True, stop=True)
                i.then_inc(o1_done, 1)

            def mix_x(p, s):
                pe.wait_ge(xs_lo, 2 * p + s + 1)
                for j in range(2):
                    for t in range(T):
                        i = three(pe, bank(4 + s)[:, 0, j * N:(j + 1) * N], [h[:, s, t, j, :] for h in xs],
                                  [h[:, t, :] for h in wgt], t == 0, t == T - 1)
                i.then_inc(pt_done, 1)

            def hidden1(p, s):
                pe.wait_ge(pt_lo, 2 * p + s + 1)
                for j in range(2):
                    for t in range(T):
                        c = j * N + t * P
                        i = three(pe, bank(2 * s + j)[:, 0, t * H2A:(t + 1) * H2A], [h[:, s, c:c + P] for h in pt],
                                  [h[:] for h in l2w1_s], True, True)
                i.then_inc(h1_done, 1)

            def mix_hidden(p, s):
                pe.wait_ge(h1_lo, 2 * p + s + 1)
                for f in range(GA):
                    for j in range(2):
                        for t in range(T):
                            i = three(pe, bank(2 * s + f)[:, 0, j * N:(j + 1) * N],
                                      [h[:, s, j, t, f * P:(f + 1) * P] for h in h1], [h[:, t, :] for h in wgt],
                                      t == 0, t == T - 1)
                i.then_inc(qt_done, 1)

            def hidden2(p, s, g):
                for f in range(GA):
                    i = three(pe, bank(4 + g)[:, 0, :], [h[:, f, g * P:(g + 1) * P] for h in l2w2_s],
                              [h[:, s, f, :] for h in qt], f == 0, f == GA - 1)
                i.then_inc(h2_done, 1)

            def narrow(p, s):
                pe.wait_ge(h2_out, GB * (2 * p + s + 1))
                for t in range(T):
                    for j in range(2):
                        k = 2 * t + j
                        for g in range(GB):
                            i = pe.matmul(bank(s)[:, 0, k * D:(k + 1) * D], h2[:, s, g, j * N + t * P:j * N + (t + 1) * P],
                                          l2w3_s[:, g, :], start=(g == 0), stop=(g == GB - 1))
                i.then_inc(s3_done, 1)

            def mix_out(p, s):
                pe.wait_ge(s3_lo, 2 * p + s + 1)
                for n in range(T):
                    for t in range(T):
                        i = three(pe, bank(2 + s)[:, 0, n * 2 * D:(n + 1) * 2 * D], [h[:, t, n * P:(n + 1) * P] for h in wgt],
                                  [h[:, s, t, :, :] for h in s3], t == 0, t == T - 1)
                i.then_inc(o2_done, 1)

            def turn3(p, s):
                pe.wait_ge(x3_ready, 2 * p + s + 1)
                for j in range(2):
                    for t in range(T):
                        k = 2 * j + t
                        i = pe.transpose(bank(4 + s)[:, 0, k * P:(k + 1) * P], x3[:, s, t, j, :], ident[:])
                i.then_inc(t3_done, 1)

            def scores3(p, s):
                pe.wait_ge(xt3_out, 2 * p + s + 1)
                for t in range(T):
                    for j in range(2):
                        k = 2 * t + j
                        pe.matmul(bank(6 + s)[:, 0, k:k + 1], xt3[:, s, j * N + t * P:j * N + (t + 1) * P], wa[:, 0:1],
                                  start=True, stop=True)
                pe.matmul(bank(4 + s)[:, 0, :], wa2_bc[:], xt3[:, s, :], start=True, stop=True).then_inc(s2_done, 1)

            def turn_exps(p, s):
                pe.wait_ge(ex_ready, 2 * p + s + 1)
                for j in range(2):
                    for c in range(T):
                        for t in range(T):
                            i = pe.transpose(bank(2 * s + j)[:, 0, c * N + t * P:c * N + (t + 1) * P],
                                             soft[:, s, 2 * t + j, c * P:(c + 1) * P], ident[:])
                i.then_inc(exr_done, 1)

            def attend3(p, s):
                pe.wait_ge(ext_lo_ok, 2 * p + s + 1)
                pe.wait_ge(x3_lo_ok, 2 * p + s + 1)
                for j in range(2):
                    for c in range(T):
                        i = three(pe, bank(2 * s)[:, 0, j * N:(j + 1) * N], [h[:, s, c, j, :] for h in (x3_hi, x3_lo)],
                                  [h[:, s, j, c, :] for h in (ext_hi, ext_lo)], c == 0, c == T - 1)
                i.then_inc(ax_done, 1)

            def output3(p, s):
                pe.wait_ge(ax_out, 2 * p + s + 1)
                for t in range(T):
                    for j in range(2):
                        k = 2 * t + j
                        i = pe.matmul(bank(2 * s + 1)[:, 0, k * D:(k + 1) * D], axt[:, s, j * N + t * P:j * N + (t + 1) * P],
                                      l3w_s[:], start=True, stop=True)
                i.then_inc(o3_done, 1)

            def step(p, first=False, ahead=True, behind=True, two_behind=True, beside=None):
                for s in range(2):
                    if two_behind:
                        pe.wait_ge(tm_done, 2 * (p - 2) + s + 1)
                    elif not first:
                        pe.wait_ge(h2_out, GB * 2 * p)
                    mix_x(p, s)
                if beside:
                    beside()
                for s in range(2):
                    if ahead:
                        attend1(p + 1, s, 6 + s)
                    if not first:
                        if s == 0:
                            pe.wait_ge(s3_lo, 2 * p)
                        else:
                            pe.wait_ge(ln2.added, 2 * p)
                    hidden1(p, s)
                for s in range(2):
                    if ahead:
                        output1(p + 1, s, 4 + s)
                    mix_hidden(p, s)
                for s in range(2):
                    pe.wait_ge(qt_lo, 2 * p + s + 1)
                    if two_behind:
                        turn_exps(p - 2, s)
                    if s == 0 and ahead:
                        pe.wait_ge(ln1.added, 2 * (p + 2))
                    for g in range(2):
                        hidden2(p, 0, 2 * s + g)
                for s in range(2):
                    pe.wait_ge(h2_out, GB * 2 * p + s + 1)
                    hidden2(p, 1, s)
                    if two_behind:
                        attend3(p - 2, s)
                for g in range(2, GB):
                    if two_behind:
                        output3(p - 2, g - 2)
                    pe.wait_ge(h2_out, GB * 2 * p + g + 1)
                    hidden2(p, 1, g)
                narrow(p, 0)
                if behind:
                    pe.wait_ge(h2_out, GB * (2 * p + 1) + 2)
                    for s in range(2):
                        turn3(p - 1, s)
                if two_behind:
                    pe.wait_ge(ln3.added, 2 * (p - 1))
                narrow(p, 1)
                if behind:
                    for s in range(2):
                        scores3(p - 1, s)
                for s in range(2):
                    mix_out(p, s)

            pe.wait_ge(sm, SM_STEPS)
            body(IT // 2 + 2, lambda: attend1(0, 0, 6))
            project(IT - 1, False)
            output1(0, 0, 0)
            attend1(0, 1, 6)
            gather(IT - 1)
            output1(0, 1, 1)
            score(IT - 1)
            pe.wait_ge(ve_out, Q)
            pe.wait_ge(wgt_ready, 1)
            turn_scores(1)

            def last_attention():
                turn_attention(1)
                pe.wait_ge(sm, 2 * SM_STEPS)

            step(0, first=True, behind=False, two_behind=False, beside=last_attention)
            pe.wait_ge(wa2_ready, 1)
            step(1, two_behind=False)
            with pe.Fori(2, IT - 1) as p:
                step(p)
            step(IT - 1, ahead=False)
            pe.wait_ge(ln2.added, Q)
            pe.wait_ge(tm_done, Q - 2)
            for s in range(2):
                turn_exps(IT - 2, s)
            attend3(IT - 2, 0)
            for s in range(2):
                turn3(IT - 1, s)
            for s in range(2):
                scores3(IT - 1, s)
            attend3(IT - 2, 1)
            for s in range(2):
                output3(IT - 2, s)
            pe.wait_ge(ln3.added, Q - 2)
            for s in range(2):
                turn_exps(IT - 1, s)
            for s in range(2):
                attend3(IT - 1, s)
            for s in range(2):
                output3(IT - 1, s)


def kernel(**inputs):
    import numpy as np
    import concourse.bacc as bacc
    from concourse.bass_utils import run_bass_kernel_spmd

    a = {k: np.ascontiguousarray(v) for k, v in inputs.items()}
    arrays = {
        "x": a["x"], "adj": a["adj"], "adj_t": np.ascontiguousarray(a["adj"].T),
        "w1_t": np.ascontiguousarray(a["L0_gnn_W1"].T),
        "w2_t": np.ascontiguousarray(a["L0_gnn_W2"].T),
        "bn_cols": np.ascontiguousarray(np.concatenate(
            [a["L0_gnn_" + k].reshape(-1, P) for k in ("b1", "g1", "be1", "b2", "g2", "be2")]).T),
        "wv_t": np.ascontiguousarray(a["L1_gnn_W_val"].T), "wq_t": np.ascontiguousarray(a["L1_gnn_W_lin"].T),
        "a_head": a["L1_gnn_a"].reshape(D, 1), "wo_t": np.ascontiguousarray(a["L1_gnn_W_out"].T),
        "src": a["L1_gnn_src"], "dst": a["L1_gnn_dst"],
        "edge_cols": np.ascontiguousarray(np.concatenate([a[k].reshape(ET, P) for k in ("L1_gnn_src", "L1_gnn_dst")]).T),
        "l2w1": a["L2_gnn_W1"], "l2w2": a["L2_gnn_W2"], "l2w3": a["L2_gnn_W3"],
        "l3w": a["L3_gnn_W"], "l3a": np.ascontiguousarray(a["L3_gnn_a"].reshape(2, D).T), "l3w_t": np.ascontiguousarray(a["L3_gnn_W"].T),
    }
    nc = bacc.Bacc("TRN2", target_bir_lowering=False, num_devices=1)
    aps = {k: nc.dram_tensor("in_" + k, v.shape, mybir.dt.from_np(v.dtype), kind="ExternalInput").ap() for k, v in arrays.items()}
    out = nc.dram_tensor("out_x", (B, N, D), F32, kind="ExternalOutput").ap()
    build(nc, *aps.values(), out)
    r = run_bass_kernel_spmd(nc, [{"in_" + k: v for k, v in arrays.items()}], core_ids=[0])
    return r.results[0]["out_x"]
```
